# Optimizing a Trainium2 kernel written in Bass

```python
import numpy as np
import jax
import jax.numpy as jnp

def _softmax(x, axis=-1):
    return jax.nn.softmax(x, axis=axis)

def _gelu(x):
    return jax.nn.gelu(x, approximate=True)

def _silu(x):
    return jax.nn.silu(x)

def _sigmoid(x):
    return jax.nn.sigmoid(x)

def _layernorm(x, axis=-1, eps=1e-05):
    m = jnp.mean(x, axis=axis, keepdims=True)
    v = jnp.var(x, axis=axis, keepdims=True)
    return (x - m) / jnp.sqrt(v + eps)

def _scatter_add(tgt, idx, src, axis=0):
    return tgt.at[idx].add(src)

def _segment_sum(src, seg, n):
    return jax.ops.segment_sum(src, seg, n)
kernel_name = 'mk_early_fusion_d1_tok_img768_r4_380f0f'

def setup_inputs(seed: int=0):
    np.random.seed(seed)
    _w = jnp.asarray

    def _rec_inputs():
        import jax
        import jax.numpy as jnp
        _rk = jax.random.key(seed)
        x = 7.57192e-06 + 1.00007 * jax.random.normal(jax.random.fold_in(_rk, 1), (16, 3, 224, 224), jnp.float32)
        txt = 0.00277252 + 1.14258 * jax.random.normal(jax.random.fold_in(_rk, 2), (16, 77, 192), jnp.float32)
        return (x, txt)
    x, txt = _rec_inputs()

    def _L0_tok_setup():
        import jax, jax.numpy as jnp
        import numpy as np
        from jax import lax
        P = 16
        S = 8
        key = jax.random.key(seed)
        k1, k2, k3, k4, k5 = jax.random.split(key, 5)
        B, C, H, W = (64, 3, 224, 224)
        D = 192
        patch_dim = C * P * P
        out = (H - P) // S + 1
        n_tok = out * out + 1
        return {'x': jax.random.normal(k1, (B, C, H, W), dtype=jnp.float32), 'w': jax.random.normal(k2, (D, patch_dim), dtype=jnp.float32) * 0.02, 'b': jax.random.normal(k3, (D,), dtype=jnp.float32) * 0.02, 'cls_token': jax.random.normal(k4, (1, 1, D), dtype=jnp.float32), 'pos_embedding': jax.random.normal(k5, (1, n_tok, D), dtype=jnp.float32)}
    _L0_tok_all = _L0_tok_setup()
    _L0_tok_in = {k: v for k, v in _L0_tok_all.items() if k in ('w', 'b', 'cls_token', 'pos_embedding')}
    del _L0_tok_all

    def _L0_attn_setup():
        import jax, jax.numpy as jnp
        import numpy as np
        D_MODEL = 192
        D_STATE = 8
        EXPAND = 2
        D_HEAD = 64
        D_CONV = 4
        D_INNER = EXPAND * D_MODEL
        N_HEADS = D_INNER // D_HEAD
        PARAM_DIM = 2
        D_PROJ = 2 * D_INNER + N_HEADS * PARAM_DIM
        D_FF = 4 * D_MODEL
        BATCH, SEQ = (2, 512)

        def _rmsnorm(x, w, eps=1e-06):
            return x * jax.lax.rsqrt(jnp.mean(x * x, axis=-1, keepdims=True) + eps) * w

        def _l2norm(x, eps=1e-12):
            return x * jax.lax.rsqrt(jnp.sum(x * x, axis=-1, keepdims=True) + eps)

        def _mixer(x, w_in, conv_w, w_bc, D_skip, w_out):
            Bsz, T, _ = x.shape
            proj = x @ w_in
            gate, vraw, params = jnp.split(proj, [D_INNER, 2 * D_INNER], axis=-1)
            vpad = jnp.pad(vraw, ((0, 0), (D_CONV - 1, 0), (0, 0)))
            kernel = conv_w.T[:, None, :]
            conv = jax.lax.conv_general_dilated(vpad, kernel, window_strides=(1,), padding='VALID', dimension_numbers=('NWC', 'WIO', 'NWC'), feature_group_count=D_INNER)
            v = jax.nn.silu(conv)
            bc = (v @ w_bc).reshape(Bsz, T, N_HEADS, 2, D_STATE)
            Bm = _l2norm(bc[..., 0, :])
            Cm = _l2norm(bc[..., 1, :])
            p = params.reshape(Bsz, T, N_HEADS, PARAM_DIM)
            A = jax.nn.softplus(p[..., 0])
            dt = jax.nn.sigmoid(p[..., 1])
            S = 1.0 / (1.0 + dt * dt * A)
            u = v.reshape(Bsz, T, N_HEADS, D_HEAD)
            tfirst = lambda a: jnp.moveaxis(a, 1, 0)

            def step(carry, inp):
                z, xs = carry
                Bt, Ct, At, dtt, St, ut = inp
                d = dtt[..., None, None]
                a = At[..., None, None]
                s = St[..., None, None]
                bu = Bt[..., :, None] * ut[..., None, :]
                z = s * (z - d * a * xs + d * bu)
                xs = xs + d * z
                y = jnp.einsum('bhn,bhnp->bhp', Ct, xs)
                return ((z, xs), y)
            z0 = jnp.zeros((Bsz, N_HEADS, D_STATE, D_HEAD), x.dtype)
            _, ys = jax.lax.scan(step, (z0, z0), (tfirst(Bm), tfirst(Cm), tfirst(A), tfirst(dt), tfirst(S), tfirst(u)))
            y = jnp.moveaxis(ys, 0, 1)
            gated = (y + D_skip[None, None, :, None] * u) * jax.nn.silu(gate).reshape(Bsz, T, N_HEADS, D_HEAD)
            return gated.reshape(Bsz, T, D_INNER) @ w_out
        key = jax.random.key(seed)
        ks = jax.random.split(key, 8)

        def s(k, shape, scale):
            return jax.random.normal(k, shape, dtype=jnp.float32) * scale
        return {'x': s(ks[0], (BATCH, SEQ, D_MODEL), 1.0), 'norm1_w': jnp.ones((D_MODEL,), jnp.float32), 'w_in': s(ks[1], (D_MODEL, D_PROJ), D_MODEL ** (-0.5)), 'conv_w': s(ks[2], (D_INNER, D_CONV), D_CONV ** (-0.5)), 'w_bc': s(ks[3], (D_INNER, 2 * N_HEADS * D_STATE), D_INNER ** (-0.5)), 'D_skip': s(ks[4], (N_HEADS,), 1.0), 'w_out': s(ks[5], (D_INNER, D_MODEL), D_INNER ** (-0.5)), 'norm2_w': jnp.ones((D_MODEL,), jnp.float32), 'ff_w1': s(ks[6], (D_MODEL, D_FF), D_MODEL ** (-0.5)), 'ff_b1': jnp.zeros((D_FF,), jnp.float32), 'ff_w2': s(ks[7], (D_FF, D_MODEL), D_FF ** (-0.5)), 'ff_b2': jnp.zeros((D_MODEL,), jnp.float32)}
    _L0_attn_all = _L0_attn_setup()
    _L0_attn_in = {k: v for k, v in _L0_attn_all.items() if k in ('norm1_w', 'w_in', 'conv_w', 'w_bc', 'D_skip', 'w_out', 'norm2_w', 'ff_w1', 'ff_b1', 'ff_w2', 'ff_b2')}
    del _L0_attn_all

    def _L0_ffn_setup():
        import jax, jax.numpy as jnp
        import numpy as np
        import math
        B, S, D = (4, 1024, 192)
        E = 8
        TOP_K = 2
        H = 512
        CAP_F = 1.25
        EPS = 1e-06
        ALPHA = 1.0
        key = jax.random.key(seed)
        k0, k1, k2, k3 = jax.random.split(key, 4)
        x = jax.random.normal(k0, (B, S, D), jnp.float32)
        gate_w = jax.random.normal(k1, (E, D), jnp.float32) * 0.02
        w13 = jax.random.normal(k2, (E, 2 * H, D), jnp.float32) * 0.02
        w2 = jax.random.normal(k3, (E, D, H), jnp.float32) * 0.02
        norm_w = jnp.ones((E, D), jnp.float32)
        return {'x': x, 'gate_w': gate_w, 'w13': w13, 'w2': w2, 'norm_w': norm_w}
    _L0_ffn_all = _L0_ffn_setup()
    _L0_ffn_in = {k: v for k, v in _L0_ffn_all.items() if k in ('gate_w', 'w13', 'w2', 'norm_w')}
    del _L0_ffn_all
    return {'x': x, 'txt': txt, 'L0_tok_w': _L0_tok_in['w'], 'L0_tok_b': _L0_tok_in['b'], 'L0_tok_cls_token': _L0_tok_in['cls_token'], 'L0_tok_pos_embedding': _L0_tok_in['pos_embedding'], 'L0_attn_norm1_w': _L0_attn_in['norm1_w'], 'L0_attn_w_in': _L0_attn_in['w_in'], 'L0_attn_conv_w': _L0_attn_in['conv_w'], 'L0_attn_w_bc': _L0_attn_in['w_bc'], 'L0_attn_D_skip': _L0_attn_in['D_skip'], 'L0_attn_w_out': _L0_attn_in['w_out'], 'L0_attn_norm2_w': _L0_attn_in['norm2_w'], 'L0_attn_ff_w1': _L0_attn_in['ff_w1'], 'L0_attn_ff_b1': _L0_attn_in['ff_b1'], 'L0_attn_ff_w2': _L0_attn_in['ff_w2'], 'L0_attn_ff_b2': _L0_attn_in['ff_b2'], 'L0_ffn_gate_w': _L0_ffn_in['gate_w'], 'L0_ffn_w13': _L0_ffn_in['w13'], 'L0_ffn_w2': _L0_ffn_in['w2'], 'L0_ffn_norm_w': _L0_ffn_in['norm_w']}

def reference(x, txt, L0_tok_w, L0_tok_b, L0_tok_cls_token, L0_tok_pos_embedding, L0_attn_norm1_w, L0_attn_w_in, L0_attn_conv_w, L0_attn_w_bc, L0_attn_D_skip, L0_attn_w_out, L0_attn_norm2_w, L0_attn_ff_w1, L0_attn_ff_b1, L0_attn_ff_w2, L0_attn_ff_b2, L0_ffn_gate_w, L0_ffn_w13, L0_ffn_w2, L0_ffn_norm_w):
    import jax
    import jax.numpy as jnp

    def _L0_tok_ref(x, w, b, cls_token, pos_embedding):
        import jax, jax.numpy as jnp
        import numpy as np
        from jax import lax
        P = 16
        S = 8
        B = x.shape[0]
        patches = lax.conv_general_dilated_patches(x, filter_shape=(P, P), window_strides=(S, S), padding='VALID', dimension_numbers=('NCHW', 'OIHW', 'NCHW'))
        pd = patches.shape[1]
        patches = patches.reshape(B, pd, -1).transpose(0, 2, 1)
        tok = jnp.einsum('bnp,dp->bnd', patches, w) + b
        cls = jnp.broadcast_to(cls_token, (B, 1, tok.shape[-1]))
        out = jnp.concatenate([cls, tok], axis=1) + pos_embedding
        return out

    def _L0_attn_ref(x, norm1_w, w_in, conv_w, w_bc, D_skip, w_out, norm2_w, ff_w1, ff_b1, ff_w2, ff_b2):
        import jax, jax.numpy as jnp
        import numpy as np
        D_MODEL = 192
        D_STATE = 8
        EXPAND = 2
        D_HEAD = 64
        D_CONV = 4
        D_INNER = EXPAND * D_MODEL
        N_HEADS = D_INNER // D_HEAD
        PARAM_DIM = 2
        D_PROJ = 2 * D_INNER + N_HEADS * PARAM_DIM
        D_FF = 4 * D_MODEL
        BATCH, SEQ = (2, 512)

        def _rmsnorm(x, w, eps=1e-06):
            return x * jax.lax.rsqrt(jnp.mean(x * x, axis=-1, keepdims=True) + eps) * w

        def _l2norm(x, eps=1e-12):
            return x * jax.lax.rsqrt(jnp.sum(x * x, axis=-1, keepdims=True) + eps)

        def _mixer(x, w_in, conv_w, w_bc, D_skip, w_out):
            Bsz, T, _ = x.shape
            proj = x @ w_in
            gate, vraw, params = jnp.split(proj, [D_INNER, 2 * D_INNER], axis=-1)
            vpad = jnp.pad(vraw, ((0, 0), (D_CONV - 1, 0), (0, 0)))
            kernel = conv_w.T[:, None, :]
            conv = jax.lax.conv_general_dilated(vpad, kernel, window_strides=(1,), padding='VALID', dimension_numbers=('NWC', 'WIO', 'NWC'), feature_group_count=D_INNER)
            v = jax.nn.silu(conv)
            bc = (v @ w_bc).reshape(Bsz, T, N_HEADS, 2, D_STATE)
            Bm = _l2norm(bc[..., 0, :])
            Cm = _l2norm(bc[..., 1, :])
            p = params.reshape(Bsz, T, N_HEADS, PARAM_DIM)
            A = jax.nn.softplus(p[..., 0])
            dt = jax.nn.sigmoid(p[..., 1])
            S = 1.0 / (1.0 + dt * dt * A)
            u = v.reshape(Bsz, T, N_HEADS, D_HEAD)
            tfirst = lambda a: jnp.moveaxis(a, 1, 0)

            def step(carry, inp):
                z, xs = carry
                Bt, Ct, At, dtt, St, ut = inp
                d = dtt[..., None, None]
                a = At[..., None, None]
                s = St[..., None, None]
                bu = Bt[..., :, None] * ut[..., None, :]
                z = s * (z - d * a * xs + d * bu)
                xs = xs + d * z
                y = jnp.einsum('bhn,bhnp->bhp', Ct, xs)
                return ((z, xs), y)
            z0 = jnp.zeros((Bsz, N_HEADS, D_STATE, D_HEAD), x.dtype)
            _, ys = jax.lax.scan(step, (z0, z0), (tfirst(Bm), tfirst(Cm), tfirst(A), tfirst(dt), tfirst(S), tfirst(u)))
            y = jnp.moveaxis(ys, 0, 1)
            gated = (y + D_skip[None, None, :, None] * u) * jax.nn.silu(gate).reshape(Bsz, T, N_HEADS, D_HEAD)
            return gated.reshape(Bsz, T, D_INNER) @ w_out
        x = x + _mixer(_rmsnorm(x, norm1_w), w_in, conv_w, w_bc, D_skip, w_out)
        h = _rmsnorm(x, norm2_w)
        return x + (jax.nn.gelu(h @ ff_w1 + ff_b1) @ ff_w2 + ff_b2)

    def _L0_ffn_ref(x, gate_w, w13, w2, norm_w):
        import jax, jax.numpy as jnp
        import numpy as np
        import math
        B, S, D = (4, 1024, 192)
        E = 8
        TOP_K = 2
        H = 512
        CAP_F = 1.25
        EPS = 1e-06
        ALPHA = 1.0
        Bx, Sx, Dx = x.shape
        N = Bx * Sx
        cap = int(math.ceil(CAP_F * TOP_K * N / E))
        xf = x.reshape(N, Dx)
        logits = xf.astype(jnp.float32) @ gate_w.T
        probs = jax.nn.softmax(logits, axis=-1)
        top_p, top_i = jax.lax.top_k(probs, TOP_K)
        w = top_p / jnp.sum(top_p, axis=-1, keepdims=True)
        flat_e = top_i.reshape(-1)
        onehot = jax.nn.one_hot(flat_e, E, dtype=jnp.int32)
        pos = jnp.take_along_axis(jnp.cumsum(onehot, axis=0) - 1, flat_e[:, None], axis=1)[:, 0]
        keep = pos < cap
        didx = flat_e * cap + jnp.minimum(pos, cap - 1)
        safe = jnp.where(keep, didx, E * cap)
        x_rep = jnp.repeat(xf, TOP_K, axis=0)
        buf = jnp.zeros((E * cap + 1, Dx), x.dtype).at[safe].set(x_rep)
        buf = buf[:-1].reshape(E, cap, Dx)
        z = 2.0 * buf
        z = z * jax.lax.rsqrt(jnp.mean(z * z, axis=-1, keepdims=True) + EPS)
        z = z * norm_w[:, None, :]
        gu = jnp.einsum('ecd,ehd->ech', z, w13)
        g, u = jnp.split(gu, 2, axis=-1)
        y = buf + ALPHA * jnp.einsum('ech,edh->ecd', jax.nn.silu(g) * u, w2)
        y_tok = y.reshape(E * cap, Dx)[didx]
        cw = (w.reshape(-1) * keep.astype(w.dtype)).astype(x.dtype)
        out = (cw[:, None] * y_tok).reshape(N, TOP_K, Dx).sum(axis=1)
        return out.reshape(Bx, Sx, Dx)
    h = _L0_tok_ref(x, L0_tok_w, L0_tok_b, L0_tok_cls_token, L0_tok_pos_embedding)
    h = jnp.concatenate([h, txt], axis=1)
    h = h + _L0_attn_ref(_layernorm(h, axis=-1), L0_attn_norm1_w, L0_attn_w_in, L0_attn_conv_w, L0_attn_w_bc, L0_attn_D_skip, L0_attn_w_out, L0_attn_norm2_w, L0_attn_ff_w1, L0_attn_ff_b1, L0_attn_ff_w2, L0_attn_ff_b2)
    h = h + _L0_ffn_ref(_layernorm(h, axis=-1), L0_ffn_gate_w, L0_ffn_w13, L0_ffn_w2, L0_ffn_norm_w)
    return h

_drawn_inputs = setup_inputs


def setup_inputs(seed=0):
    import zlib

    import numpy as np

    out = dict(_drawn_inputs(seed))
    spreads = {'L0_attn_norm1_w': (1.0, 0.2),
     'L0_attn_norm2_w': (1.0, 0.2),
     'L0_attn_ff_b1': (0.0, 0.1),
     'L0_attn_ff_b2': (0.0, 0.1),
     'L0_ffn_norm_w': (1.0, 0.6)}
    factors = {'L0_tok_b': 3.151, 'L0_ffn_gate_w': 4.142, 'L0_ffn_w13': 8.0, 'L0_ffn_w2': 8.0}
    for name, (base, spread) in spreads.items():
        noise = np.random.default_rng([zlib.crc32(name.encode()), seed]).standard_normal(out[name].shape)
        drawn = base * np.exp(spread * noise) if base else spread * noise
        out[name] = jnp.asarray(drawn.astype(out[name].dtype))
    for name, factor in factors.items():
        out[name] = (out[name] * factor).astype(out[name].dtype)
    return out
```

```python
from contextlib import ExitStack

import concourse.bass as bass
from concourse import mybir
from concourse.bass import IndirectOffsetOnAxis

F32 = mybir.dt.float32
I32 = mybir.dt.int32
ALU = mybir.AluOpType
ACT = mybir.ActivationFunctionType
AX = mybir.AxisListType

B = 16
D = 192
K2 = D // 2
GRID = 27
BLK = 28
NPATCH = GRID * GRID
NTXT = 77
T = 1 + NPATCH + NTXT
L = 120
CH = 7
TP = CH * L
NT = B * CH
N = B * TP
GT4 = 4
NG = NT // GT4
GW = GT4 * L
H = 6
P = 64
DI = H * P
NS = 8
SEQ = H * B
EP = H * 2 * NS
ROWS = 4
STEPS = 15
PAD = L - 1
KW = L + 2
FF = 768
NE = 8
HID = 512
CAP = -(-(2 * B * T * 5) // (4 * NE))
ES = 4096
SG = 512
LN_EPS = 1e-5
RMS_EPS = 1e-6
L2_EPS = 1e-12


AHEAD = 12


def done(n):
    return n + 1 + AHEAD


def start_counts(eng, *sems):
    for s in sems:
        eng.sem_inc(s, AHEAD)


def settle(eng, settled):
    eng.sem_inc(settled, 1)


class Space:

    def __init__(self, nc, outer):
        self.nc, self.outer = nc, outer
        self.settled = self.sem("settled")

    def phase(self):
        return ExitStack()

    def sb(self, ctx, name, shape, dt=F32):
        return ctx.enter_context(self.nc.sbuf_tensor(name, shape, dt))

    def ps(self, ctx, name, shape, dt=F32):
        return ctx.enter_context(self.nc.psum_tensor(name, shape, dt))

    def sem(self, name):
        return self.outer.enter_context(self.nc.semaphore(name))


def row_tiles(buf, g):
    return buf[bass.ds(g * GW, GW), :].rearrange("(j p) d -> p j d", p=L)


def tokenizer(nc, sp, blocks, tok_w, tok_b, cls, pos, txt, h_rows, slots):
    with sp.phase() as ctx:
        tiles = -(-GRID // ROWS)
        rows_of = [min(ROWS, GRID - g * ROWS) for g in range(tiles)]
        wide = [r * BLK - 1 for r in rows_of]
        tiles_with = [sum(r < n for n in rows_of) for r in range(ROWS)]

        def patch_rows(rows, r):
            return rows.rearrange("(g c) d -> g c d", c=GRID)[r:GRID:ROWS].rearrange("g c d -> c g d")

        main = sp.sb(ctx, "tk_main", [128, 2, BLK * BLK])
        rest = sp.sb(ctx, "tk_rest", [128, 2, BLK * BLK])
        w_main = sp.sb(ctx, "tk_w_main", [128, 4, D])
        w_rest = sp.sb(ctx, "tk_w_rest", [128, 2, D])
        bias = sp.sb(ctx, "tk_bias", [128, D])
        posb = sp.sb(ctx, "tk_posb", [ROWS * BLK, tiles, D])
        out = sp.sb(ctx, "tk_out", [ROWS * BLK, 2, tiles, D])
        zeros = sp.sb(ctx, "tk_zeros", [128, 8192])
        clsrow = sp.sb(ctx, "tk_clsrow", [B, D])
        posrow = sp.sb(ctx, "tk_posrow", [B, D])
        acc = sp.ps(ctx, "tk_acc", [128, 2, 512])
        s_const, s_zero, s_zout = sp.sem("tk_const"), sp.sem("tk_zero"), sp.sem("tk_zeroed")
        s_in = [sp.sem("tk_in0"), sp.sem("tk_in1")]
        s_mm, s_ev, s_posb = sp.sem("tk_mm"), sp.sem("tk_ev"), sp.sem("tk_posb_ready")
        s_st = [sp.sem("tk_st0"), sp.sem("tk_st1")]
        s_cls, s_misc = sp.sem("tk_cls"), sp.sem("tk_misc")
        hb = h_rows.rearrange("(b t) d -> b t d", b=B)
        with nc.Block() as block:
            @block.sync
            def _(eng):
                start_counts(eng, *s_st, s_ev)
                eng.dma_start(w_main[:, :, :], tok_w[0:128].rearrange("f a b d -> f (a b) d")).then_inc(s_const, 16)
                for dc in range(2):
                    eng.dma_start(w_rest[64 * dc:64 * dc + 64, :, :], tok_w[128:192, :, dc, :]).then_inc(s_const, 16)

                def load(b, p):
                    img = blocks[:, bass.ds(b, 1), :].rearrange("f o n -> f (o n)")
                    eng.dma_start(main[:, p, :], img[0:128, :]).then_inc(s_in[p], 16)
                    eng.dma_start(rest[0:64, p, :], img[128:192, :]).then_inc(s_in[p], 16)
                    eng.dma_start(rest[64:128, p, 0:BLK * BLK - 1], img[128:192, 1:BLK * BLK]).then_inc(s_in[p], 16)

                for p in range(2):
                    load(p, p)
                with eng.Fori(0, B // 2 - 1) as i:
                    for p in range(2):
                        eng.wait_ge(s_mm, 14 * i + 7 * p + 7)
                        load(2 * i + p + 2, p)

            @block.scalar
            def _(eng):
                eng.wait_ge(s_zero, 2)
                for r in range(ROWS):
                    eng.dma_start(posb[r * BLK:r * BLK + GRID, 0:tiles_with[r], :],
                                  patch_rows(pos[1:1 + NPATCH, :], r)).then_inc(s_const, 16)
                eng.dma_start(bias[:, :], tok_b.rearrange("(o d) -> o d", o=1).to_broadcast([128, D])).then_inc(s_const, 16)
                eng.dma_start(clsrow[:, :], cls.to_broadcast([B, D])).then_inc(s_const, 16)
                eng.dma_start(posrow[:, :], pos[0:1, :].to_broadcast([B, D])).then_inc(s_const, 16)
                eng.dma_start(hb[:, 1 + NPATCH:T, :], txt).then_inc(s_misc, 16)
                eng.wait_ge(s_cls, 1)
                eng.dma_start(hb[:, 0, :], clsrow[:, :]).then_inc(s_misc, 16)
                eng.dma_start(hb[:, T:TP, :], zeros[0:B, 0:(TP - T) * D].rearrange("b (t d) -> b t d", d=D)).then_inc(s_misc, 16)
                view = slots.rearrange("(p r) d -> p (r d)", p=128)
                for i in range(6):
                    eng.dma_start(view[:, 8192 * i:8192 * (i + 1)], zeros[:, :]).then_inc(s_zout, 16)
                with eng.Fori(0, B // 2) as i:
                    for p in range(2):
                        b = 2 * i + p
                        eng.wait_ge(s_ev, AHEAD + 7 * b + 7)
                        img = hb[bass.ds(b, 1), 1:1 + NPATCH, :].rearrange("o t d -> (o t) d")
                        for r in range(ROWS):
                            eng.dma_start(patch_rows(img, r), out[r * BLK:r * BLK + GRID, p, 0:tiles_with[r], :]).then_inc(s_st[p], 16)
                for p in range(2):
                    eng.wait_ge(s_st[p], AHEAD + 16 * ROWS * (B // 2))
                eng.wait_ge(s_misc, 48)
                eng.wait_ge(s_zout, 96)

            @block.gpsimd
            def _(eng):
                eng.memset(posb[:, :, :], 0.0).then_inc(s_zero, 1)
                eng.memset(zeros[:, :], 0.0).then_inc(s_zero, 1)

            @block.vector
            def _(eng):
                eng.wait_ge(s_const, 16 * 10)
                for g in range(tiles):
                    eng.tensor_tensor(posb[:, g, :], posb[:, g, :], bias[0:ROWS * BLK, :], ALU.add).then_inc(s_posb, 1)
                eng.tensor_tensor(clsrow[:, :], clsrow[:, :], posrow[:, :], ALU.add).then_inc(s_cls, 1)
                eng.wait_ge(s_posb, 7)
                with eng.Fori(0, B // 2) as i:
                    for p in range(2):
                        eng.wait_ge(s_st[p], AHEAD + 16 * ROWS * i)
                        for g in range(7):
                            m = wide[g]
                            eng.wait_ge(s_mm, 14 * i + 7 * p + g + 1)
                            eng.tensor_tensor(out[0:m, p, g, :], acc[0:m, (7 * p + g) % 2, 0:D],
                                              posb[0:m, g, :], ALU.add).then_inc(s_ev, 1)

            @block.tensor
            def _(eng):
                eng.wait_ge(s_const, 16 * 10)
                with eng.Fori(0, B // 2) as i:
                    for p in range(2):
                        eng.wait_ge(s_in[p], 48 * i + 48)
                        for g in range(tiles):
                            m = wide[g]
                            n = 14 * i + 7 * p + g
                            if 7 * p + g >= 2:
                                eng.wait_ge(s_ev, AHEAD + n - 1)
                            else:
                                eng.wait_ge(s_ev, AHEAD + 14 * i)
                            o = acc[0:m, (7 * p + g) % 2, 0:D]
                            for dr in range(2):
                                at = (g * ROWS + dr) * BLK
                                for dc in range(2):
                                    eng.matmul(o, main[:, p, at + dc:at + dc + m], w_main[:, 2 * dr + dc, :],
                                               start=(dr == 0 and dc == 0), stop=False)
                                mm = eng.matmul(o, rest[:, p, at:at + m], w_rest[:, dr, :],
                                                start=False, stop=(dr == 1))
                            mm.then_inc(s_mm, 1)


def normalise(nc, sp, c, h_rows, w_in, norm1, x_rows, xt, params):
    with sp.phase() as ctx:
        ident = sp.sb(ctx, "nm_ident", [128, 128])
        wp = sp.sb(ctx, "nm_wp", [K2, 2, 2 * H])
        n1 = sp.sb(ctx, "nm_n1", [K2, 2])
        half = sp.sb(ctx, "nm_half", [128, GT4])
        h = sp.sb(ctx, "nm_h", [L, 2, GT4, D])
        st = sp.sb(ctx, "nm_st", [L, 2, GT4, 6])
        mv = sp.sb(ctx, "nm_mv", [L, 2, GT4, 2])
        sc = sp.sb(ctx, "nm_sc", [L, 2, 4, GT4])
        x = sp.sb(ctx, "nm_x", [L, 2, GT4, D])
        xr = sp.sb(ctx, "nm_xr", [L, 2, GT4, D])
        xts = sp.sb(ctx, "nm_xts", [K2, 2, 2, GW])
        pts = sp.sb(ctx, "nm_pts", [2 * H, 2, GW])
        tp = sp.ps(ctx, "nm_tp", [128, 4, 512])
        pp = sp.ps(ctx, "nm_pp", [128, 2, 512])
        s_const, s_w, s_half = sp.sem("nm_const"), sp.sem("nm_w"), sp.sem("nm_half_set")
        s_in = [sp.sem("nm_in0"), sp.sem("nm_in1")]
        s_mv, s_sc, s_x, s_xr = sp.sem("nm_mv"), sp.sem("nm_sc"), sp.sem("nm_x"), sp.sem("nm_xr")
        s_tp, s_xt, s_pp, s_pt = sp.sem("nm_tp"), sp.sem("nm_xt"), sp.sem("nm_pp"), sp.sem("nm_pt")
        s_st = [sp.sem("nm_st0"), sp.sem("nm_st1")]
        s_link, s_glink = sp.sem("nm_link"), sp.sem("nm_glink")

        with nc.Block() as block:
            @block.sync
            def _(eng):
                eng.dma_start(ident[:, :], c["ident"]).then_inc(s_const, 16)
                eng.dma_start(wp[:, :, :], w_in[:, 2 * DI:2 * DI + 2 * H].rearrange("(k p) n -> p k n", p=K2)).then_inc(s_const, 16)
                eng.dma_start(n1[:, :], norm1).then_inc(s_const, 16)
                start_counts(eng, *s_st, s_x, s_xr, s_tp, s_xt, s_pt)
                for p in range(2):
                    eng.dma_start(h[:, p, :, :], row_tiles(h_rows, p)).then_inc(s_in[p], 16)
                with eng.Fori(0, NG // 2 - 1) as i:
                    for p in range(2):
                        eng.wait_ge(s_x, done(2 * i + p))
                        eng.dma_start(h[:, p, :, :], row_tiles(h_rows, 2 * i + p + 2)).then_inc(s_in[p], 16)

            @block.vector
            def _(eng):
                eng.wait_ge(s_const, 48)
                for k in range(2):
                    eng.tensor_scalar(wp[:, k, :], wp[:, k, :], n1[:, k:k + 1], None, ALU.mult).then_inc(s_w, 1)
                with eng.Fori(0, NG // 2) as i:
                    for p in range(2):
                        eng.wait_ge(s_in[p], 16 * i + 16)
                        for j in range(GT4):
                            eng.bn_stats(st[:, p, j, :], h[:, p, j, :]).then_inc(s_link, 1)
                        eng.wait_ge(s_link, 8 * i + 4 * p + 4)
                        settle(eng, sp.settled)
                        for j in range(GT4):
                            mm = eng.bn_aggr(mv[:, p, j, :], st[:, p, j, :])
                        mm.then_inc(s_mv, 1)
                        eng.wait_ge(s_sc, 2 * i + p + 1)
                        eng.wait_ge(s_st[p], AHEAD + 48 * i)
                        for j in range(GT4):
                            mm = eng.tensor_scalar(x[:, p, j, :], h[:, p, j, :], mv[:, p, j, 0:1], sc[:, p, 0, j:j + 1],
                                                   ALU.subtract, ALU.mult)
                        mm.then_inc(s_x, 1)
                        eng.wait_ge(s_pp, 2 * i + p + 1)
                        eng.tensor_copy(pts[:, p, :], pp[0:2 * H, p, 0:GW]).then_inc(s_pt, 1)

            @block.gpsimd
            def _(eng):
                eng.memset(half[:, :], -0.5).then_inc(s_half, 1)
                eng.wait_ge(s_half, 1)
                with eng.Fori(0, NG // 2) as i:
                    for p in range(2):
                        steps = [0]

                        def link(ins):
                            steps[0] += 1
                            ins.then_inc(s_glink, 1)
                            eng.wait_ge(s_glink, 10 * i + 5 * p + steps[0])
                            settle(eng, sp.settled)

                        eng.wait_ge(s_mv, 2 * i + p + 1)
                        eng.wait_ge(s_xr, done(2 * i + p - 2))
                        settle(eng, sp.settled)
                        rstd, r, tmp, tm2 = (sc[:, p, q, :] for q in range(4))
                        link(eng.tensor_scalar(tmp, mv[:, p, :, 1], LN_EPS, None, ALU.add))
                        link(eng.tensor_tensor(rstd, tmp, half[0:L, :], ALU.pow))
                        link(eng.tensor_tensor(tm2, rstd, rstd, ALU.mult))
                        link(eng.tensor_tensor(tm2, tm2, mv[:, p, :, 1], ALU.mult))
                        link(eng.tensor_scalar(tm2, tm2, RMS_EPS, None, ALU.add))
                        eng.tensor_tensor(r, tm2, half[0:L, :], ALU.pow).then_inc(s_sc, 1)

            @block.scalar
            def _(eng):
                with eng.Fori(0, NG // 2) as i:
                    for p in range(2):
                        g = 2 * i + p
                        eng.wait_ge(s_x, done(g))
                        eng.wait_ge(s_tp, done(g - 2))
                        for j in range(GT4):
                            mm = eng.activation(xr[:, p, j, :], x[:, p, j, :], ACT.Copy, scale=sc[:, p, 1, j:j + 1])
                        mm.then_inc(s_xr, 1)
                        eng.wait_ge(s_st[p], AHEAD + 48 * i)
                        eng.wait_ge(s_tp, done(g))
                        for k in range(2):
                            mm = eng.activation(xts[:, p, k, :], tp[0:K2, 2 * p + k, 0:GW], ACT.Copy)
                        mm.then_inc(s_xt, 1)
                        eng.dma_start(row_tiles(x_rows, g), x[:, p, :, :]).then_inc(s_st[p], 16)
                        eng.wait_ge(s_xt, done(g))
                        eng.dma_start(xt[:, :, bass.ds(g * GW, GW)], xts[:, p, :, :]).then_inc(s_st[p], 16)
                        eng.wait_ge(s_pt, done(g))
                        eng.dma_start(params[:, bass.ds(g * GW, GW)], pts[:, p, :]).then_inc(s_st[p], 16)
                for p in range(2):
                    eng.wait_ge(s_st[p], AHEAD + 48 * (NG // 2))

            @block.tensor
            def _(eng):
                eng.wait_ge(s_w, 2)
                with eng.Fori(0, NG // 2) as i:
                    for p in range(2):
                        g = 2 * i + p
                        eng.wait_ge(s_xr, done(g))
                        eng.wait_ge(s_xt, done(g - 2))
                        for k in range(2):
                            for j in range(GT4):
                                mm = eng.transpose(tp[0:K2, 2 * p + k, L * j:L * j + L],
                                                   xr[:, p, j, K2 * k:K2 * k + K2], ident[0:L, 0:L])
                        mm.then_inc(s_tp, 1)
                        eng.wait_ge(s_xt, done(g))
                        eng.wait_ge(s_pt, done(g - 2))
                        for k in range(2):
                            mm = eng.matmul(pp[0:2 * H, p, 0:GW], wp[:, k, :], xts[:, p, k, :], start=(k == 0), stop=(k == 1))
                        mm.then_inc(s_pp, 1)


def mixer(nc, sp, c, x_rows, xt, params, x2_rows):
    with sp.phase() as ctx:
        def sb(name, shape):
            return sp.sb(ctx, "mx_" + name, shape)

        def sem(name):
            return sp.sem("mx_" + name)

        ident = sb("ident", [128, 128])
        wg = sb("wg", [K2, 2, 2 * DI])
        n1 = sb("n1", [K2, 2])
        wbc = sb("wbc", [128, 3, EP])
        wout = sb("wout", [128, 3, D])
        cw = sb("cw", [128, 3, 4])
        dskip = sb("dskip", [L, H])
        block_mask = sb("block_mask", [EP, DI])
        step_mask = sb("step_mask", [EP, EP])
        head_mask = sb("head_mask", [H * NS, H * L])
        spread = sb("spread", [SEQ, 2, EP])
        image_mask = sb("image_mask", [SEQ, B])
        half = sb("half", [L, 2 * H])
        s_all, d_all, n_all, tmp_all = (sb(n, [SEQ, TP]) for n in ("s", "d", "n", "t"))
        ring = sb("ring", [SEQ, STEPS, PAD + KW])
        z = sb("z", [SEQ, PAD + KW])
        zt = sb("zt", [SEQ, KW])
        unit_rows = sb("unit_rows", [SEQ, 2, L])
        kern = sb("kern", [L, L, SEQ])
        coef = sb("coef", [L, 4, SEQ])
        phi_rhs = sb("phi_rhs", [SEQ, 2, 2, B])
        phi = sb("phi", [EP, 2, B])
        halo = sb("halo", [128, B, 3, 3])
        state = sb("state", [EP, B, DI])
        xts = sb("xts", [K2, 2, 2, L])
        xin = sb("xin", [L, 2, D])
        vb = sb("vb", [128, 2, 3, 3 + L])
        cv = sb("cv", [128, 2, 3, L])
        vt = sb("vt", [128, 2, 3, L])
        u = sb("u", [L, 2, DI])
        ud = sb("ud", [L, 2, DI])
        sg = sb("sg", [L, 2, DI])
        sq = sb("sq", [L, 2, EP])
        rs = sb("rs", [L, 2, 2 * H])
        rn = sb("rn", [L, 2, 2 * H])
        bcn = sb("bcn", [L, 2, EP])
        br = sb("br", [L, 2, EP])
        cr = sb("cr", [L, 2, EP])
        tb = sb("tb", [EP, 2, EP])
        bt = sb("bt", [H * NS, 2, L])
        cm = sb("cm", [H * NS, 2, H, L])
        crt = sb("crt", [EP, 2, L])
        m = sb("m", [L, 2, H, L])
        gy = sb("gy", [L, 2, DI])
        gyt = sb("gyt", [128, 2, 3, L])
        x2 = sb("x2", [L, 2, D])

        bank = [sp.ps(ctx, f"mx_bank{i}", [128, 512]) for i in range(8)]
        b_v, b_gate, b_bc, b_u, b_s0, b_s1, b_y, b_st = bank
        b_s = (b_s0, b_s1)

        s_const, s_w, s_mem, s_par = sem("const"), sem("w"), sem("mem"), sem("par")
        s_xt = [sem("xt0"), sem("xt1")]
        s_xin = [sem("xin0"), sem("xin1")]
        s_store = [sem("store0"), sem("store1")]
        s_prep, s_alink = sem("prep"), sem("prep_act")
        s_conv_part = sem("conv_part")
        s_start, s_ring, s_link = sem("start"), sem("ring"), sem("link")
        s_kt, s_kern, s_unit = sem("kernel_transposed"), sem("kernel_kept"), sem("unit_rows")
        s_ct, s_coef, s_pr, s_pm, s_phi = sem("coef_t"), sem("coef"), sem("phi_rhs"), sem("phi_mm"), sem("phi")
        names = ("vmm", "gmm", "vtaken", "halo_in", "halo_out", "conv", "silu", "bcmm", "ut", "sq", "u", "gate",
                 "rs", "rn", "bcn", "br", "cr", "tb", "tr", "cm", "bt", "crt", "smm", "m", "ymm", "stmm", "st",
                 "ud", "gsum", "gy", "gyt_mm", "gyt", "omm", "x2", "rlink")
        e = {n: sem(n) for n in names}

        def tile(buf, k_c, k_b):
            return buf[bass.ds((k_b * CH + k_c) * L, L), :]

        with nc.Block() as block:
            @block.sync
            def _(eng):
                start_counts(eng, *s_store, s_kt, s_ct, s_pm, s_kern, s_link, *e.values())
                for dst, name in ((ident, "ident"), (block_mask, "block_mask"), (step_mask, "step_mask"),
                                  (head_mask, "head_mask"), (image_mask, "image_mask"), (n1, "norm1")):
                    eng.dma_start(dst[:, :], c[name]).then_inc(s_const, 16)
                for dst, name in ((spread, "spread"), (cw, "conv_w")):
                    eng.dma_start(dst[:, :, :], c[name]).then_inc(s_const, 16)
                eng.dma_start(wg[:, :, :], c["w_in"][:, 0:2 * DI].rearrange("(k p) n -> p k n", p=K2)).then_inc(s_const, 16)
                eng.dma_start(wbc[:, :, :], c["w_bc"].rearrange("(k p) n -> p k n", p=128)).then_inc(s_const, 16)
                eng.dma_start(wout[:, :, :], c["w_out"].rearrange("(k p) n -> p k n", p=128)).then_inc(s_const, 16)
                eng.dma_start(dskip[:, :], c["d_skip"].rearrange("(o h) -> o h", o=1).to_broadcast([L, H])).then_inc(s_const, 16)
                pv = params.rearrange("(q h) (b t) -> q h b t", q=2, b=B)
                for h in range(H):
                    eng.dma_start(s_all[h * B:(h + 1) * B, :], pv[0, h]).then_inc(s_par, 16)
                    eng.dma_start(d_all[h * B:(h + 1) * B, :], pv[1, h]).then_inc(s_par, 16)
                xtv = xt.rearrange("p k (b t) -> p k b t", b=B)
                with eng.Fori(0, CH) as ci:
                    with eng.Fori(0, B // 2) as bi:
                        for p in range(2):
                            b = 2 * bi + p
                            k = ci * B + b
                            eng.wait_ge(e["gmm"], done(k - 2))
                            src = xtv[:, :, bass.ds(b, 1), bass.ds(ci * L, L)].rearrange("p k o t -> p k (o t)")
                            eng.dma_start(xts[:, p, :, :], src).then_inc(s_xt[p], 16)
                            eng.wait_ge(e["x2"], done(k - 2))
                            eng.dma_start(xin[:, p, :], tile(x_rows, ci, b)).then_inc(s_xin[p], 16)

            @block.gpsimd
            def _(eng):
                eng.memset(half[:, :], -0.5).then_inc(s_mem, 1)
                eng.memset(halo[:, :, :, :], 0.0).then_inc(s_mem, 1)
                eng.memset(state[:, :, :], 0.0).then_inc(s_mem, 1)
                eng.wait_ge(s_mem, 3)
                eng.wait_ge(s_const, 16 * 12)
                with eng.Fori(0, CH) as ci:
                    with eng.Fori(0, B // 2) as bi:
                        for p in range(2):
                            b = 2 * bi + p
                            k = ci * B + b
                            eng.wait_ge(e["conv"], done(k - 2))
                            eng.wait_ge(e["halo_out"], done(k - 1))
                            settle(eng, sp.settled)
                            hb = halo[:, bass.ds(b, 1), :, :].rearrange("p o f t -> p (o f) t")
                            eng.tensor_copy(vb[:, p, :, 0:3], hb).then_inc(e["halo_in"], 1)
                            eng.wait_ge(e["vtaken"], done(k))
                            eng.wait_ge(e["halo_in"], done(k))
                            settle(eng, sp.settled)
                            eng.tensor_copy(hb, vb[:, p, :, L:L + 3]).then_inc(e["halo_out"], 1)
                            if p == 0:
                                eng.wait_ge(s_phi, ci + 1)
                            eng.wait_ge(e["stmm"], done(k - 2))
                            settle(eng, sp.settled)
                            pb = phi[:, :, bass.ds(b, 1)].unsqueeze(1).to_broadcast([EP, H, 2, NS])
                            eng.tensor_tensor(tb[:, p, :].rearrange("q (h j n) -> q h j n", h=H, j=2),
                                              step_mask[:, :].rearrange("q (h j n) -> q h j n", h=H, j=2), pb,
                                              ALU.mult).then_inc(e["tb"], 1)
                            eng.wait_ge(e["rs"], done(k))
                            eng.wait_ge(e["bcn"], done(k - 2))
                            settle(eng, sp.settled)
                            eng.tensor_scalar(rs[:, p, :], rs[:, p, :], L2_EPS, None, ALU.add).then_inc(e["rlink"], 1)
                            eng.wait_ge(e["rlink"], done(k))
                            settle(eng, sp.settled)
                            eng.tensor_tensor(rn[:, p, :], rs[:, p, :], half[:, :], ALU.pow).then_inc(e["rn"], 1)
                            eng.wait_ge(e["u"], done(k))
                            eng.wait_ge(e["gsum"], done(k - 2))
                            settle(eng, sp.settled)
                            eng.tensor_tensor(ud[:, p, :].rearrange("t (h q) -> t h q", h=H),
                                              u[:, p, :].rearrange("t (h q) -> t h q", h=H),
                                              dskip[:, :].unsqueeze(2).to_broadcast([L, H, P]), ALU.mult).then_inc(e["ud"], 1)
                            eng.wait_ge(e["bcn"], done(k))
                            eng.wait_ge(e["tr"], done(k - 2))
                            settle(eng, sp.settled)
                            for dst, off, q0, name in ((cr, H * NS, 0, "cr"), (br, 0, 2, "br")):
                                src = bcn[:, p, off:off + H * NS].rearrange("t (h n) -> t h n", h=H)
                                for j in range(2):
                                    w = coef[:, q0 + j, :].rearrange("t (h b) -> t h b", h=H)[:, :, bass.ds(b, 1)]
                                    ins = eng.tensor_tensor(dst[:, p, :].rearrange("t (h j n) -> t h j n", h=H, j=2)[:, :, j, :],
                                                            src, w.to_broadcast([L, H, NS]), ALU.mult)
                                ins.then_inc(e[name], 1)

            @block.scalar
            def _(eng):
                eng.wait_ge(s_prep, 1)
                eng.activation(tmp_all[:, :], tmp_all[:, :], ACT.Exp, scale=-1.0).then_inc(s_alink, 1)
                eng.wait_ge(s_alink, 1)
                eng.activation(tmp_all[:, :], tmp_all[:, :], ACT.Ln, bias=1.0).then_inc(s_alink, 1)
                eng.activation(d_all[:, :], d_all[:, :], ACT.Exp, scale=-1.0).then_inc(s_alink, 1)
                with eng.Fori(0, CH) as ci:
                    with eng.Fori(0, L // STEPS) as qi:
                        for r in range(0, STEPS, 5):
                            eng.wait_ge(s_kt, AHEAD + 24 * ci + 3 * qi + r // 5 + 1)
                            eng.activation(kern[:, bass.ds(qi * STEPS + r, 5), :],
                                           bank[4 + r // 5][0:L, 0:5 * SEQ].rearrange("t (r s) -> t r s", r=5), ACT.Copy).then_inc(s_kern, 1)
                    eng.wait_ge(s_ct, AHEAD + ci + 1)
                    eng.activation(coef[:, :, :], b_s0[0:L, 0:4 * SEQ].rearrange("t (q s) -> t q s", q=4), ACT.Copy).then_inc(s_coef, 1)
                    eng.wait_ge(s_pm, AHEAD + ci + 1)
                    eng.activation(phi[:, :, :], b_s1[0:EP, 0:2 * B].rearrange("q (j b) -> q j b", j=2), ACT.Copy).then_inc(s_phi, 1)
                    with eng.Fori(0, B // 2) as bi:
                        for p in range(2):
                            b = 2 * bi + p
                            k = ci * B + b
                            eng.wait_ge(e["vmm"], done(k))
                            eng.wait_ge(e["conv"], done(k - 2))
                            eng.wait_ge(e["halo_out"], done(k - 2))
                            eng.activation(vb[:, p, :, 3:3 + L], b_v[:, 0:3 * L].rearrange("q (f t) -> q f t", f=3), ACT.Copy).then_inc(e["vtaken"], 1)
                            eng.wait_ge(e["gmm"], done(k))
                            eng.wait_ge(e["gy"], done(k - 2))
                            eng.activation(sg[:, p, :], b_gate[0:L, 0:DI], ACT.Silu).then_inc(e["gate"], 1)
                            eng.wait_ge(e["conv"], done(k))
                            eng.wait_ge(e["ut"], done(k - 2))
                            eng.activation(vt[:, p, :, :], cv[:, p, :, :], ACT.Silu).then_inc(e["silu"], 1)
                            eng.wait_ge(e["bcmm"], done(k))
                            eng.wait_ge(e["rs"], done(k - 2))
                            eng.activation(sq[:, p, :], b_bc[0:L, 0:EP], ACT.Square).then_inc(e["sq"], 1)
                            eng.wait_ge(e["ut"], done(k))
                            eng.wait_ge(e["stmm"], done(k - 2))
                            eng.wait_ge(e["ud"], done(k - 2))
                            eng.activation(u[:, p, :], b_u[0:L, 0:DI], ACT.Copy).then_inc(e["u"], 1)
                            eng.wait_ge(e["cm"], done(k))
                            eng.wait_ge(e["ymm"], done(k - 2))
                            eng.activation(bt[:, p, :], b_bc[0:H * NS, 128:128 + L], ACT.Copy).then_inc(e["bt"], 1)
                            eng.activation(crt[:, p, :], b_bc[0:EP, 128 + 2 * L:128 + 3 * L], ACT.Copy).then_inc(e["crt"], 1)
                            eng.wait_ge(e["gyt_mm"], done(k))
                            eng.wait_ge(e["omm"], done(k - 2))
                            eng.activation(gyt[:, p, :, :], b_u[:, 0:3 * L].rearrange("q (f t) -> q f t", f=3), ACT.Copy).then_inc(e["gyt"], 1)
                            eng.wait_ge(e["x2"], done(k))
                            eng.dma_start(tile(x2_rows, ci, b), x2[:, p, :]).then_inc(s_store[p], 16)
                for p in range(2):
                    eng.wait_ge(s_store[p], AHEAD + 16 * (NT // 2))

            @block.vector
            def _(eng):
                steps = [0]

                def prep(ins):
                    steps[0] += 1
                    ins.then_inc(s_prep, 1)
                    eng.wait_ge(s_prep, steps[0])

                eng.wait_ge(s_par, 16 * 2 * H)
                prep(eng.scalar_tensor_tensor(tmp_all[:, :], s_all[:, :], -1.0, s_all[:, :], ALU.mult, ALU.max))
                eng.wait_ge(s_alink, 3)
                prep(eng.scalar_tensor_tensor(n_all[:, :], s_all[:, :], 0.0, tmp_all[:, :], ALU.max, ALU.add))
                prep(eng.tensor_scalar(d_all[:, :], d_all[:, :], 1.0, None, ALU.add))
                prep(eng.reciprocal(d_all[:, :], d_all[:, :]))
                prep(eng.tensor_tensor(n_all[:, :], n_all[:, :], d_all[:, :], ALU.mult))
                prep(eng.tensor_tensor(tmp_all[:, :], n_all[:, :], d_all[:, :], ALU.mult))
                prep(eng.tensor_scalar(tmp_all[:, :], tmp_all[:, :], 1.0, None, ALU.add))
                prep(eng.reciprocal(s_all[:, :], tmp_all[:, :]))
                prep(eng.scalar_tensor_tensor(n_all[:, :], n_all[:, :], -1.0, s_all[:, :], ALU.mult, ALU.mult))
                eng.wait_ge(s_const, 16 * 12)
                for k in range(2):
                    eng.tensor_scalar(wg[:, k, :], wg[:, k, :], n1[:, k:k + 1], None, ALU.mult).then_inc(s_w, 1)
                with eng.Fori(0, CH) as ci:
                    eng.wait_ge(s_kt, AHEAD + 24 * ci)
                    eng.wait_ge(s_ct, AHEAD + ci)
                    eng.memset(ring[:, :, :], 0.0).then_inc(s_start, 1)
                    eng.memset(z[:, 0:PAD + 2], 0.0).then_inc(s_start, 1)
                    eng.wait_ge(s_start, 5 * ci + 2)
                    eng.memset(ring[:, STEPS - 1, PAD + 1:PAD + 2], 1.0).then_inc(s_start, 1)
                    eng.memset(z[:, PAD:PAD + 1], 1.0).then_inc(s_start, 1)
                    eng.tensor_copy(z[:, PAD + 2:PAD + 2 + L], d_all[:, bass.ds(ci * L, L)]).then_inc(s_start, 1)
                    eng.wait_ge(s_start, 5 * ci + 5)
                    settle(eng, sp.settled)
                    with eng.Fori(0, L // STEPS) as qi:
                        q = ci * (L // STEPS) + qi
                        eng.wait_ge(s_kt, AHEAD + 3 * q)
                        for r in range(STEPS):
                            t = qi * STEPS + r
                            at = ci * L + t
                            zz = z[:, bass.ds(t, KW)]
                            old = ring[:, (r - 1) % STEPS, bass.ds(t, KW)]
                            new = ring[:, r, bass.ds(t, KW)]
                            count = 3 * STEPS * q + 3 * r
                            eng.wait_ge(s_link, AHEAD + count)
                            eng.tensor_scalar(zt[:, :], old, n_all[:, bass.ds(at, 1)], None, ALU.mult).then_inc(s_link, 1)
                            eng.wait_ge(s_link, AHEAD + count + 1)
                            eng.scalar_tensor_tensor(zz, zz, s_all[:, bass.ds(at, 1)], zt[:, :], ALU.mult, ALU.add).then_inc(s_link, 1)
                            eng.wait_ge(s_link, AHEAD + count + 2)
                            eng.scalar_tensor_tensor(new, zz, d_all[:, bass.ds(at, 1)], old, ALU.mult, ALU.add).then_inc(s_link, 1)
                            if r % 5 == 4:
                                eng.wait_ge(s_link, AHEAD + count + 3)
                                eng.tensor_copy(unit_rows[:, :, bass.ds(qi * STEPS + r - 4, 5)].rearrange("s u t -> s t u"),
                                                ring[:, r - 4:r + 1, PAD:PAD + 2]).then_inc(s_ring, 1)
                    eng.wait_ge(s_pm, AHEAD + ci)
                    for to, src in ((0, z[:, PAD:PAD + 2]), (1, ring[:, STEPS - 1, PAD:PAD + 2])):
                        for fr in range(2):
                            eng.tensor_scalar(phi_rhs[:, fr, to, :], image_mask[:, :], src[:, fr:fr + 1], None, ALU.mult).then_inc(s_pr, 1)
                    with eng.Fori(0, B // 2) as bi:
                        for p in range(2):
                            b = 2 * bi + p
                            k = ci * B + b
                            eng.wait_ge(e["vtaken"], done(k))
                            eng.wait_ge(e["halo_in"], done(k))
                            eng.wait_ge(e["silu"], done(k - 2))
                            for f in range(3):
                                eng.tensor_scalar(cv[:, p, f, :], vb[:, p, f, 0:L], cw[:, f, 0:1], None, ALU.mult).then_inc(s_conv_part, 1)
                            for tap in range(1, 4):
                                eng.wait_ge(s_conv_part, 9 * k + 3 * tap)
                                for f in range(3):
                                    ins = eng.scalar_tensor_tensor(cv[:, p, f, :], vb[:, p, f, tap:tap + L], cw[:, f, tap:tap + 1],
                                                                   cv[:, p, f, :], ALU.mult, ALU.add)
                                    if tap < 3:
                                        ins.then_inc(s_conv_part, 1)
                            ins.then_inc(e["conv"], 1)
                            eng.wait_ge(e["sq"], done(k))
                            eng.wait_ge(e["rn"], done(k - 2))
                            eng.tensor_reduce(rs[:, p, :], sq[:, p, :].rearrange("t (g n) -> t g n", n=NS), AX.X, ALU.add).then_inc(e["rs"], 1)
                            eng.wait_ge(e["rn"], done(k))
                            eng.wait_ge(e["br"], done(k - 2))
                            eng.wait_ge(e["tr"], done(k - 2))
                            eng.tensor_tensor(bcn[:, p, :].rearrange("t (g n) -> t g n", n=NS),
                                              b_bc[0:L, 0:EP].rearrange("t (g n) -> t g n", n=NS),
                                              rn[:, p, :].unsqueeze(2).to_broadcast([L, 2 * H, NS]), ALU.mult).then_inc(e["bcn"], 1)
                            eng.wait_ge(e["tr"], done(k))
                            eng.wait_ge(e["smm"], done(k - 2))
                            eng.tensor_tensor(cm[:, p, :, :],
                                              b_bc[0:H * NS, 128 + L:128 + 2 * L].unsqueeze(1).to_broadcast([H * NS, H, L]),
                                              head_mask[:, :].rearrange("q (h t) -> q h t", h=H), ALU.mult).then_inc(e["cm"], 1)
                            eng.wait_ge(e["smm"], done(k))
                            eng.wait_ge(e["ymm"], done(k - 2))
                            eng.wait_ge(s_kern, AHEAD + 24 * ci + 24)
                            for part in range(2):
                                kv = kern[:, :, :].rearrange("q t (h b) -> q h b t", h=H)[:, 3 * part:3 * part + 3, bass.ds(b, 1), :]
                                ins = eng.tensor_tensor(m[:, p, 3 * part:3 * part + 3, :],
                                                        b_s[part][0:L, 0:3 * L].rearrange("q (h t) -> q h t", h=3),
                                                        kv.rearrange("q h o t -> q (h o) t"), ALU.mult)
                            ins.then_inc(e["m"], 1)
                            eng.wait_ge(e["stmm"], done(k))
                            eng.tensor_tensor(state[:, bass.ds(b, 1), :].rearrange("q o n -> q (o n)"),
                                              b_st[0:EP, 0:DI], block_mask[:, :], ALU.mult).then_inc(e["st"], 1)
                            eng.wait_ge(e["ud"], done(k))
                            eng.wait_ge(e["gyt_mm"], done(k - 2))
                            eng.tensor_tensor(gy[:, p, :], b_y[0:L, 0:DI], ud[:, p, :], ALU.add).then_inc(e["gsum"], 1)
                            eng.wait_ge(e["gsum"], done(k))
                            eng.wait_ge(e["gate"], done(k))
                            eng.tensor_tensor(gy[:, p, :], gy[:, p, :], sg[:, p, :], ALU.mult).then_inc(e["gy"], 1)
                            eng.wait_ge(e["omm"], done(k))
                            eng.wait_ge(s_xin[p], 16 * (ci * (B // 2) + bi) + 16)
                            eng.wait_ge(s_store[p], AHEAD + 16 * (ci * (B // 2) + bi))
                            eng.tensor_tensor(x2[:, p, :], b_gate[0:L, 0:D], xin[:, p, :], ALU.add).then_inc(e["x2"], 1)

            @block.tensor
            def _(eng):
                eng.wait_ge(s_const, 16 * 12)
                eng.wait_ge(s_w, 2)
                eng.wait_ge(s_mem, 3)
                with eng.Fori(0, CH) as ci:
                    last = ci * B - 1
                    eng.wait_ge(e["m"], done(last))
                    eng.wait_ge(e["gsum"], done(last))
                    eng.wait_ge(e["br"], done(last))
                    eng.wait_ge(e["tb"], done(last))
                    settle(eng, sp.settled)
                    with eng.Fori(0, L // STEPS) as qi:
                        q = ci * (L // STEPS) + qi
                        for r in range(STEPS):
                            if r % 5 == 0:
                                eng.wait_ge(s_ring, 3 * q + r // 5 + 1)
                                eng.wait_ge(s_kern, AHEAD + 3 * q)
                            mm = eng.transpose(bank[4 + r // 5][0:L, SEQ * (r % 5):SEQ * (r % 5) + SEQ],
                                               ring[:, r, 0:KW + PAD][:, PAD + 2:PAD + 2 + L], ident[0:SEQ, 0:SEQ])
                            if r % 5 == 4:
                                mm.then_inc(s_kt, 1)
                    eng.wait_ge(s_kern, AHEAD + 24 * ci + 24)
                    for q4, src in enumerate((unit_rows[:, 0, :], unit_rows[:, 1, :], z[:, PAD + 2:PAD + 2 + L],
                                              ring[:, STEPS - 1, PAD + 2:PAD + 2 + L])):
                        mm = eng.transpose(b_s0[0:L, SEQ * q4:SEQ * q4 + SEQ], src, ident[0:SEQ, 0:SEQ])
                    mm.then_inc(s_ct, 1)
                    eng.wait_ge(s_pr, 4 * ci + 4)
                    for fr in range(2):
                        mm = eng.matmul(b_s1[0:EP, 0:2 * B], spread[:, fr, :], phi_rhs[:, fr, :, :].rearrange("s j b -> s (j b)"),
                                        start=(fr == 0), stop=(fr == 1))
                    mm.then_inc(s_pm, 1)
                    eng.wait_ge(s_coef, ci + 1)
                    eng.wait_ge(s_phi, ci + 1)
                    settle(eng, sp.settled)
                    with eng.Fori(0, B // 2) as bi:
                        for p in range(2):
                            b = 2 * bi + p
                            k = ci * B + b
                            eng.wait_ge(s_xt[p], 16 * (ci * (B // 2) + bi) + 16)
                            eng.wait_ge(e["vtaken"], done(k - 1))
                            for f in range(3):
                                for kk in range(2):
                                    mm = eng.matmul(b_v[:, L * f:L * f + L], wg[:, kk, DI + 128 * f:DI + 128 * f + 128],
                                                    xts[:, p, kk, :], start=(kk == 0), stop=(kk == 1))
                            mm.then_inc(e["vmm"], 1)
                            eng.wait_ge(e["gate"], done(k - 1))
                            eng.wait_ge(e["x2"], done(k - 1))
                            for kk in range(2):
                                mm = eng.matmul(b_gate[0:L, 0:DI], xts[:, p, kk, :], wg[:, kk, 0:DI],
                                                start=(kk == 0), stop=(kk == 1))
                            mm.then_inc(e["gmm"], 1)
                            eng.wait_ge(e["silu"], done(k))
                            eng.wait_ge(e["bt"], done(k - 1))
                            eng.wait_ge(e["crt"], done(k - 1))
                            eng.wait_ge(e["cm"], done(k - 1))
                            for f in range(3):
                                mm = eng.matmul(b_bc[0:L, 0:EP], vt[:, p, f, :], wbc[:, f, :], start=(f == 0), stop=(f == 2))
                            mm.then_inc(e["bcmm"], 1)
                            eng.wait_ge(e["gyt"], done(k - 1))
                            for f in range(3):
                                mm = eng.transpose(b_u[0:L, 128 * f:128 * f + 128], vt[:, p, f, :], ident[:, :])
                            mm.then_inc(e["ut"], 1)
                            eng.wait_ge(e["bcn"], done(k))
                            eng.wait_ge(e["cr"], done(k))
                            settle(eng, sp.settled)
                            for j in range(2):
                                eng.transpose(b_bc[0:H * NS, 128 + L * j:128 + L * j + L], bcn[:, p, H * NS * j:H * NS * (j + 1)], ident[0:L, 0:L])
                            eng.transpose(b_bc[0:EP, 128 + 2 * L:128 + 3 * L], cr[:, p, :], ident[0:L, 0:L]).then_inc(e["tr"], 1)
                            eng.wait_ge(e["bt"], done(k))
                            eng.wait_ge(e["cm"], done(k))
                            eng.wait_ge(e["m"], done(k - 1))
                            for part in range(2):
                                mm = eng.matmul(b_s[part][0:L, 0:3 * L], bt[:, p, :],
                                                cm[:, p, 3 * part:3 * part + 3, :].rearrange("q h t -> q (h t)"), start=True, stop=True)
                            mm.then_inc(e["smm"], 1)
                            eng.wait_ge(e["crt"], done(k))
                            eng.wait_ge(e["st"], done(k - 1))
                            eng.wait_ge(e["gsum"], done(k - 1))
                            sv = state[:, bass.ds(b, 1), :].rearrange("q o n -> q (o n)")
                            eng.matmul(b_y[0:L, 0:DI], crt[:, p, :], sv, start=True, stop=False)
                            eng.wait_ge(e["m"], done(k))
                            eng.wait_ge(e["u"], done(k))
                            for h in range(H):
                                mm = eng.matmul(b_y[0:L, P * h:P * h + P], m[:, p, h, :], u[:, p, P * h:P * h + P],
                                                start=False, stop=(h == H - 1))
                            mm.then_inc(e["ymm"], 1)
                            eng.wait_ge(e["br"], done(k))
                            eng.wait_ge(e["tb"], done(k))
                            eng.matmul(b_st[0:EP, 0:DI], br[:, p, :], u[:, p, :], start=True, stop=False)
                            eng.matmul(b_st[0:EP, 0:DI], tb[:, p, :], sv, start=False, stop=True).then_inc(e["stmm"], 1)
                            eng.wait_ge(e["gy"], done(k))
                            for f in range(3):
                                mm = eng.transpose(b_u[:, L * f:L * f + L], gy[:, p, 128 * f:128 * f + 128], ident[0:L, 0:L])
                            mm.then_inc(e["gyt_mm"], 1)
                            eng.wait_ge(e["gyt"], done(k))
                            for f in range(3):
                                mm = eng.matmul(b_gate[0:L, 0:D], gyt[:, p, f, :], wout[:, f, :], start=(f == 0), stop=(f == 2))
                            mm.then_inc(e["omm"], 1)


def turns(eng, n, stages, peeled=0):
    deepest = max(lag for lag, _ in stages)
    head = deepest + deepest % 2 + peeled

    def slot(s):
        for lag, f in stages:
            if 0 <= s - lag < n:
                f(s - lag, (s - lag) % 2, (s - lag) // 2)

    for s in range(head):
        slot(s)
    with eng.Fori(head // 2, n // 2) as i:
        for q in range(2):
            for lag, f in stages:
                f(2 * i + (q - lag), (q - lag) % 2, i + (q - lag) // 2)
    for s in range(n, n + deepest):
        slot(s)


def chain(eng, sem, before, settled=None):
    steps = [0]

    def link(ins):
        steps[0] += 1
        ins.then_inc(sem, 1)
        eng.wait_ge(sem, before + steps[0])
        if settled:
            settle(eng, settled)

    return link


class Route:

    def __init__(self, sp, ctx):
        self.mean = sp.sb(ctx, "rt_mean", [L, NT])
        self.rstd = sp.sb(ctx, "rt_rstd", [L, NT])
        self.gap = sp.sb(ctx, "rt_gap", [L, NT])
        self.keep = sp.sb(ctx, "rt_keep", [L, 2, NT])
        self.slot = sp.sb(ctx, "rt_slot", [L, 2, NT])


def feed_forward(nc, sp, c, x2_rows, h_rows, h2_rows, slots, rt):
    NF = FF // 128
    with sp.phase() as ctx:
        def sb(name, shape, dt=F32):
            return sp.sb(ctx, "ff_" + name, shape, dt)

        def sem(name):
            return sp.sem("ff_" + name)

        ident = sb("ident", [128, 128])
        w1 = sb("w1", [K2, 2, FF])
        n2 = sb("n2", [K2, 2])
        w2 = sb("w2", [128, NF, D])
        b1 = sb("b1", [128, NF])
        b2 = sb("b2", [L, D])
        gate = sb("gate", [K2, 2, NE])
        before = sb("before", [L, L])
        ones = sb("ones", [L, L])
        valid = sb("valid", [L, NT])
        expert = sb("expert", [L, NE])
        rank = sb("rank", [L, NE])
        base = sb("base", [L, NE])
        half = sb("half", [L, GT4])
        x2 = sb("x2", [L, 2, GT4, D])
        h = sb("h", [L, 2, GT4, D])
        hx = sb("hx", [L, 2, GT4, D])
        ss = sb("ss", [L, 2, GT4])
        r = sb("r", [L, 2, GT4])
        xr = sb("xr", [L, 2, GT4, D])
        xt = sb("xt", [K2, 2, 2, GW])
        gt = sb("gt", [128, 2, NF, GW])
        h2 = sb("h2", [L, 2, GT4, D])
        st = sb("st", [L, 2, GT4, 6])
        mv = sb("mv", [L, 2, GT4, 2])
        rstd = sb("rstd", [L, 2, GT4])
        q = sb("q", [L, 2, GT4])
        x3 = sb("x3", [L, 2, GT4, D])
        x3t = sb("x3t", [K2, 2, 2, GW])
        z = sb("z", [L, 2, GT4, D])
        lg = sb("lg", [L, 2, GT4, NE])
        mask = sb("mask", [L, 2, 2, GT4, NE])
        both = sb("both", [L, 2, GT4, NE])
        work = sb("work", [L, GT4, NE])
        best = sb("best", [L, 4, GT4])
        run = sb("run", [L, GT4 + 1, NE])
        place = sb("place", [L, GT4, NE])
        small = sb("small", [L, 4, GT4])
        sidx = sb("sidx", [L, 2, 2, GT4], I32)
        bank = [sp.ps(ctx, f"ff_bank{i}", [128, 512]) for i in range(8)]
        s_const, s_w, s_mem = sem("const"), sem("w"), sem("mem")
        s_in = [sem("in0"), sem("in1")]
        s_store = [sem("store0"), sem("store1")]
        s_scat = [sem("scat0"), sem("scat1")]
        s_scale, s_norm, s_h2a = sem("scale_link"), sem("norm_link"), sem("h2_first")
        s_st, s_choose, s_both, s_place = sem("st_link"), sem("choose_link"), sem("both_link"), sem("place_link")
        names = ("ss", "r", "xr", "xt_mm", "xt", "up", "gelu", "down", "hx", "h2", "stats", "q", "x3", "x3t_mm", "x3t",
                 "z", "lmm", "lg", "both", "count", "sidx", "kept")
        e = {n: sem(n) for n in names}

        with nc.Block() as block:
            @block.sync
            def _(eng):
                start_counts(eng, *s_store, *e.values())
                for dst, name in ((ident, "ident"), (n2, "norm2"), (b1, "ff_b1"), (before, "before"), (ones, "ones"),
                                  (valid, "valid"), (expert, "expert")):
                    eng.dma_start(dst[:, :], c[name]).then_inc(s_const, 16)
                eng.dma_start(w1[:, :, :], c["ff_w1"].rearrange("(k p) n -> p k n", p=K2)).then_inc(s_const, 16)
                eng.dma_start(w2[:, :, :], c["ff_w2"].rearrange("(k p) n -> p k n", p=128)).then_inc(s_const, 16)
                eng.dma_start(gate[:, :, :], c["gate"].rearrange("(k p) n -> p k n", p=K2)).then_inc(s_const, 16)
                eng.dma_start(b2[:, :], c["ff_b2"].rearrange("(o d) -> o d", o=1).to_broadcast([L, D])).then_inc(s_const, 16)

                def load(g, p, i):
                    eng.wait_ge(e["xr"], done(g - 2))
                    eng.wait_ge(e["hx"], done(g - 2))
                    eng.dma_start(x2[:, p, :, :], row_tiles(x2_rows, g)).then_inc(s_in[p], 16)
                    eng.dma_start(h[:, p, :, :], row_tiles(h_rows, g)).then_inc(s_in[p], 16)

                def store(g, p, i):
                    eng.wait_ge(e["h2"], done(g))
                    eng.dma_start(row_tiles(h2_rows, g), h2[:, p, :, :]).then_inc(s_store[p], 16)

                turns(eng, NG, [(0, load), (2, store)])
                for p in range(2):
                    eng.wait_ge(s_store[p], AHEAD + 16 * (NG // 2))

            @block.gpsimd
            def _(eng):
                eng.memset(half[:, :], -0.5).then_inc(s_mem, 1)
                eng.memset(run[:, GT4, :], 0.0).then_inc(s_mem, 1)
                eng.wait_ge(s_mem, 2)
                eng.wait_ge(s_const, 16 * 11)

                def scale(g, p, i):
                    link = chain(eng, s_scale, 2 * g, settled=sp.settled)
                    eng.wait_ge(e["ss"], done(g))
                    eng.wait_ge(e["xr"], done(g - 2))
                    settle(eng, sp.settled)
                    link(eng.tensor_scalar(ss[:, p, :], ss[:, p, :], 1.0 / D, RMS_EPS, ALU.mult, ALU.add))
                    eng.tensor_tensor(r[:, p, :], ss[:, p, :], half[:, :], ALU.pow).then_inc(e["r"], 1)
                    eng.wait_ge(e["h2"], done(g - 2))
                    eng.wait_ge(s_in[p], 32 * i + 32)
                    settle(eng, sp.settled)
                    link(eng.tensor_tensor(hx[:, p, :, :], x2[:, p, :, :], h[:, p, :, :], ALU.add))
                    eng.tensor_tensor(hx[:, p, :, :], hx[:, p, :, :], b2[:, :].unsqueeze(1).to_broadcast([L, GT4, D]), ALU.add).then_inc(e["hx"], 1)

                def norm(g, p, i):
                    link = chain(eng, s_norm, 6 * g, settled=sp.settled)
                    var, rs, qq = mv[:, p, :, 1], rstd[:, p, :], q[:, p, :]
                    eng.wait_ge(e["stats"], done(g))
                    eng.wait_ge(e["z"], done(g - 2))
                    eng.wait_ge(e["kept"], done(g - 2))
                    settle(eng, sp.settled)
                    link(eng.tensor_scalar(qq, var, LN_EPS, None, ALU.add))
                    link(eng.tensor_tensor(rs, qq, half[:, :], ALU.pow))
                    link(eng.tensor_tensor(qq, rs, rs, ALU.mult))
                    link(eng.tensor_tensor(qq, qq, var, ALU.mult))
                    link(eng.tensor_scalar(qq, qq, 4.0, RMS_EPS, ALU.mult, ALU.add))
                    link(eng.tensor_tensor(qq, qq, half[:, :], ALU.pow))
                    eng.tensor_scalar(qq, qq, 2.0, None, ALU.mult).then_inc(e["q"], 1)

                def scatter(g, p, i):
                    eng.wait_ge(e["sidx"], done(g))
                    eng.wait_ge(e["z"], done(g))
                    settle(eng, sp.settled)
                    for k in range(2):
                        for j in range(GT4):
                            eng.indirect_dma_start(
                                out=slots[:, :], out_offset=IndirectOffsetOnAxis(ap=sidx[:, p, k, j:j + 1], axis=0),
                                in_=z[:, p, j, :], in_offset=None, bounds_check=NE * ES - 1, oob_is_err=False).then_inc(s_scat[p], 16)

                turns(eng, NG, [(0, scale), (1, norm), (2, scatter)])
                for p in range(2):
                    eng.wait_ge(s_scat[p], 128 * (NG // 2))

            @block.scalar
            def _(eng):
                def squares(g, p, i):
                    eng.wait_ge(s_in[p], 32 * i + 32)
                    eng.wait_ge(e["r"], done(g - 2))
                    eng.wait_ge(e["xt_mm"], done(g - 2))
                    for j in range(GT4):
                        ins = eng.activation(xr[:, p, j, :], x2[:, p, j, :], ACT.Square, accum_out=ss[:, p, j:j + 1])
                    ins.then_inc(e["ss"], 1)

                def scaled(g, p, i):
                    eng.wait_ge(e["r"], done(g))
                    for j in range(GT4):
                        ins = eng.activation(xr[:, p, j, :], x2[:, p, j, :], ACT.Copy, scale=r[:, p, j:j + 1])
                    ins.then_inc(e["xr"], 1)

                def kept(g, p, i):
                    eng.wait_ge(e["xt_mm"], done(g))
                    eng.wait_ge(e["up"], AHEAD + NF * (g - 1))
                    for k in range(2):
                        ins = eng.activation(xt[:, p, k, :], bank[k][0:K2, 0:GW], ACT.Copy)
                    ins.then_inc(e["xt"], 1)

                def gelu(g, p, i):
                    eng.wait_ge(e["down"], done(2 * (g - 2) + 1))
                    for f in range(NF):
                        eng.wait_ge(e["up"], done(NF * g + f))
                        eng.activation(gt[:, p, f, :], bank[2 + f % 2][:, 0:GW], ACT.Gelu_apprx_tanh, bias=b1[:, f:f + 1]).then_inc(e["gelu"], 1)

                def zrow(g, p, i):
                    eng.wait_ge(e["q"], done(g))
                    eng.wait_ge(e["x3"], done(g))
                    eng.wait_ge(s_scat[p], 128 * i)
                    for j in range(GT4):
                        ins = eng.activation(z[:, p, j, :], x3[:, p, j, :], ACT.Copy, scale=q[:, p, j:j + 1])
                    ins.then_inc(e["z"], 1)

                eng.wait_ge(s_const, 16 * 11)
                turns(eng, NG, [(0, squares), (0, scaled), (0, kept), (0, gelu), (1, zrow)], peeled=2)

            @block.vector
            def _(eng):
                eng.wait_ge(s_const, 16 * 11)
                for k in range(2):
                    eng.tensor_scalar(w1[:, k, :], w1[:, k, :], n2[:, k:k + 1], None, ALU.mult).then_inc(s_w, 1)
                eng.tensor_scalar(rank[:, :], expert[:, :], -1.0, float(NE), ALU.mult, ALU.add).then_inc(s_w, 1)
                eng.tensor_scalar(base[:, :], expert[:, :], float(ES), None, ALU.mult).then_inc(s_w, 1)
                eng.wait_ge(s_w, 4)
                eng.wait_ge(s_mem, 2)

                def total(g, p, i):
                    eng.wait_ge(e["hx"], done(g))
                    eng.wait_ge(s_store[p], AHEAD + 16 * i)
                    for j in range(2):
                        eng.wait_ge(e["down"], done(2 * g + j))
                        ins = eng.tensor_tensor(h2[:, p, 2 * j:2 * j + 2, :], bank[4 + j][0:L, 0:2 * D].rearrange("t (j d) -> t j d", j=2),
                                                hx[:, p, 2 * j:2 * j + 2, :], ALU.add)
                        if j:
                            ins.then_inc(e["h2"], 1)
                        else:
                            ins.then_inc(s_h2a, 1)
                    eng.wait_ge(s_h2a, g + 1)
                    eng.wait_ge(e["h2"], done(g))
                    eng.wait_ge(e["q"], done(g - 2))
                    link = chain(eng, s_st, GT4 * g, settled=sp.settled)
                    for j in range(GT4):
                        link(eng.bn_stats(st[:, p, j, :], h2[:, p, j, :]))
                    for j in range(GT4):
                        ins = eng.bn_aggr(mv[:, p, j, :], st[:, p, j, :])
                    ins.then_inc(e["stats"], 1)

                def centred(g, p, i):
                    eng.wait_ge(e["q"], done(g))
                    eng.wait_ge(e["x3t_mm"], done(g - 2))
                    eng.wait_ge(e["z"], done(g - 2))
                    for j in range(GT4):
                        ins = eng.tensor_scalar(x3[:, p, j, :], h2[:, p, j, :], mv[:, p, j, 0:1], rstd[:, p, j:j + 1],
                                                ALU.subtract, ALU.mult)
                    ins.then_inc(e["x3"], 1)
                    at = bass.ds(g * GT4, GT4)
                    eng.tensor_copy(rt.mean[:, at], mv[:, p, :, 0])
                    eng.tensor_copy(rt.rstd[:, at], rstd[:, p, :]).then_inc(e["kept"], 1)
                    eng.wait_ge(e["x3t_mm"], done(g))
                    eng.wait_ge(e["lmm"], done(g - 2))
                    for k in range(2):
                        ins = eng.tensor_copy(x3t[:, p, k, :], bank[k][0:K2, 0:GW])
                    ins.then_inc(e["x3t"], 1)

                def choose(g, p, i):
                    link = chain(eng, s_choose, 13 * g)
                    eng.wait_ge(e["lmm"], done(g))
                    eng.wait_ge(e["count"], done(g - 2))
                    link(eng.tensor_copy(lg[:, p, :, :], bank[6][0:L, 0:GT4 * NE].rearrange("t (j e) -> t j e", j=GT4)))
                    ll = lg[:, p, :, :]
                    rk = rank[:, :].unsqueeze(1).to_broadcast([L, GT4, NE])

                    def wide(v):
                        return v.unsqueeze(2).to_broadcast([L, GT4, NE])

                    for k in range(2):
                        mk = mask[:, p, k, :, :]
                        link(eng.tensor_reduce(best[:, k, :], ll, AX.X, ALU.max))
                        link(eng.tensor_tensor(work[:, :, :], ll, wide(best[:, k, :]), ALU.is_equal))
                        link(eng.tensor_tensor(work[:, :, :], work[:, :, :], rk, ALU.mult))
                        link(eng.tensor_reduce(best[:, 2 + k, :], work[:, :, :], AX.X, ALU.max))
                        link(eng.tensor_tensor(mk, work[:, :, :], wide(best[:, 2 + k, :]), ALU.is_equal))
                        if k == 0:
                            link(eng.scalar_tensor_tensor(ll, mk, -1e30, ll, ALU.mult, ALU.add))
                    at = bass.ds(g * GT4, GT4)
                    link(eng.tensor_tensor(rt.gap[:, at], best[:, 1, :], best[:, 0, :], ALU.subtract))
                    eng.tensor_tensor(both[:, p, :, :], mask[:, p, 0, :, :], mask[:, p, 1, :, :], ALU.add).then_inc(s_both, 1)
                    eng.wait_ge(s_both, g + 1)
                    eng.tensor_tensor(both[:, p, :, :], both[:, p, :, :], wide(valid[:, at]), ALU.mult).then_inc(e["both"], 1)

                def places(g, p, i):
                    link = chain(eng, s_place, (1 + GT4 + 1 + 2 * 8) * g)
                    eng.wait_ge(e["count"], done(g))
                    eng.wait_ge(s_scat[p], 128 * i)
                    at = bass.ds(g * GT4, GT4)
                    link(eng.tensor_copy(run[:, 0, :], run[:, GT4, :]))
                    for j in range(GT4):
                        link(eng.tensor_tensor(run[:, j + 1, :], run[:, j, :], bank[7][0:L, 32 + NE * j:32 + NE * j + NE], ALU.add))
                    link(eng.tensor_tensor(place[:, :, :], run[:, 0:GT4, :],
                                           bank[7][0:L, 0:GT4 * NE].rearrange("t (j e) -> t j e", j=GT4), ALU.add))
                    bs = base[:, :].unsqueeze(1).to_broadcast([L, GT4, NE])
                    for k in range(2):
                        mk = mask[:, p, k, :, :]
                        pk, ek, kp, sl = (small[:, n, :] for n in range(4))
                        link(eng.tensor_tensor(work[:, :, :], mk, place[:, :, :], ALU.mult))
                        link(eng.tensor_reduce(pk, work[:, :, :], AX.X, ALU.add))
                        link(eng.tensor_tensor(work[:, :, :], mk, bs, ALU.mult))
                        link(eng.tensor_reduce(ek, work[:, :, :], AX.X, ALU.add))
                        link(eng.scalar_tensor_tensor(rt.keep[:, k, at], pk, float(CAP), valid[:, at], ALU.is_lt, ALU.mult))
                        link(eng.tensor_tensor(sl, pk, ek, ALU.add))
                        link(eng.tensor_tensor(rt.slot[:, k, at], sl, rt.keep[:, k, at], ALU.mult))
                        link(eng.scalar_tensor_tensor(kp, sl, -65536.0, rt.keep[:, k, at], ALU.add, ALU.mult))
                        ins = eng.tensor_scalar(sidx[:, p, k, :], kp, 65536.0, None, ALU.add)
                    ins.then_inc(e["sidx"], 1)

                turns(eng, NG, [(0, total), (0, centred), (0, choose), (0, places)], peeled=2)

            @block.tensor
            def _(eng):
                eng.wait_ge(s_const, 16 * 11)
                eng.wait_ge(s_w, 4)

                def transposed(src, dst):
                    for k in range(2):
                        for j in range(GT4):
                            ins = eng.transpose(dst[k][0:K2, L * j:L * j + L], src[:, j, K2 * k:K2 * k + K2], ident[0:L, 0:L])
                    return ins

                def up(g, p, i):
                    eng.wait_ge(e["xr"], done(g))
                    eng.wait_ge(e["x3t"], done(g - 1))
                    transposed(xr[:, p, :, :], bank).then_inc(e["xt_mm"], 1)
                    eng.wait_ge(e["xt"], done(g))
                    for f in range(NF):
                        eng.wait_ge(e["gelu"], done(NF * g + f - 2))
                        for k in range(2):
                            ins = eng.matmul(bank[2 + f % 2][:, 0:GW], w1[:, k, 128 * f:128 * f + 128], xt[:, p, k, :],
                                             start=(k == 0), stop=(k == 1))
                        ins.then_inc(e["up"], 1)

                def down(g, p, i):
                    eng.wait_ge(e["gelu"], done(NF * g + NF - 1))
                    eng.wait_ge(e["h2"], done(g - 1))
                    for j in range(GT4):
                        o = bank[4 + j // 2][0:L, D * (j % 2):D * (j % 2) + D]
                        for f in range(NF):
                            ins = eng.matmul(o, gt[:, p, f, L * j:L * j + L], w2[:, f, :], start=(f == 0), stop=(f == NF - 1))
                        if j % 2:
                            ins.then_inc(e["down"], 1)

                def logits(g, p, i):
                    eng.wait_ge(e["x3"], done(g))
                    transposed(x3[:, p, :, :], bank).then_inc(e["x3t_mm"], 1)
                    eng.wait_ge(e["x3t"], done(g))
                    eng.wait_ge(e["both"], done(g - 1))
                    for j in range(GT4):
                        for k in range(2):
                            ins = eng.matmul(bank[6][0:L, NE * j:NE * j + NE], x3t[:, p, k, L * j:L * j + L], gate[:, k, :],
                                             start=(k == 0), stop=(k == 1))
                    ins.then_inc(e["lmm"], 1)

                def counts(g, p, i):
                    eng.wait_ge(e["both"], done(g))
                    eng.wait_ge(e["sidx"], done(g - 1))
                    rhs = both[:, p, :, :].rearrange("t j e -> t (j e)")
                    eng.matmul(bank[7][0:L, 0:GT4 * NE], before[:, :], rhs, start=True, stop=True)
                    eng.matmul(bank[7][0:L, 32:32 + GT4 * NE], ones[:, :], rhs, start=True, stop=True).then_inc(e["count"], 1)

                turns(eng, NG, [(0, up), (0, down), (0, logits), (0, counts)])


def expert_turns(eng, stages, between=None):
    per = ES // SG
    half = per // 2

    def expert(x, px, first=False):
        for q in range(2):
            for lag, f in stages:
                if q >= lag:
                    f(x * per + (q - lag), (q - lag) % 2, x * half, x, px)
                elif not first:
                    f(x * per + (q - lag), (q - lag) % 2, x * half - 1, x - 1, 1 - px)
        with eng.Fori(1, half) as i:
            for q in range(2):
                for lag, f in stages:
                    f(x * per + (2 * i + (q - lag)), (q - lag) % 2, x * half + (i + (q - lag) // 2), x, px)

    between = between or (lambda x, px, turn: None)
    expert(0, 0, first=True)
    between(1, 1, 0)
    with eng.Fori(0, (NE - 2) // 2) as y:
        expert(2 * y + 1, 1)
        between(2 * y + 2, 0, y + 1)
        expert(2 * y + 2, 0)
        between(2 * y + 3, 1, y + 1)
    expert(NE - 1, 1)
    for q in range(2):
        for lag, f in stages:
            if lag > q:
                f(NE * per + q - lag, (q - lag) % 2, NE * half - 1, NE - 1, 1)


def experts(nc, sp, c, slots, answers):
    NJ = SG // 128
    NH = HID // 128
    per = ES // SG
    with sp.phase() as ctx:
        def sb(name, shape, dt=F32):
            return sp.sb(ctx, "ex_" + name, shape, dt)

        def sem(name):
            return sp.sem("ex_" + name)

        ident = sb("ident", [128, 128])
        norm = sb("norm", [K2, NE, 2])
        w13 = sb("w13", [K2, 2, 2, 2 * HID])
        w2 = sb("w2", [128, 2, NH, D])
        z = sb("z", [128, 2, NJ, D])
        zt = sb("zt", [K2, 2, 2, SG])
        sil = sb("sil", [128, 2, SG])
        ht = sb("ht", [128, 2, NH, SG])
        ans = sb("ans", [128, 2, NJ, D])
        bank = [sp.ps(ctx, f"ex_bank{i}", [128, 512]) for i in range(8)]
        s_const = sem("const")
        s_in = [sem("in0"), sem("in1")]
        s_win = [sem("w_in0"), sem("w_in1")]
        s_store = [sem("store0"), sem("store1")]
        s_half = sem("ans_first")
        names = ("w", "z_mm", "zt0", "zt1", "gu", "silu", "h", "down", "ans")
        e = {n: sem(n) for n in names}

        def group(buf, u):
            return buf[bass.ds(u * SG, SG), :].rearrange("(p j) d -> p j d", j=NJ)

        with nc.Block() as block:
            @block.sync
            def _(eng):
                start_counts(eng, *s_store, *e.values())
                eng.dma_start(ident[:, :], c["ident"]).then_inc(s_const, 16)
                eng.dma_start(norm[:, :, :], c["norm_e"]).then_inc(s_const, 16)

                def load(u, p, i):
                    eng.wait_ge(e["z_mm"], done(u - 2))
                    eng.dma_start(z[:, p, :, :], group(slots, u)).then_inc(s_in[p], 16)

                def store(u, p, i):
                    eng.wait_ge(e["ans"], done(2 * u + 1))
                    eng.dma_start(group(answers, u), ans[:, p, :, :]).then_inc(s_store[p], 16)

                turns(eng, NE * per, [(0, load), (3, store)])
                for p in range(2):
                    eng.wait_ge(s_store[p], AHEAD + 16 * NE * per // 2)

            @block.gpsimd
            def _(eng):
                def weights(x, px):
                    eng.dma_start(w13[:, px, :, :], c["w13"][bass.ds(x, 1)].rearrange("o (k p) n -> p (o k) n", p=K2)).then_inc(s_win[px], 16)
                    eng.dma_start(w2[:, px, :, :], c["w2"][bass.ds(x, 1)].rearrange("o (k p) n -> p (o k) n", p=128)).then_inc(s_win[px], 16)

                weights(0, 0)
                weights(1, 1)
                with eng.Fori(0, (NE - 2) // 2) as y:
                    for px in range(2):
                        eng.wait_ge(e["down"], done(2 * per * (2 * y + px + 1) - 1))
                        settle(eng, sp.settled)
                        weights(2 * y + px + 2, px)

            @block.scalar
            def _(eng):
                def kept(u, p, i, x, px):
                    eng.wait_ge(e["z_mm"], done(u))
                    eng.wait_ge(e["gu"], AHEAD + NH * (u - 1))
                    eng.activation(zt[:, p, 0, :], bank[0][0:K2, :], ACT.Copy).then_inc(e["zt0"], 1)

                def silu(u, p, i, x, px):
                    for f in range(NH):
                        eng.wait_ge(e["gu"], done(NH * u + f))
                        eng.wait_ge(e["h"], done(NH * u + f - 2))
                        eng.activation(sil[:, f % 2, :], bank[2 + 2 * (f % 2)][:, :], ACT.Silu).then_inc(e["silu"], 1)

                expert_turns(eng, [(0, kept), (1, silu)])

            @block.vector
            def _(eng):
                def scaled(x, px, turn):
                    eng.wait_ge(s_win[px], 32 * turn + 32)
                    for k in range(2):
                        ins = eng.tensor_scalar(w13[:, px, k, :], w13[:, px, k, :],
                                                norm[:, bass.ds(x, 1), k:k + 1].rearrange("p o s -> p (o s)"), None, ALU.mult)
                    ins.then_inc(e["w"], 1)

                def kept(u, p, i, x, px):
                    eng.wait_ge(e["z_mm"], done(u))
                    eng.wait_ge(e["gu"], AHEAD + NH * (u - 1))
                    eng.tensor_copy(zt[:, p, 1, :], bank[1][0:K2, :]).then_inc(e["zt1"], 1)

                def product(u, p, i, x, px):
                    eng.wait_ge(e["down"], AHEAD + 2 * (u - 1))
                    for f in range(NH):
                        eng.wait_ge(e["silu"], done(NH * u + f))
                        eng.tensor_tensor(ht[:, p, f, :], sil[:, f % 2, :], bank[3 + 2 * (f % 2)][:, :], ALU.mult).then_inc(e["h"], 1)

                def answer(u, p, i, x, px):
                    eng.wait_ge(s_store[p], AHEAD + 16 * i)
                    for j in range(2):
                        eng.wait_ge(e["down"], done(2 * u + j))
                        eng.tensor_copy(ans[:, p, 2 * j:2 * j + 2, :],
                                        bank[6 + j][:, 0:2 * D].rearrange("t (j d) -> t j d", j=2)).then_inc(e["ans"], 1)

                eng.wait_ge(s_const, 32)
                scaled(0, 0, 0)
                expert_turns(eng, [(0, kept), (1, product), (2, answer)], scaled)

            @block.tensor
            def _(eng):
                def turned(u, p, i, x, px):
                    eng.wait_ge(s_in[p], 16 * i + 16)
                    eng.wait_ge(e["zt0"], done(u - 1))
                    eng.wait_ge(e["zt1"], done(u - 1))
                    for k in range(2):
                        for j in range(NJ):
                            ins = eng.transpose(bank[k][0:K2, 128 * j:128 * j + 128], z[:, p, j, K2 * k:K2 * k + K2], ident[:, :])
                    ins.then_inc(e["z_mm"], 1)

                def up(u, p, i, x, px):
                    eng.wait_ge(e["zt0"], done(u))
                    eng.wait_ge(e["zt1"], done(u))
                    eng.wait_ge(e["w"], done(x))
                    for f in range(NH):
                        eng.wait_ge(e["h"], done(NH * u + f - 2))
                        for v in range(2):
                            for k in range(2):
                                ins = eng.matmul(bank[2 + 2 * (f % 2) + v][:, :], w13[:, px, k, HID * v + 128 * f:HID * v + 128 * f + 128],
                                                 zt[:, p, k, :], start=(k == 0), stop=(k == 1))
                        ins.then_inc(e["gu"], 1)

                def down(u, p, i, x, px):
                    eng.wait_ge(e["h"], done(NH * u + NH - 1))
                    for j in range(NJ):
                        if j % 2 == 0:
                            eng.wait_ge(e["ans"], done(2 * (u - 1) + j // 2))
                        o = bank[6 + j // 2][:, D * (j % 2):D * (j % 2) + D]
                        for f in range(NH):
                            ins = eng.matmul(o, ht[:, p, f, 128 * j:128 * j + 128], w2[:, px, f, :], start=(f == 0), stop=(f == NH - 1))
                        if j % 2:
                            ins.then_inc(e["down"], 1)

                eng.wait_ge(s_const, 32)
                expert_turns(eng, [(0, turned), (1, up), (2, down)])


def combine(nc, sp, h2_rows, answers, out, rt):
    with sp.phase() as ctx:
        def sb(name, shape, dt=F32):
            return sp.sb(ctx, "cb_" + name, shape, dt)

        def sem(name):
            return sp.sem("cb_" + name)

        h2 = sb("h2", [L, 2, GT4, D])
        f = sb("f", [L, 2, 2, GT4, D])
        o = sb("o", [L, 2, GT4, D])
        idx = sb("idx", [L, 2, 2, GT4], I32)
        e2 = sb("e2", [L, NT])
        w = sb("w", [L, 2, NT])
        alpha = sb("alpha", [L, NT])
        beta = sb("beta", [L, NT])
        s_in = [sem("in0"), sem("in1")]
        s_f = [sem("f0"), sem("f1")]
        s_store = [sem("store0"), sem("store1")]
        s_exp, s_prep, s_acc = sem("exp"), sem("prep"), sem("acc")
        e = {n: sem(n) for n in ("idx", "o")}

        with nc.Block() as block:
            @block.sync
            def _(eng):
                start_counts(eng, *s_store, *e.values())

                def load(g, p, i):
                    eng.wait_ge(e["o"], done(g - 2))
                    eng.dma_start(h2[:, p, :, :], row_tiles(h2_rows, g)).then_inc(s_in[p], 16)

                def store(g, p, i):
                    eng.wait_ge(e["o"], done(g))
                    eng.dma_start(row_tiles(out, g), o[:, p, :, :]).then_inc(s_store[p], 16)

                turns(eng, NG, [(0, load), (2, store)])
                for p in range(2):
                    eng.wait_ge(s_store[p], AHEAD + 16 * (NG // 2))

            @block.gpsimd
            def _(eng):
                def gather(g, p, i):
                    eng.wait_ge(e["idx"], done(g))
                    eng.wait_ge(e["o"], done(g - 2))
                    settle(eng, sp.settled)
                    for k in range(2):
                        for j in range(GT4):
                            eng.indirect_dma_start(out=f[:, p, k, j, :], out_offset=None, in_=answers[:, :],
                                                   in_offset=IndirectOffsetOnAxis(ap=idx[:, p, k, j:j + 1], axis=0)).then_inc(s_f[p], 16)

                turns(eng, NG, [(0, gather)])

            @block.scalar
            def _(eng):
                eng.activation(e2[:, :], rt.gap[:, :], ACT.Exp).then_inc(s_exp, 1)

            @block.vector
            def _(eng):
                def index(g, p, i):
                    eng.wait_ge(s_f[p], 128 * i)
                    eng.tensor_copy(idx[:, p, :, :], rt.slot[:, :, bass.ds(g * GT4, GT4)]).then_inc(e["idx"], 1)

                def summed(g, p, i):
                    eng.wait_ge(s_in[p], 16 * i + 16)
                    eng.wait_ge(s_store[p], AHEAD + 16 * i)
                    for j in range(GT4):
                        at = bass.ds(g * GT4 + j, 1)
                        ins = eng.tensor_scalar(o[:, p, j, :], h2[:, p, j, :], alpha[:, at], beta[:, at], ALU.mult, ALU.add)
                    ins.then_inc(s_acc, 1)
                    eng.wait_ge(s_acc, 2 * g + 1)
                    eng.wait_ge(s_f[p], 128 * i + 128)
                    for k in range(2):
                        if k:
                            eng.wait_ge(s_acc, 2 * g + 2)
                        for j in range(GT4):
                            ins = eng.scalar_tensor_tensor(o[:, p, j, :], f[:, p, k, j, :], w[:, k, bass.ds(g * GT4 + j, 1)],
                                                           o[:, p, j, :], ALU.mult, ALU.add)
                        ins.then_inc(e["o"] if k else s_acc, 1)

                link = chain(eng, s_prep, 0)
                eng.wait_ge(s_exp, 1)
                link(eng.tensor_scalar(alpha[:, :], e2[:, :], 1.0, None, ALU.add))
                link(eng.reciprocal(w[:, 0, :], alpha[:, :]))
                link(eng.tensor_tensor(w[:, 1, :], e2[:, :], w[:, 0, :], ALU.mult))
                link(eng.tensor_tensor(w[:, :, :], w[:, :, :], rt.keep[:, :, :], ALU.mult))
                link(eng.tensor_tensor(alpha[:, :], w[:, 0, :], w[:, 1, :], ALU.add))
                link(eng.tensor_tensor(alpha[:, :], alpha[:, :], rt.rstd[:, :], ALU.mult))
                link(eng.scalar_tensor_tensor(beta[:, :], rt.mean[:, :], -1.0, alpha[:, :], ALU.mult, ALU.mult))
                link(eng.tensor_scalar(alpha[:, :], alpha[:, :], 1.0, None, ALU.add))
                turns(eng, NG, [(0, index), (1, summed)], peeled=2)


def program(nc, a, out, upto=9, keep="Internal"):
    with ExitStack() as outer:
        sp = Space(nc, outer)

        def rows(name, n, w=D):
            return nc.dram_tensor(name, (n, w), F32, kind=keep).ap()

        h_rows, x_rows = rows("h_rows", N), rows("x_rows", N)
        x2_rows, h2_rows = rows("x2_rows", N), rows("h2_rows", N)
        xt = nc.dram_tensor("x_t", (K2, 2, N), F32, kind=keep).ap()
        params = rows("params", 2 * H, N)
        slots, answers = rows("slots", NE * ES), rows("answers", NE * ES)
        tokenizer(nc, sp, a["blocks"], a["tok_w"], a["tok_b"], a["cls"], a["pos"], a["txt"], h_rows, slots)
        if upto < 2:
            return
        normalise(nc, sp, a, h_rows, a["w_in"], a["norm1"], x_rows, xt, params)
        if upto < 3:
            return
        mixer(nc, sp, a, x_rows, xt, params, x2_rows)
        if upto < 4:
            return
        with ExitStack() as ctx:
            route = Route(sp, ctx)
            feed_forward(nc, sp, a, x2_rows, h_rows, h2_rows, slots, route)
            if upto < 5:
                return
            experts(nc, sp, a, slots, answers)
            if upto < 6:
                return
            combine(nc, sp, h2_rows, answers, out, route)


def constants():
    import numpy as np
    ident = np.eye(128, dtype=np.float32)
    rows = np.arange(EP)
    head_of = rows // (2 * NS)
    block_mask = (head_of[:, None] == (np.arange(DI) // P)[None, :]).astype(np.float32)
    step_mask = ((head_of[:, None] == head_of[None, :]) & (rows[:, None] % NS == rows[None, :] % NS)).astype(np.float32)
    head_mask = np.repeat((np.arange(H * NS)[:, None] // NS == np.arange(H)[None, :]).astype(np.float32), L, axis=1)
    seq = np.arange(SEQ)
    comp = rows // NS % 2
    spread = np.stack([((seq // B)[:, None] == head_of[None, :]) & (comp == j)[None, :] for j in range(2)], 1).astype(np.float32)
    image_mask = (seq[:, None] % B == np.arange(B)[None, :]).astype(np.float32)
    before = (np.arange(L)[:, None] < np.arange(L)[None, :]).astype(np.float32)
    ones = np.ones((L, L), np.float32)
    valid = np.ones((L, CH), np.float32)
    valid[T - (CH - 1) * L:, CH - 1] = 0
    valid = np.tile(valid, (1, B))
    expert = np.tile(np.arange(NE, dtype=np.float32), (L, 1))
    return {"ident": ident, "block_mask": block_mask, "step_mask": step_mask, "head_mask": head_mask,
            "spread": spread, "image_mask": image_mask, "before": before, "ones": ones,
            "valid": valid, "expert": expert}


def lay_out(inputs):
    import numpy as np
    a = {k: np.asarray(v) for k, v in inputs.items()}
    w_in, w_bc = a["L0_attn_w_in"], a["L0_attn_w_bc"]
    out = {
        "blocks": a["x"].reshape(B, 3, BLK, 8, BLK, 8).transpose(1, 3, 5, 0, 2, 4).reshape(D, B, BLK * BLK),
        "txt": a["txt"],
        "tok_w": a["L0_tok_w"].reshape(D, 3, 2, 8, 2, 8).transpose(1, 3, 5, 2, 4, 0).reshape(D, 2, 2, D),
        "tok_b": a["L0_tok_b"],
        "cls": a["L0_tok_cls_token"].reshape(1, D),
        "pos": a["L0_tok_pos_embedding"].reshape(1 + NPATCH, D),
        "norm1": a["L0_attn_norm1_w"].reshape(2, K2).T,
        "w_in": np.concatenate([w_in[:, :2 * DI], w_in[:, 2 * DI::2], w_in[:, 2 * DI + 1::2]], axis=1),
        "conv_w": a["L0_attn_conv_w"].reshape(3, 128, 4).transpose(1, 0, 2),
        "w_bc": w_bc.reshape(DI, H, 2, NS).transpose(0, 2, 1, 3).reshape(DI, EP),
        "d_skip": a["L0_attn_D_skip"],
        "w_out": a["L0_attn_w_out"],
        "norm2": a["L0_attn_norm2_w"].reshape(2, K2).T,
        "ff_w1": a["L0_attn_ff_w1"], "ff_b1": a["L0_attn_ff_b1"].reshape(FF // 128, 128).T,
        "ff_w2": a["L0_attn_ff_w2"], "ff_b2": a["L0_attn_ff_b2"],
        "gate": a["L0_ffn_gate_w"].transpose(1, 0),
        "w13": a["L0_ffn_w13"].transpose(0, 2, 1),
        "w2": a["L0_ffn_w2"].transpose(0, 2, 1),
        "norm_e": a["L0_ffn_norm_w"].reshape(NE, 2, K2).transpose(2, 0, 1),
    }
    out.update(constants())
    return {k: np.ascontiguousarray(v) for k, v in out.items()}


def kernel(**inputs):
    import concourse.bacc as bacc
    from concourse import mybir as mb
    from concourse.bass_utils import run_bass_kernel_spmd as run

    nc = bacc.Bacc("TRN2", target_bir_lowering=False, num_devices=1)
    arrays = lay_out(inputs)
    aps = {k: nc.dram_tensor(f"in_{k}", v.shape, mb.dt.from_np(v.dtype), kind="ExternalInput").ap()
           for k, v in arrays.items()}
    out = nc.dram_tensor("out_rows", (N, D), F32, kind="ExternalOutput").ap()
    program(nc, aps, out)
    r = run(nc, [{f"in_{k}": v for k, v in arrays.items()}], core_ids=[0])
    return r.results[0]["out_rows"].reshape(B, TP, D)[:, :T]
```

```python
from contextlib import ExitStack

import concourse.bass as bass
from concourse import mybir
from concourse.bass import IndirectOffsetOnAxis

F32 = mybir.dt.float32
I32 = mybir.dt.int32
ALU = mybir.AluOpType
ACT = mybir.ActivationFunctionType
AX = mybir.AxisListType

B = 16
D = 192
K2 = D // 2
GRID = 27
BLK = 28
NPATCH = GRID * GRID
NTXT = 77
T = 1 + NPATCH + NTXT
L = 120
CH = 7
TP = CH * L
NT = B * CH
N = B * TP
GT4 = 4
NG = NT // GT4
GW = GT4 * L
H = 6
P = 64
DI = H * P
NS = 8
SEQ = H * B
EP = H * 2 * NS
ROWS = 4
STEPS = 15
PAD = L - 1
KW = L + 2
FF = 768
NE = 8
HID = 512
CAP = -(-(2 * B * T * 5) // (4 * NE))
ES = 4096
SG = 512
LN_EPS = 1e-5
RMS_EPS = 1e-6
L2_EPS = 1e-12


AHEAD = 40


def done(n):
    return n + 1 + AHEAD


def start_counts(eng, *sems):
    for s in sems:
        eng.sem_inc(s, AHEAD)


def settle(eng, settled):
    eng.sem_inc(settled, 1)


def chain(eng, sem, before, settled=None):
    steps = [0]

    def link(ins):
        steps[0] += 1
        ins.then_inc(sem, 1)
        eng.wait_ge(sem, before + steps[0])
        if settled:
            settle(eng, settled)

    return link


class Space:

    def __init__(self, nc, outer):
        self.nc, self.outer = nc, outer
        self.settled = self.sem("settled")

    def phase(self):
        return ExitStack()

    def sb(self, ctx, name, shape, dt=F32):
        return ctx.enter_context(self.nc.sbuf_tensor(name, shape, dt))

    def ps(self, ctx, name, shape, dt=F32):
        return ctx.enter_context(self.nc.psum_tensor(name, shape, dt))

    def sem(self, name):
        return self.outer.enter_context(self.nc.semaphore(name))


def row_tiles(buf, g):
    return buf[bass.ds(g * GW, GW), :].rearrange("(j p) d -> p j d", p=L)


def tokenizer(nc, sp, blocks, tok_w, tok_b, cls, pos, txt, h_rows, slots):
    with sp.phase() as ctx:
        tiles = -(-GRID // ROWS)
        rows_of = [min(ROWS, GRID - g * ROWS) for g in range(tiles)]
        wide = [r * BLK - 1 for r in rows_of]
        tiles_with = [sum(r < n for n in rows_of) for r in range(ROWS)]

        def patch_rows(rows, r):
            return rows.rearrange("(g c) d -> g c d", c=GRID)[r:GRID:ROWS].rearrange("g c d -> c g d")

        main = sp.sb(ctx, "tk_main", [128, 2, BLK * BLK])
        rest = sp.sb(ctx, "tk_rest", [128, 2, BLK * BLK])
        w_main = sp.sb(ctx, "tk_w_main", [128, 4, D])
        w_rest = sp.sb(ctx, "tk_w_rest", [128, 2, D])
        bias = sp.sb(ctx, "tk_bias", [128, D])
        posb = sp.sb(ctx, "tk_posb", [ROWS * BLK, tiles, D])
        out = sp.sb(ctx, "tk_out", [ROWS * BLK, 2, tiles, D])
        zeros = sp.sb(ctx, "tk_zeros", [128, 8192])
        clsrow = sp.sb(ctx, "tk_clsrow", [B, D])
        posrow = sp.sb(ctx, "tk_posrow", [B, D])
        acc = sp.ps(ctx, "tk_acc", [128, 2, 512])
        s_const, s_zero, s_zout = sp.sem("tk_const"), sp.sem("tk_zero"), sp.sem("tk_zeroed")
        s_in = [sp.sem("tk_in0"), sp.sem("tk_in1")]
        s_mm, s_ev, s_posb = sp.sem("tk_mm"), sp.sem("tk_ev"), sp.sem("tk_posb_ready")
        s_st = [sp.sem("tk_st0"), sp.sem("tk_st1")]
        s_cls, s_misc = sp.sem("tk_cls"), sp.sem("tk_misc")
        hb = h_rows.rearrange("(b t) d -> b t d", b=B)
        with nc.Block() as block:
            @block.sync
            def _(eng):
                start_counts(eng, *s_st, s_ev)
                eng.dma_start(w_main[:, :, :], tok_w[0:128].rearrange("f a b d -> f (a b) d")).then_inc(s_const, 16)
                for dc in range(2):
                    eng.dma_start(w_rest[64 * dc:64 * dc + 64, :, :], tok_w[128:192, :, dc, :]).then_inc(s_const, 16)

                def load(b, p):
                    img = blocks[:, bass.ds(b, 1), :].rearrange("f o n -> f (o n)")
                    eng.dma_start(main[:, p, :], img[0:128, :]).then_inc(s_in[p], 16)
                    eng.dma_start(rest[0:64, p, :], img[128:192, :]).then_inc(s_in[p], 16)
                    eng.dma_start(rest[64:128, p, 0:BLK * BLK - 1], img[128:192, 1:BLK * BLK]).then_inc(s_in[p], 16)

                for p in range(2):
                    load(p, p)
                with eng.Fori(0, B // 2 - 1) as i:
                    for p in range(2):
                        eng.wait_ge(s_mm, 14 * i + 7 * p + 7)
                        load(2 * i + p + 2, p)

            @block.scalar
            def _(eng):
                eng.wait_ge(s_zero, 2)
                for r in range(ROWS):
                    eng.dma_start(posb[r * BLK:r * BLK + GRID, 0:tiles_with[r], :],
                                  patch_rows(pos[1:1 + NPATCH, :], r)).then_inc(s_const, 16)
                eng.dma_start(bias[:, :], tok_b.rearrange("(o d) -> o d", o=1).to_broadcast([128, D])).then_inc(s_const, 16)
                eng.dma_start(clsrow[:, :], cls.to_broadcast([B, D])).then_inc(s_const, 16)
                eng.dma_start(posrow[:, :], pos[0:1, :].to_broadcast([B, D])).then_inc(s_const, 16)
                eng.dma_start(hb[:, 1 + NPATCH:T, :], txt).then_inc(s_misc, 16)
                eng.wait_ge(s_cls, 1)
                eng.dma_start(hb[:, 0, :], clsrow[:, :]).then_inc(s_misc, 16)
                eng.dma_start(hb[:, T:TP, :], zeros[0:B, 0:(TP - T) * D].rearrange("b (t d) -> b t d", d=D)).then_inc(s_misc, 16)
                view = slots.rearrange("(p r) d -> p (r d)", p=128)
                for i in range(6):
                    eng.dma_start(view[:, 8192 * i:8192 * (i + 1)], zeros[:, :]).then_inc(s_zout, 16)
                with eng.Fori(0, B // 2) as i:
                    for p in range(2):
                        b = 2 * i + p
                        eng.wait_ge(s_ev, AHEAD + 7 * b + 7)
                        img = hb[bass.ds(b, 1), 1:1 + NPATCH, :].rearrange("o t d -> (o t) d")
                        for r in range(ROWS):
                            eng.dma_start(patch_rows(img, r), out[r * BLK:r * BLK + GRID, p, 0:tiles_with[r], :]).then_inc(s_st[p], 16)
                for p in range(2):
                    eng.wait_ge(s_st[p], AHEAD + 16 * ROWS * (B // 2))
                eng.wait_ge(s_misc, 48)
                eng.wait_ge(s_zout, 96)

            @block.gpsimd
            def _(eng):
                eng.memset(posb[:, :, :], 0.0).then_inc(s_zero, 1)
                eng.memset(zeros[:, :], 0.0).then_inc(s_zero, 1)

            @block.vector
            def _(eng):
                eng.wait_ge(s_const, 16 * 10)
                for g in range(tiles):
                    eng.tensor_tensor(posb[:, g, :], posb[:, g, :], bias[0:ROWS * BLK, :], ALU.add).then_inc(s_posb, 1)
                eng.tensor_tensor(clsrow[:, :], clsrow[:, :], posrow[:, :], ALU.add).then_inc(s_cls, 1)
                eng.wait_ge(s_posb, 7)
                with eng.Fori(0, B // 2) as i:
                    for p in range(2):
                        eng.wait_ge(s_st[p], AHEAD + 16 * ROWS * i)
                        for g in range(7):
                            m = wide[g]
                            eng.wait_ge(s_mm, 14 * i + 7 * p + g + 1)
                            eng.tensor_tensor(out[0:m, p, g, :], acc[0:m, (7 * p + g) % 2, 0:D],
                                              posb[0:m, g, :], ALU.add).then_inc(s_ev, 1)

            @block.tensor
            def _(eng):
                eng.wait_ge(s_const, 16 * 10)
                with eng.Fori(0, B // 2) as i:
                    for p in range(2):
                        eng.wait_ge(s_in[p], 48 * i + 48)
                        for g in range(tiles):
                            m = wide[g]
                            n = 14 * i + 7 * p + g
                            if 7 * p + g >= 2:
                                eng.wait_ge(s_ev, AHEAD + n - 1)
                            else:
                                eng.wait_ge(s_ev, AHEAD + 14 * i)
                            o = acc[0:m, (7 * p + g) % 2, 0:D]
                            for dr in range(2):
                                at = (g * ROWS + dr) * BLK
                                for dc in range(2):
                                    eng.matmul(o, main[:, p, at + dc:at + dc + m], w_main[:, 2 * dr + dc, :],
                                               start=(dr == 0 and dc == 0), stop=False)
                                mm = eng.matmul(o, rest[:, p, at:at + m], w_rest[:, dr, :],
                                                start=False, stop=(dr == 1))
                            mm.then_inc(s_mm, 1)


def normalise(nc, sp, c, h_rows, w_in, norm1, x_rows, xt, params):
    with sp.phase() as ctx:
        ident = sp.sb(ctx, "nm_ident", [128, 128])
        wp = sp.sb(ctx, "nm_wp", [K2, 2, 2 * H])
        n1 = sp.sb(ctx, "nm_n1", [K2, 2])
        half = sp.sb(ctx, "nm_half", [128, GT4])
        h = sp.sb(ctx, "nm_h", [L, 2, GT4, D])
        st = sp.sb(ctx, "nm_st", [L, 2, GT4, 6])
        mv = sp.sb(ctx, "nm_mv", [L, 2, GT4, 2])
        sc = sp.sb(ctx, "nm_sc", [L, 2, 4, GT4])
        x = sp.sb(ctx, "nm_x", [L, 2, GT4, D])
        xr = sp.sb(ctx, "nm_xr", [L, 2, GT4, D])
        xts = sp.sb(ctx, "nm_xts", [K2, 2, 2, GW])
        pts = sp.sb(ctx, "nm_pts", [2 * H, 2, GW])
        tp = sp.ps(ctx, "nm_tp", [128, 4, 512])
        pp = sp.ps(ctx, "nm_pp", [128, 2, 512])
        s_const, s_w, s_half = sp.sem("nm_const"), sp.sem("nm_w"), sp.sem("nm_half_set")
        s_in = [sp.sem("nm_in0"), sp.sem("nm_in1")]
        s_mv, s_sc, s_x, s_xr = sp.sem("nm_mv"), sp.sem("nm_sc"), sp.sem("nm_x"), sp.sem("nm_xr")
        s_tp, s_xt, s_pp, s_pt = sp.sem("nm_tp"), sp.sem("nm_xt"), sp.sem("nm_pp"), sp.sem("nm_pt")
        s_st = [sp.sem("nm_st0"), sp.sem("nm_st1")]
        s_link, s_glink = sp.sem("nm_link"), sp.sem("nm_glink")

        with nc.Block() as block:
            @block.sync
            def _(eng):
                eng.dma_start(ident[:, :], c["ident"]).then_inc(s_const, 16)
                eng.dma_start(wp[:, :, :], w_in[:, 2 * DI:2 * DI + 2 * H].rearrange("(k p) n -> p k n", p=K2)).then_inc(s_const, 16)
                eng.dma_start(n1[:, :], norm1).then_inc(s_const, 16)
                start_counts(eng, *s_st, s_x, s_xr, s_tp, s_xt, s_pt)
                for p in range(2):
                    eng.dma_start(h[:, p, :, :], row_tiles(h_rows, p)).then_inc(s_in[p], 16)
                with eng.Fori(0, NG // 2 - 1) as i:
                    for p in range(2):
                        eng.wait_ge(s_x, done(2 * i + p))
                        eng.dma_start(h[:, p, :, :], row_tiles(h_rows, 2 * i + p + 2)).then_inc(s_in[p], 16)

            @block.vector
            def _(eng):
                eng.wait_ge(s_const, 48)
                for k in range(2):
                    eng.tensor_scalar(wp[:, k, :], wp[:, k, :], n1[:, k:k + 1], None, ALU.mult).then_inc(s_w, 1)
                with eng.Fori(0, NG // 2) as i:
                    for p in range(2):
                        eng.wait_ge(s_in[p], 16 * i + 16)
                        for j in range(GT4):
                            eng.bn_stats(st[:, p, j, :], h[:, p, j, :]).then_inc(s_link, 1)
                        eng.wait_ge(s_link, 8 * i + 4 * p + 4)
                        settle(eng, sp.settled)
                        for j in range(GT4):
                            mm = eng.bn_aggr(mv[:, p, j, :], st[:, p, j, :])
                        mm.then_inc(s_mv, 1)
                        eng.wait_ge(s_sc, 2 * i + p + 1)
                        eng.wait_ge(s_st[p], AHEAD + 48 * i)
                        for j in range(GT4):
                            mm = eng.tensor_scalar(x[:, p, j, :], h[:, p, j, :], mv[:, p, j, 0:1], sc[:, p, 0, j:j + 1],
                                                   ALU.subtract, ALU.mult)
                        mm.then_inc(s_x, 1)
                        eng.wait_ge(s_pp, 2 * i + p + 1)
                        eng.tensor_copy(pts[:, p, :], pp[0:2 * H, p, 0:GW]).then_inc(s_pt, 1)

            @block.gpsimd
            def _(eng):
                eng.memset(half[:, :], -0.5).then_inc(s_half, 1)
                eng.wait_ge(s_half, 1)
                with eng.Fori(0, NG // 2) as i:
                    for p in range(2):
                        steps = [0]

                        def link(ins):
                            steps[0] += 1
                            ins.then_inc(s_glink, 1)
                            eng.wait_ge(s_glink, 10 * i + 5 * p + steps[0])
                            settle(eng, sp.settled)

                        eng.wait_ge(s_mv, 2 * i + p + 1)
                        eng.wait_ge(s_xr, done(2 * i + p - 2))
                        settle(eng, sp.settled)
                        rstd, r, tmp, tm2 = (sc[:, p, q, :] for q in range(4))
                        link(eng.tensor_scalar(tmp, mv[:, p, :, 1], LN_EPS, None, ALU.add))
                        link(eng.tensor_tensor(rstd, tmp, half[0:L, :], ALU.pow))
                        link(eng.tensor_tensor(tm2, rstd, rstd, ALU.mult))
                        link(eng.tensor_tensor(tm2, tm2, mv[:, p, :, 1], ALU.mult))
                        link(eng.tensor_scalar(tm2, tm2, RMS_EPS, None, ALU.add))
                        eng.tensor_tensor(r, tm2, half[0:L, :], ALU.pow).then_inc(s_sc, 1)

            @block.scalar
            def _(eng):
                with eng.Fori(0, NG // 2) as i:
                    for p in range(2):
                        g = 2 * i + p
                        eng.wait_ge(s_x, done(g))
                        eng.wait_ge(s_tp, done(g - 2))
                        for j in range(GT4):
                            mm = eng.activation(xr[:, p, j, :], x[:, p, j, :], ACT.Copy, scale=sc[:, p, 1, j:j + 1])
                        mm.then_inc(s_xr, 1)
                        eng.wait_ge(s_st[p], AHEAD + 48 * i)
                        eng.wait_ge(s_tp, done(g))
                        for k in range(2):
                            mm = eng.activation(xts[:, p, k, :], tp[0:K2, 2 * p + k, 0:GW], ACT.Copy)
                        mm.then_inc(s_xt, 1)
                        eng.dma_start(row_tiles(x_rows, g), x[:, p, :, :]).then_inc(s_st[p], 16)
                        eng.wait_ge(s_xt, done(g))
                        eng.dma_start(xt[:, :, bass.ds(g * GW, GW)], xts[:, p, :, :]).then_inc(s_st[p], 16)
                        eng.wait_ge(s_pt, done(g))
                        eng.dma_start(params[:, bass.ds(g * GW, GW)], pts[:, p, :]).then_inc(s_st[p], 16)
                for p in range(2):
                    eng.wait_ge(s_st[p], AHEAD + 48 * (NG // 2))

            @block.tensor
            def _(eng):
                eng.wait_ge(s_w, 2)
                with eng.Fori(0, NG // 2) as i:
                    for p in range(2):
                        g = 2 * i + p
                        eng.wait_ge(s_xr, done(g))
                        eng.wait_ge(s_xt, done(g - 2))
                        for k in range(2):
                            for j in range(GT4):
                                mm = eng.transpose(tp[0:K2, 2 * p + k, L * j:L * j + L],
                                                   xr[:, p, j, K2 * k:K2 * k + K2], ident[0:L, 0:L])
                        mm.then_inc(s_tp, 1)
                        eng.wait_ge(s_xt, done(g))
                        eng.wait_ge(s_pt, done(g - 2))
                        for k in range(2):
                            mm = eng.matmul(pp[0:2 * H, p, 0:GW], wp[:, k, :], xts[:, p, k, :], start=(k == 0), stop=(k == 1))
                        mm.then_inc(s_pp, 1)


GROUPS = ((0, 4), (4, 8), (8, 12), (12, 15))
KG = len(GROUPS) * L // STEPS


def mixer_turns(eng, stages, boundary):
    half = B // 2

    def slot(c, j, q, more, first=False):
        for lag, f in stages:
            if lag is None:
                if more:
                    f(c + 1, j, q)
            elif q >= lag or not isinstance(j, int):
                f(c, 2 * j + (q - lag), (q - lag) % 2, c * half + j + (q - lag) // 2)
            elif not first:
                f(c - 1, B + q - lag, (q - lag) % 2, c * half - 1)

    def chunk(c, more, first=False):
        for q in range(2):
            slot(c, 0, q, more, first)
        with eng.Fori(1, half) as j:
            for q in range(2):
                slot(c, j, q, more)
        if more:
            boundary(c + 1)

    with eng.Fori(0, half) as j:
        for q in range(2):
            for lag, f in stages:
                if lag is None:
                    f(0, j, q)
    boundary(0)
    chunk(0, True, first=True)
    with eng.Fori(1, CH - 2) as c:
        chunk(c, True)
    chunk(CH - 2, True)
    chunk(CH - 1, False)
    for q in range(2):
        for lag, f in stages:
            if lag is not None and lag > q:
                f(CH - 1, B + q - lag, (q - lag) % 2, CH * half - 1)

def mixer(nc, sp, c, x_rows, xt, params, x2_rows):
    with sp.phase() as ctx:
        def sb(name, shape):
            return sp.sb(ctx, "mx_" + name, shape)

        def sem(name):
            return sp.sem("mx_" + name)

        ident = sb("ident", [128, 128])
        wg = sb("wg", [K2, 2, 2 * DI])
        n1 = sb("n1", [K2, 2])
        wbc = sb("wbc", [128, 3, EP])
        wout = sb("wout", [128, 3, D])
        cw = sb("cw", [128, 3, 4])
        dskip = sb("dskip", [L, H])
        block_mask = sb("block_mask", [EP, DI])
        step_mask = sb("step_mask", [EP, EP])
        head_col = sb("head_col", [H * NS, H])
        spread = sb("spread", [SEQ, 2, EP])
        image_mask = sb("image_mask", [SEQ, B])
        half = sb("half", [L, 2 * H])
        s_all, d_all, n_all, tmp_all = (sb(n, [SEQ, TP]) for n in ("s", "d", "n", "t"))
        ring = sb("ring", [SEQ, STEPS, PAD + KW])
        z = sb("z", [SEQ, PAD + KW])
        zt = sb("zt", [SEQ, KW])
        unit_rows = sb("unit_rows", [SEQ, 2, L])
        kern = sb("kern", [L, 2, L, SEQ])
        coef = sb("coef", [L, 2, 4, SEQ])
        phi_rhs = sb("phi_rhs", [SEQ, 2, 2, B])
        phi = sb("phi", [EP, 2, 2, B])
        halo = sb("halo", [128, B, 3, 3])
        state = sb("state", [EP, B, DI])
        xts = sb("xts", [K2, 2, 2, L])
        xin = sb("xin", [L, 2, D])
        vb = sb("vb", [128, 2, 3, 3 + L])
        cv = sb("cv", [128, 2, 3, L])
        vt = sb("vt", [128, 2, 3, L])
        u = sb("u", [L, 2, DI])
        ud = sb("ud", [L, 2, DI])
        sg = sb("sg", [L, 2, DI])
        sq = sb("sq", [L, 2, EP])
        rs = sb("rs", [L, 2, 2 * H])
        rn = sb("rn", [L, 2, 2 * H])
        bcn = sb("bcn", [L, 2, EP])
        br = sb("br", [L, 2, EP])
        cr = sb("cr", [L, 2, EP])
        tb = sb("tb", [EP, 2, EP])
        bt = sb("bt", [H * NS, 2, L])
        cm = sb("cm", [H * NS, 2, H, L])
        crt = sb("crt", [EP, 2, L])
        m = sb("m", [L, 2, H, L])
        gy = sb("gy", [L, 2, DI])
        gyt = sb("gyt", [128, 2, 3, L])
        x2 = sb("x2", [L, 2, D])

        bank = [sp.ps(ctx, f"mx_bank{i}", [128, 512]) for i in range(8)]
        b_v, b_gate, b_bc, b_u, b_s0, b_s1, b_y, b_st = bank
        b_s = (b_s0, b_s1)

        s_const, s_w, s_mem, s_par = sem("const"), sem("w"), sem("mem"), sem("par")
        s_xt = [sem("xt0"), sem("xt1")]
        s_xin = [sem("xin0"), sem("xin1")]
        s_store = [sem("store0"), sem("store1")]
        s_prep, s_alink = sem("prep"), sem("prep_act")
        s_conv_part, s_zero = sem("conv_part"), sem("zero")
        s_start, s_ring, s_link = sem("start"), sem("ring"), sem("link")
        s_kt, s_kern, s_unit = sem("kernel_transposed"), sem("kernel_kept"), sem("unit_rows")
        s_ct, s_coef, s_pr, s_pm, s_phi = sem("coef_t"), sem("coef"), sem("phi_rhs"), sem("phi_mm"), sem("phi")
        names = ("vmm", "gmm", "vtaken", "halo_in", "halo_out", "conv", "silu", "bcmm", "ut", "sq", "u", "gate",
                 "rs", "rn", "bcn", "br", "cr", "tb", "tr", "cm", "bt", "crt", "smm", "m", "ymm", "stmm", "st",
                 "ud", "gsum", "gy", "gyt_mm", "gyt", "omm", "x2", "rlink")
        e = {n: sem(n) for n in names}

        def tile(buf, k_c, k_b):
            return buf[bass.ds((k_b * CH + k_c) * L, L), :]

        def image(buf, b):
            return buf[:, bass.ds(b, 1)]

        with nc.Block() as block:
            @block.sync
            def _(eng):
                start_counts(eng, *s_store, s_kt, s_ct, s_pm, s_kern, s_link, *e.values())
                pv = params.rearrange("(q h) (b t) -> q h b t", q=2, b=B)
                for h in range(H):
                    eng.dma_start(s_all[h * B:(h + 1) * B, :], pv[0, h]).then_inc(s_par, 16)
                    eng.dma_start(d_all[h * B:(h + 1) * B, :], pv[1, h]).then_inc(s_par, 16)
                for dst, name in ((ident, "ident"), (block_mask, "block_mask"), (step_mask, "step_mask"),
                                  (head_col, "head_col"), (image_mask, "image_mask"), (n1, "norm1")):
                    eng.dma_start(dst[:, :], c[name]).then_inc(s_const, 16)
                for dst, name in ((spread, "spread"), (cw, "conv_w")):
                    eng.dma_start(dst[:, :, :], c[name]).then_inc(s_const, 16)
                eng.dma_start(wg[:, :, :], c["w_in"][:, 0:2 * DI].rearrange("(k p) n -> p k n", p=K2)).then_inc(s_const, 16)
                eng.dma_start(wbc[:, :, :], c["w_bc"].rearrange("(k p) n -> p k n", p=128)).then_inc(s_const, 16)
                eng.dma_start(wout[:, :, :], c["w_out"].rearrange("(k p) n -> p k n", p=128)).then_inc(s_const, 16)
                eng.dma_start(dskip[:, :], c["d_skip"].rearrange("(o h) -> o h", o=1).to_broadcast([L, H])).then_inc(s_const, 16)
                xtv = xt.rearrange("p k (b t) -> p k b t", b=B)

                def load(ci, b, p, i):
                    k = ci * B + b
                    eng.wait_ge(e["gmm"], done(k - 2))
                    src = xtv[:, :, bass.ds(b, 1), bass.ds(ci * L, L)].rearrange("p k o t -> p k (o t)")
                    eng.dma_start(xts[:, p, :, :], src).then_inc(s_xt[p], 16)
                    eng.wait_ge(e["x2"], done(k - 2))
                    eng.dma_start(xin[:, p, :], tile(x_rows, ci, b)).then_inc(s_xin[p], 16)

                def nothing(*_):
                    pass

                mixer_turns(eng, [(0, load), (None, nothing)], nothing)

            @block.gpsimd
            def _(eng):
                eng.memset(half[:, :], -0.5).then_inc(s_mem, 1)
                eng.memset(halo[:, :, :, :], 0.0).then_inc(s_mem, 1)
                eng.memset(state[:, :, :], 0.0).then_inc(s_mem, 1)
                eng.wait_ge(s_mem, 3)
                eng.wait_ge(s_const, 16 * 12)

                def halos(ci, b, p, i):
                    k = ci * B + b
                    hb = image(halo, b).rearrange("p o f t -> p (o f) t")
                    eng.wait_ge(e["conv"], done(k - 2))
                    eng.wait_ge(e["halo_out"], done(k - 1))
                    settle(eng, sp.settled)
                    eng.tensor_copy(vb[:, p, :, 0:3], hb).then_inc(e["halo_in"], 1)
                    eng.wait_ge(e["vtaken"], done(k))
                    eng.wait_ge(e["halo_in"], done(k))
                    settle(eng, sp.settled)
                    eng.tensor_copy(hb, vb[:, p, :, L:L + 3]).then_inc(e["halo_out"], 1)

                def step(ci, b, p, i):
                    k = ci * B + b
                    eng.wait_ge(s_phi, ci + 1)
                    eng.wait_ge(e["stmm"], done(k - 2))
                    settle(eng, sp.settled)
                    pb = phi[:, bass.ds(ci % 2, 1), :, bass.ds(b, 1)].rearrange("q o j u -> q j (o u)")
                    eng.tensor_tensor(tb[:, p, :].rearrange("q (h j n) -> q h j n", h=H, j=2),
                                      step_mask[:, :].rearrange("q (h j n) -> q h j n", h=H, j=2),
                                      pb.unsqueeze(1).to_broadcast([EP, H, 2, NS]), ALU.mult).then_inc(e["tb"], 1)

                def norms(ci, b, p, i):
                    k = ci * B + b
                    eng.wait_ge(e["rs"], done(k))
                    eng.wait_ge(e["bcn"], done(k - 2))
                    settle(eng, sp.settled)
                    eng.tensor_scalar(rs[:, p, :], rs[:, p, :], L2_EPS, None, ALU.add).then_inc(e["rlink"], 1)
                    eng.wait_ge(e["rlink"], done(k))
                    settle(eng, sp.settled)
                    eng.tensor_tensor(rn[:, p, :], rs[:, p, :], half[:, :], ALU.pow).then_inc(e["rn"], 1)

                def weighted(ci, b, p, i):
                    k = ci * B + b
                    eng.wait_ge(e["bcn"], done(k))
                    eng.wait_ge(s_coef, ci + 1)
                    eng.wait_ge(e["tr"], done(k - 2))
                    eng.wait_ge(e["stmm"], done(k - 2))
                    settle(eng, sp.settled)
                    for dst, off, q0, name in ((cr, H * NS, 0, "cr"), (br, 0, 2, "br")):
                        src = bcn[:, p, off:off + H * NS].rearrange("t (h n) -> t h n", h=H)
                        for j in range(2):
                            w = coef[:, bass.ds(ci % 2, 1), q0 + j, :].rearrange("t o (h b) -> t (o h) b", h=H)[:, :, bass.ds(b, 1)]
                            ins = eng.tensor_tensor(dst[:, p, :].rearrange("t (h j n) -> t h j n", h=H, j=2)[:, :, j, :],
                                                    src, w.to_broadcast([L, H, NS]), ALU.mult)
                        ins.then_inc(e[name], 1)

                def skipped(ci, b, p, i):
                    k = ci * B + b
                    eng.wait_ge(e["u"], done(k))
                    eng.wait_ge(e["gsum"], done(k - 2))
                    settle(eng, sp.settled)
                    eng.tensor_tensor(ud[:, p, :].rearrange("t (h q) -> t h q", h=H),
                                      u[:, p, :].rearrange("t (h q) -> t h q", h=H),
                                      dskip[:, :].unsqueeze(2).to_broadcast([L, H, P]), ALU.mult).then_inc(e["ud"], 1)

                def nothing(*_):
                    pass

                mixer_turns(eng, [(0, halos), (0, step), (0, norms), (0, weighted), (0, skipped), (None, nothing)], nothing)

            @block.scalar
            def _(eng):
                eng.wait_ge(s_prep, 1)
                eng.activation(tmp_all[:, :], tmp_all[:, :], ACT.Exp, scale=-1.0).then_inc(s_alink, 1)
                eng.wait_ge(s_alink, 1)
                eng.activation(tmp_all[:, :], tmp_all[:, :], ACT.Ln, bias=1.0).then_inc(s_alink, 1)
                eng.activation(d_all[:, :], d_all[:, :], ACT.Exp, scale=-1.0).then_inc(s_alink, 1)
                eng.wait_ge(s_const, 16 * 12)

                def masked(ci, b, p, i):
                    k = ci * B + b
                    eng.wait_ge(e["tr"], done(k))
                    eng.wait_ge(e["smm"], done(k - 2))
                    eng.activation(bt[:, p, :], b_bc[0:H * NS, 128:128 + L], ACT.Copy).then_inc(e["bt"], 1)
                    for h in range(H):
                        ins = eng.activation(cm[:, p, h, :], b_bc[0:H * NS, 128 + L:128 + 2 * L], ACT.Copy, scale=head_col[:, h:h + 1])
                    ins.then_inc(e["cm"], 1)

                def unit_c(ci, b, p, i):
                    k = ci * B + b
                    eng.wait_ge(e["ymm"], done(k - 2))
                    eng.activation(crt[:, p, :], b_bc[0:EP, 128 + 2 * L:128 + 3 * L], ACT.Copy).then_inc(e["crt"], 1)

                def values(ci, b, p, i):
                    k = ci * B + b
                    eng.wait_ge(e["vmm"], done(k))
                    eng.wait_ge(e["conv"], done(k - 2))
                    eng.wait_ge(e["halo_out"], done(k - 2))
                    eng.activation(vb[:, p, :, 3:3 + L], b_v[:, 0:3 * L].rearrange("q (f t) -> q f t", f=3), ACT.Copy).then_inc(e["vtaken"], 1)

                def gates(ci, b, p, i):
                    k = ci * B + b
                    eng.wait_ge(e["gmm"], done(k))
                    eng.wait_ge(e["gy"], done(k - 2))
                    eng.activation(sg[:, p, :], b_gate[0:L, 0:DI], ACT.Silu).then_inc(e["gate"], 1)

                def silu(ci, b, p, i):
                    k = ci * B + b
                    eng.wait_ge(e["conv"], done(k))
                    eng.wait_ge(e["ut"], done(k - 2))
                    eng.activation(vt[:, p, :, :], cv[:, p, :, :], ACT.Silu).then_inc(e["silu"], 1)

                def squares(ci, b, p, i):
                    k = ci * B + b
                    eng.wait_ge(e["bcmm"], done(k))
                    eng.wait_ge(e["rs"], done(k - 2))
                    eng.activation(sq[:, p, :], b_bc[0:L, 0:EP], ACT.Square).then_inc(e["sq"], 1)

                def inputs(ci, b, p, i):
                    k = ci * B + b
                    eng.wait_ge(e["ut"], done(k))
                    eng.wait_ge(e["stmm"], done(k - 2))
                    eng.wait_ge(e["ud"], done(k - 2))
                    eng.activation(u[:, p, :], b_u[0:L, 0:DI], ACT.Copy).then_inc(e["u"], 1)

                def gated(ci, b, p, i):
                    k = ci * B + b
                    eng.wait_ge(e["gyt_mm"], done(k))
                    eng.wait_ge(e["omm"], done(k - 2))
                    eng.activation(gyt[:, p, :, :], b_u[:, 0:3 * L].rearrange("q (f t) -> q f t", f=3), ACT.Copy).then_inc(e["gyt"], 1)

                def store(ci, b, p, i):
                    k = ci * B + b
                    eng.wait_ge(e["x2"], done(k))
                    eng.dma_start(tile(x2_rows, ci, b), x2[:, p, :]).then_inc(s_store[p], 16)

                def kernel_rows(ci, j, q):
                    eng.wait_ge(e["m"], done(ci * B - B - 1))
                    for a in range(2):
                        r0, r1 = GROUPS[2 * q + a]
                        eng.wait_ge(s_kt, AHEAD + KG * ci + 4 * j + 2 * q + a + 1)
                        eng.activation(kern[:, bass.ds(ci % 2, 1), bass.ds(j * STEPS + r0, r1 - r0), :].rearrange("t o r s -> t (o r) s"),
                                       b_s[a][0:L, 0:(r1 - r0) * SEQ].rearrange("t (r s) -> t r s", s=SEQ), ACT.Copy).then_inc(s_kern, 1)

                def boundary(ci):
                    eng.wait_ge(s_ct, AHEAD + ci + 1)
                    eng.wait_ge(e["br"], done(ci * B - B - 1))
                    eng.activation(coef[:, bass.ds(ci % 2, 1), :, :].rearrange("t o q s -> t (o q) s"),
                                   b_s0[0:L, 0:4 * SEQ].rearrange("t (q s) -> t q s", q=4), ACT.Copy).then_inc(s_coef, 1)
                    eng.wait_ge(s_pm, AHEAD + ci + 1)
                    eng.wait_ge(e["tb"], done(ci * B - B - 1))
                    eng.activation(phi[:, bass.ds(ci % 2, 1), :, :].rearrange("q o j b -> q (o j) b"),
                                   b_s1[0:EP, 0:2 * B].rearrange("q (j b) -> q j b", j=2), ACT.Copy).then_inc(s_phi, 1)

                mixer_turns(eng, [(1, masked), (0, values), (1, unit_c), (0, gates), (0, silu), (0, squares), (0, inputs),
                                  (1, gated), (2, store), (None, kernel_rows)], boundary)
                for p in range(2):
                    eng.wait_ge(s_store[p], AHEAD + 16 * (NT // 2))

            @block.vector
            def _(eng):
                link = chain(eng, s_prep, 0)
                eng.memset(z[:, 0:PAD], 0.0).then_inc(s_zero, 1)
                eng.memset(ring[:, :, 0:PAD], 0.0).then_inc(s_zero, 1)
                eng.wait_ge(s_par, 16 * 2 * H)
                link(eng.scalar_tensor_tensor(tmp_all[:, :], s_all[:, :], -1.0, s_all[:, :], ALU.mult, ALU.max))
                eng.wait_ge(s_alink, 3)
                link(eng.scalar_tensor_tensor(n_all[:, :], s_all[:, :], 0.0, tmp_all[:, :], ALU.max, ALU.add))
                link(eng.tensor_scalar(d_all[:, :], d_all[:, :], 1.0, None, ALU.add))
                link(eng.reciprocal(d_all[:, :], d_all[:, :]))
                link(eng.tensor_tensor(n_all[:, :], n_all[:, :], d_all[:, :], ALU.mult))
                link(eng.tensor_tensor(tmp_all[:, :], n_all[:, :], d_all[:, :], ALU.mult))
                link(eng.tensor_scalar(tmp_all[:, :], tmp_all[:, :], 1.0, None, ALU.add))
                link(eng.reciprocal(s_all[:, :], tmp_all[:, :]))
                link(eng.scalar_tensor_tensor(n_all[:, :], n_all[:, :], -1.0, s_all[:, :], ALU.mult, ALU.mult))
                eng.wait_ge(s_const, 16 * 12)
                for k in range(2):
                    eng.tensor_scalar(wg[:, k, :], wg[:, k, :], n1[:, k:k + 1], None, ALU.mult).then_inc(s_w, 1)
                eng.wait_ge(s_zero, 2)

                def start(ci):
                    eng.wait_ge(s_kt, AHEAD + KG * ci)
                    eng.wait_ge(s_ct, AHEAD + ci)
                    eng.memset(ring[:, :, PAD:PAD + KW], 0.0).then_inc(s_start, 1)
                    eng.memset(z[:, PAD:PAD + 1], 1.0).then_inc(s_start, 1)
                    eng.memset(z[:, PAD + 1:PAD + 2], 0.0).then_inc(s_start, 1)
                    eng.tensor_copy(z[:, PAD + 2:PAD + 2 + L], d_all[:, bass.ds(ci * L, L)]).then_inc(s_start, 1)
                    eng.wait_ge(s_start, 5 * ci + 4)
                    eng.memset(ring[:, STEPS - 1, PAD + 1:PAD + 2], 1.0).then_inc(s_start, 1)
                    eng.wait_ge(s_start, 5 * ci + 5)
                    settle(eng, sp.settled)

                def kernel_steps(ci, j, q):
                    for a in range(2):
                        r0, r1 = GROUPS[2 * q + a]
                        group = KG * ci + 4 * j + 2 * q + a
                        eng.wait_ge(s_kt, AHEAD + group - 3)
                        for r in range(r0, r1):
                            t = j * STEPS + r
                            at = ci * L + t
                            zz = z[:, bass.ds(t, KW)]
                            old = ring[:, (r - 1) % STEPS, bass.ds(t, KW)]
                            new = ring[:, r, bass.ds(t, KW)]
                            count = AHEAD + 3 * at
                            eng.wait_ge(s_link, count)
                            eng.tensor_scalar(zt[:, :], old, n_all[:, bass.ds(at, 1)], None, ALU.mult).then_inc(s_link, 1)
                            eng.wait_ge(s_link, count + 1)
                            eng.scalar_tensor_tensor(zz, zz, s_all[:, bass.ds(at, 1)], zt[:, :], ALU.mult, ALU.add).then_inc(s_link, 1)
                            eng.wait_ge(s_link, count + 2)
                            eng.scalar_tensor_tensor(new, zz, d_all[:, bass.ds(at, 1)], old, ALU.mult, ALU.add).then_inc(s_link, 1)
                        eng.wait_ge(s_link, count + 3)
                        eng.tensor_copy(unit_rows[:, :, bass.ds(j * STEPS + r0, r1 - r0)].rearrange("s u t -> s t u"),
                                        ring[:, r0:r1, PAD:PAD + 2]).then_inc(s_ring, 1)

                def boundary(ci):
                    eng.wait_ge(s_pm, AHEAD + ci)
                    for to, src in ((0, z[:, PAD:PAD + 2]), (1, ring[:, STEPS - 1, PAD:PAD + 2])):
                        for fr in range(2):
                            ins = eng.tensor_scalar(phi_rhs[:, fr, to, :], image_mask[:, :], src[:, fr:fr + 1], None, ALU.mult)
                    ins.then_inc(s_pr, 1)
                    if not (isinstance(ci, int) and ci == CH - 1):
                        eng.wait_ge(s_pr, ci + 1)
                        start(ci + 1)

                def conv(ci, b, p, i):
                    k = ci * B + b
                    eng.wait_ge(e["vtaken"], done(k))
                    eng.wait_ge(e["halo_in"], done(k))
                    eng.wait_ge(e["silu"], done(k - 2))
                    for f in range(3):
                        eng.tensor_scalar(cv[:, p, f, :], vb[:, p, f, 0:L], cw[:, f, 0:1], None, ALU.mult).then_inc(s_conv_part, 1)
                    for tap in range(1, 4):
                        eng.wait_ge(s_conv_part, 9 * k + 3 * tap)
                        for f in range(3):
                            ins = eng.scalar_tensor_tensor(cv[:, p, f, :], vb[:, p, f, tap:tap + L], cw[:, f, tap:tap + 1],
                                                           cv[:, p, f, :], ALU.mult, ALU.add)
                            if tap < 3:
                                ins.then_inc(s_conv_part, 1)
                    ins.then_inc(e["conv"], 1)

                def sums(ci, b, p, i):
                    k = ci * B + b
                    eng.wait_ge(e["sq"], done(k))
                    eng.wait_ge(e["rn"], done(k - 2))
                    eng.tensor_reduce(rs[:, p, :], sq[:, p, :].rearrange("t (g n) -> t g n", n=NS), AX.X, ALU.add).then_inc(e["rs"], 1)

                def unit(ci, b, p, i):
                    k = ci * B + b
                    eng.wait_ge(e["rn"], done(k))
                    eng.wait_ge(e["br"], done(k - 2))
                    eng.wait_ge(e["tr"], done(k - 2))
                    eng.tensor_tensor(bcn[:, p, :].rearrange("t (g n) -> t g n", n=NS),
                                      b_bc[0:L, 0:EP].rearrange("t (g n) -> t g n", n=NS),
                                      rn[:, p, :].unsqueeze(2).to_broadcast([L, 2 * H, NS]), ALU.mult).then_inc(e["bcn"], 1)

                def kernel_by(ci, b, p, i):
                    k = ci * B + b
                    eng.wait_ge(e["smm"], done(k))
                    eng.wait_ge(e["ymm"], done(k - 2))
                    eng.wait_ge(s_kern, AHEAD + KG * ci + KG)
                    for part in range(2):
                        kv = kern[:, bass.ds(ci % 2, 1), :, :].rearrange("q o t (h b) -> q h b (o t)", h=H)[:, 3 * part:3 * part + 3, bass.ds(b, 1), :]
                        ins = eng.tensor_tensor(m[:, p, 3 * part:3 * part + 3, :],
                                                b_s[part][0:L, 0:3 * L].rearrange("q (h t) -> q h t", h=3),
                                                kv.rearrange("q h o t -> q (h o) t"), ALU.mult)
                    ins.then_inc(e["m"], 1)

                def new_state(ci, b, p, i):
                    k = ci * B + b
                    eng.wait_ge(e["stmm"], done(k))
                    eng.tensor_tensor(image(state, b).rearrange("q o n -> q (o n)"),
                                      b_st[0:EP, 0:DI], block_mask[:, :], ALU.mult).then_inc(e["st"], 1)

                def gating(ci, b, p, i):
                    k = ci * B + b
                    eng.wait_ge(e["ymm"], done(k))
                    eng.wait_ge(e["ud"], done(k))
                    eng.wait_ge(e["gyt_mm"], done(k - 2))
                    eng.tensor_tensor(gy[:, p, :], b_y[0:L, 0:DI], ud[:, p, :], ALU.add).then_inc(e["gsum"], 1)
                    eng.wait_ge(e["gsum"], done(k))
                    eng.wait_ge(e["gate"], done(k))
                    eng.tensor_tensor(gy[:, p, :], gy[:, p, :], sg[:, p, :], ALU.mult).then_inc(e["gy"], 1)

                def output(ci, b, p, i):
                    k = ci * B + b
                    eng.wait_ge(e["omm"], done(k))
                    eng.wait_ge(s_xin[p], 16 * i + 16)
                    eng.wait_ge(s_store[p], AHEAD + 16 * i)
                    eng.tensor_tensor(x2[:, p, :], b_st[0:L, 0:D], xin[:, p, :], ALU.add).then_inc(e["x2"], 1)

                start(0)
                mixer_turns(eng, [(0, conv), (2, output), (1, kernel_by), (0, sums), (0, unit), (None, kernel_steps),
                                  (1, gating), (1, new_state)], boundary)

            @block.tensor
            def _(eng):
                eng.wait_ge(s_const, 16 * 12)
                eng.wait_ge(s_w, 2)
                eng.wait_ge(s_mem, 3)

                def turned(ci, b, p, i):
                    k = ci * B + b
                    eng.wait_ge(e["bcn"], done(k))
                    eng.wait_ge(e["cr"], done(k))
                    settle(eng, sp.settled)
                    for j in range(2):
                        eng.transpose(b_bc[0:H * NS, 128 + L * j:128 + L * j + L], bcn[:, p, H * NS * j:H * NS * (j + 1)], ident[0:L, 0:L])
                    eng.transpose(b_bc[0:EP, 128 + 2 * L:128 + 3 * L], cr[:, p, :], ident[0:L, 0:L]).then_inc(e["tr"], 1)

                def values(ci, b, p, i):
                    k = ci * B + b
                    eng.wait_ge(s_xt[p], 16 * i + 16)
                    eng.wait_ge(e["vtaken"], done(k - 1))
                    for f in range(3):
                        for kk in range(2):
                            mm = eng.matmul(b_v[:, L * f:L * f + L], wg[:, kk, DI + 128 * f:DI + 128 * f + 128],
                                            xts[:, p, kk, :], start=(kk == 0), stop=(kk == 1))
                    mm.then_inc(e["vmm"], 1)

                def gates(ci, b, p, i):
                    k = ci * B + b
                    eng.wait_ge(e["gate"], done(k - 1))
                    for kk in range(2):
                        mm = eng.matmul(b_gate[0:L, 0:DI], xts[:, p, kk, :], wg[:, kk, 0:DI], start=(kk == 0), stop=(kk == 1))
                    mm.then_inc(e["gmm"], 1)

                def project(ci, b, p, i):
                    k = ci * B + b
                    eng.wait_ge(e["gyt"], done(k))
                    eng.wait_ge(e["st"], done(k))
                    for f in range(3):
                        mm = eng.matmul(b_st[0:L, 0:D], gyt[:, p, f, :], wout[:, f, :], start=(f == 0), stop=(f == 2))
                    mm.then_inc(e["omm"], 1)

                def scores(ci, b, p, i):
                    k = ci * B + b
                    eng.wait_ge(e["bt"], done(k))
                    eng.wait_ge(e["cm"], done(k))
                    eng.wait_ge(e["m"], done(k - 1))
                    if isinstance(ci, int) and ci == CH - 1:
                        eng.wait_ge(s_kern, AHEAD + KG * CH)
                    else:
                        eng.wait_ge(s_kern, AHEAD + KG + 2 * (k + 1))
                    eng.wait_ge(s_coef, ci + 1)
                    eng.wait_ge(s_phi, ci + 1)
                    for part in range(2):
                        mm = eng.matmul(b_s[part][0:L, 0:3 * L], bt[:, p, :],
                                        cm[:, p, 3 * part:3 * part + 3, :].rearrange("q h t -> q (h t)"), start=True, stop=True)
                    mm.then_inc(e["smm"], 1)

                def states_in(ci, b, p, i):
                    k = ci * B + b
                    eng.wait_ge(e["silu"], done(k))
                    eng.wait_ge(e["bt"], done(k - 1))
                    eng.wait_ge(e["crt"], done(k - 1))
                    eng.wait_ge(e["cm"], done(k - 1))
                    for f in range(3):
                        mm = eng.matmul(b_bc[0:L, 0:EP], vt[:, p, f, :], wbc[:, f, :], start=(f == 0), stop=(f == 2))
                    mm.then_inc(e["bcmm"], 1)
                    eng.wait_ge(e["gyt"], done(k - 2))
                    for f in range(3):
                        mm = eng.transpose(b_u[0:L, 128 * f:128 * f + 128], vt[:, p, f, :], ident[:, :])
                    mm.then_inc(e["ut"], 1)

                def scan(ci, b, p, i):
                    k = ci * B + b
                    sv = image(state, b).rearrange("q o n -> q (o n)")
                    eng.wait_ge(e["crt"], done(k))
                    eng.wait_ge(e["st"], done(k - 1))
                    eng.wait_ge(e["gsum"], done(k - 1))
                    eng.matmul(b_y[0:L, 0:DI], crt[:, p, :], sv, start=True, stop=False)
                    eng.wait_ge(e["m"], done(k))
                    eng.wait_ge(e["u"], done(k))
                    for h in range(H):
                        mm = eng.matmul(b_y[0:L, P * h:P * h + P], m[:, p, h, :], u[:, p, P * h:P * h + P],
                                        start=False, stop=(h == H - 1))
                    mm.then_inc(e["ymm"], 1)
                    eng.wait_ge(e["br"], done(k))
                    eng.wait_ge(e["tb"], done(k))
                    eng.wait_ge(e["x2"], done(k - 1))
                    eng.matmul(b_st[0:EP, 0:DI], br[:, p, :], u[:, p, :], start=True, stop=False)
                    eng.matmul(b_st[0:EP, 0:DI], tb[:, p, :], sv, start=False, stop=True).then_inc(e["stmm"], 1)

                def gated(ci, b, p, i):
                    k = ci * B + b
                    eng.wait_ge(e["gy"], done(k))
                    if not (isinstance(ci, int) and ci == CH - 1 and isinstance(b, int) and b == B - 1):
                        eng.wait_ge(e["u"], done(k + 1))
                    for f in range(3):
                        mm = eng.transpose(b_u[:, L * f:L * f + L], gy[:, p, 128 * f:128 * f + 128], ident[0:L, 0:L])
                    mm.then_inc(e["gyt_mm"], 1)

                def kernel_rows(ci, j, q):
                    for a in range(2):
                        r0, r1 = GROUPS[2 * q + a]
                        group = KG * ci + 4 * j + 2 * q + a
                        eng.wait_ge(s_ring, group + 1)
                        eng.wait_ge(e["m"], done((ci - 1) * B + 2 * j + q - 1))
                        eng.wait_ge(s_kern, AHEAD + group - 1)
                        for r in range(r0, r1):
                            mm = eng.transpose(b_s[a][0:L, SEQ * (r - r0):SEQ * (r - r0) + SEQ],
                                               ring[:, r, PAD + 2:PAD + 2 + L], ident[0:SEQ, 0:SEQ])
                        mm.then_inc(s_kt, 1)

                def boundary(ci):
                    eng.wait_ge(s_kern, AHEAD + KG * ci + KG)
                    for n, src in enumerate((unit_rows[:, 0, :], unit_rows[:, 1, :], z[:, PAD + 2:PAD + 2 + L],
                                             ring[:, STEPS - 1, PAD + 2:PAD + 2 + L])):
                        mm = eng.transpose(b_s0[0:L, SEQ * n:SEQ * n + SEQ], src, ident[0:SEQ, 0:SEQ])
                    mm.then_inc(s_ct, 1)
                    eng.wait_ge(s_pr, ci + 1)
                    for fr in range(2):
                        mm = eng.matmul(b_s1[0:EP, 0:2 * B], spread[:, fr, :], phi_rhs[:, fr, :, :].rearrange("s j b -> s (j b)"),
                                        start=(fr == 0), stop=(fr == 1))
                    mm.then_inc(s_pm, 1)

                mixer_turns(eng, [(1, turned), (0, values), (2, project), (0, gates), (1, scores), (0, states_in),
                                  (1, scan), (1, gated), (None, kernel_rows)], boundary)


def turns(eng, n, stages, peeled=0):
    deepest = max(lag for lag, _ in stages)
    head = deepest + deepest % 2 + peeled

    def slot(s):
        for lag, f in stages:
            if 0 <= s - lag < n:
                f(s - lag, (s - lag) % 2, (s - lag) // 2)

    for s in range(head):
        slot(s)
    with eng.Fori(head // 2, n // 2) as i:
        for q in range(2):
            for lag, f in stages:
                f(2 * i + (q - lag), (q - lag) % 2, i + (q - lag) // 2)
    for s in range(n, n + deepest):
        slot(s)


class Route:

    def __init__(self, sp, ctx):
        self.mean = sp.sb(ctx, "rt_mean", [L, NT])
        self.rstd = sp.sb(ctx, "rt_rstd", [L, NT])
        self.gap = sp.sb(ctx, "rt_gap", [L, NT])
        self.keep = sp.sb(ctx, "rt_keep", [L, 2, NT])
        self.slot = sp.sb(ctx, "rt_slot", [L, 2, NT])


def feed_forward(nc, sp, c, x2_rows, h_rows, h2_rows, slots, rt):
    NF = FF // 128
    with sp.phase() as ctx:
        def sb(name, shape, dt=F32):
            return sp.sb(ctx, "ff_" + name, shape, dt)

        def sem(name):
            return sp.sem("ff_" + name)

        ident = sb("ident", [128, 128])
        w1 = sb("w1", [K2, 2, FF])
        n2 = sb("n2", [K2, 2])
        w2 = sb("w2", [128, NF, D])
        b1 = sb("b1", [128, NF])
        b2 = sb("b2", [L, D])
        gate = sb("gate", [K2, 2, NE])
        before = sb("before", [L, L])
        ones = sb("ones", [L, L])
        valid = sb("valid", [L, NT])
        expert = sb("expert", [L, NE])
        rank = sb("rank", [L, NE])
        base = sb("base", [L, NE])
        half = sb("half", [L, GT4])
        x2 = sb("x2", [L, 2, GT4, D])
        h = sb("h", [L, 2, GT4, D])
        hx = sb("hx", [L, 2, GT4, D])
        ss = sb("ss", [L, 2, GT4])
        r = sb("r", [L, 2, GT4])
        xr = sb("xr", [L, 2, GT4, D])
        xt = sb("xt", [K2, 2, 2, GW])
        gt = sb("gt", [128, 2, NF, GW])
        h2 = sb("h2", [L, 2, GT4, D])
        st = sb("st", [L, 2, GT4, 6])
        mv = sb("mv", [L, 2, GT4, 2])
        rstd = sb("rstd", [L, 2, GT4])
        q = sb("q", [L, 2, GT4])
        x3 = sb("x3", [L, 2, GT4, D])
        x3t = sb("x3t", [K2, 2, 2, GW])
        z = sb("z", [L, 2, GT4, D])
        lg = sb("lg", [L, 2, GT4, NE])
        mask = sb("mask", [L, 2, 2, GT4, NE])
        both = sb("both", [L, 2, GT4, NE])
        work = sb("work", [L, GT4, NE])
        best = sb("best", [L, 4, GT4])
        run = sb("run", [L, GT4 + 1, NE])
        place = sb("place", [L, GT4, NE])
        small = sb("small", [L, 4, GT4])
        sidx = sb("sidx", [L, 2, 2, GT4], I32)
        bank = [sp.ps(ctx, f"ff_bank{i}", [128, 512]) for i in range(8)]
        s_const, s_w, s_mem = sem("const"), sem("w"), sem("mem")
        s_in = [sem("in0"), sem("in1")]
        s_store = [sem("store0"), sem("store1")]
        s_scat = [sem("scat0"), sem("scat1")]
        s_scale, s_norm, s_h2a = sem("scale_link"), sem("norm_link"), sem("h2_first")
        s_st, s_choose, s_both, s_place = sem("st_link"), sem("choose_link"), sem("both_link"), sem("place_link")
        names = ("ss", "r", "xr", "xt_mm", "xt", "up", "gelu", "down", "hx", "h2", "stats", "q", "x3", "x3t_mm", "x3t",
                 "z", "lmm", "lg", "both", "count", "sidx", "kept")
        e = {n: sem(n) for n in names}

        with nc.Block() as block:
            @block.sync
            def _(eng):
                start_counts(eng, *s_store, *e.values())
                for dst, name in ((ident, "ident"), (n2, "norm2"), (b1, "ff_b1"), (before, "before"), (ones, "ones"),
                                  (valid, "valid"), (expert, "expert")):
                    eng.dma_start(dst[:, :], c[name]).then_inc(s_const, 16)
                eng.dma_start(w1[:, :, :], c["ff_w1"].rearrange("(k p) n -> p k n", p=K2)).then_inc(s_const, 16)
                eng.dma_start(w2[:, :, :], c["ff_w2"].rearrange("(k p) n -> p k n", p=128)).then_inc(s_const, 16)
                eng.dma_start(gate[:, :, :], c["gate"].rearrange("(k p) n -> p k n", p=K2)).then_inc(s_const, 16)
                eng.dma_start(b2[:, :], c["ff_b2"].rearrange("(o d) -> o d", o=1).to_broadcast([L, D])).then_inc(s_const, 16)

                def load(g, p, i):
                    eng.wait_ge(e["xr"], done(g - 2))
                    eng.wait_ge(e["hx"], done(g - 2))
                    eng.dma_start(x2[:, p, :, :], row_tiles(x2_rows, g)).then_inc(s_in[p], 16)
                    eng.dma_start(h[:, p, :, :], row_tiles(h_rows, g)).then_inc(s_in[p], 16)

                def store(g, p, i):
                    eng.wait_ge(e["h2"], done(g))
                    eng.dma_start(row_tiles(h2_rows, g), h2[:, p, :, :]).then_inc(s_store[p], 16)

                turns(eng, NG, [(0, load), (2, store)])
                for p in range(2):
                    eng.wait_ge(s_store[p], AHEAD + 16 * (NG // 2))

            @block.gpsimd
            def _(eng):
                eng.memset(half[:, :], -0.5).then_inc(s_mem, 1)
                eng.memset(run[:, GT4, :], 0.0).then_inc(s_mem, 1)
                eng.wait_ge(s_mem, 2)
                eng.wait_ge(s_const, 16 * 11)

                def scale(g, p, i):
                    link = chain(eng, s_scale, 2 * g, settled=sp.settled)
                    eng.wait_ge(e["ss"], done(g))
                    eng.wait_ge(e["xr"], done(g - 2))
                    settle(eng, sp.settled)
                    link(eng.tensor_scalar(ss[:, p, :], ss[:, p, :], 1.0 / D, RMS_EPS, ALU.mult, ALU.add))
                    eng.tensor_tensor(r[:, p, :], ss[:, p, :], half[:, :], ALU.pow).then_inc(e["r"], 1)
                    eng.wait_ge(e["h2"], done(g - 2))
                    eng.wait_ge(s_in[p], 32 * i + 32)
                    settle(eng, sp.settled)
                    link(eng.tensor_tensor(hx[:, p, :, :], x2[:, p, :, :], h[:, p, :, :], ALU.add))
                    eng.tensor_tensor(hx[:, p, :, :], hx[:, p, :, :], b2[:, :].unsqueeze(1).to_broadcast([L, GT4, D]), ALU.add).then_inc(e["hx"], 1)

                def norm(g, p, i):
                    link = chain(eng, s_norm, 6 * g, settled=sp.settled)
                    var, rs, qq = mv[:, p, :, 1], rstd[:, p, :], q[:, p, :]
                    eng.wait_ge(e["stats"], done(g))
                    eng.wait_ge(e["z"], done(g - 2))
                    eng.wait_ge(e["kept"], done(g - 2))
                    settle(eng, sp.settled)
                    link(eng.tensor_scalar(qq, var, LN_EPS, None, ALU.add))
                    link(eng.tensor_tensor(rs, qq, half[:, :], ALU.pow))
                    link(eng.tensor_tensor(qq, rs, rs, ALU.mult))
                    link(eng.tensor_tensor(qq, qq, var, ALU.mult))
                    link(eng.tensor_scalar(qq, qq, 4.0, RMS_EPS, ALU.mult, ALU.add))
                    link(eng.tensor_tensor(qq, qq, half[:, :], ALU.pow))
                    eng.tensor_scalar(qq, qq, 2.0, None, ALU.mult).then_inc(e["q"], 1)

                def scatter(g, p, i):
                    eng.wait_ge(e["sidx"], done(g))
                    eng.wait_ge(e["z"], done(g))
                    settle(eng, sp.settled)
                    for k in range(2):
                        for j in range(GT4):
                            eng.indirect_dma_start(
                                out=slots[:, :], out_offset=IndirectOffsetOnAxis(ap=sidx[:, p, k, j:j + 1], axis=0),
                                in_=z[:, p, j, :], in_offset=None, bounds_check=NE * ES - 1, oob_is_err=False).then_inc(s_scat[p], 16)

                turns(eng, NG, [(0, scale), (1, norm), (2, scatter)])
                for p in range(2):
                    eng.wait_ge(s_scat[p], 128 * (NG // 2))

            @block.scalar
            def _(eng):
                def squares(g, p, i):
                    eng.wait_ge(s_in[p], 32 * i + 32)
                    eng.wait_ge(e["r"], done(g - 2))
                    eng.wait_ge(e["xt_mm"], done(g - 2))
                    for j in range(GT4):
                        ins = eng.activation(xr[:, p, j, :], x2[:, p, j, :], ACT.Square, accum_out=ss[:, p, j:j + 1])
                    ins.then_inc(e["ss"], 1)

                def scaled(g, p, i):
                    eng.wait_ge(e["r"], done(g))
                    for j in range(GT4):
                        ins = eng.activation(xr[:, p, j, :], x2[:, p, j, :], ACT.Copy, scale=r[:, p, j:j + 1])
                    ins.then_inc(e["xr"], 1)

                def kept(g, p, i):
                    eng.wait_ge(e["xt_mm"], done(g))
                    eng.wait_ge(e["up"], AHEAD + NF * (g - 1))
                    for k in range(2):
                        ins = eng.activation(xt[:, p, k, :], bank[k][0:K2, 0:GW], ACT.Copy)
                    ins.then_inc(e["xt"], 1)

                def gelu(g, p, i):
                    eng.wait_ge(e["down"], done(2 * (g - 2) + 1))
                    for f in range(NF):
                        eng.wait_ge(e["up"], done(NF * g + f))
                        eng.activation(gt[:, p, f, :], bank[2 + f % 2][:, 0:GW], ACT.Gelu_apprx_tanh, bias=b1[:, f:f + 1]).then_inc(e["gelu"], 1)

                def zrow(g, p, i):
                    eng.wait_ge(e["q"], done(g))
                    eng.wait_ge(e["x3"], done(g))
                    eng.wait_ge(s_scat[p], 128 * i)
                    for j in range(GT4):
                        ins = eng.activation(z[:, p, j, :], x3[:, p, j, :], ACT.Copy, scale=q[:, p, j:j + 1])
                    ins.then_inc(e["z"], 1)

                eng.wait_ge(s_const, 16 * 11)
                turns(eng, NG, [(0, squares), (0, scaled), (0, kept), (0, gelu), (1, zrow)], peeled=2)

            @block.vector
            def _(eng):
                eng.wait_ge(s_const, 16 * 11)
                for k in range(2):
                    eng.tensor_scalar(w1[:, k, :], w1[:, k, :], n2[:, k:k + 1], None, ALU.mult).then_inc(s_w, 1)
                eng.tensor_scalar(rank[:, :], expert[:, :], -1.0, float(NE), ALU.mult, ALU.add).then_inc(s_w, 1)
                eng.tensor_scalar(base[:, :], expert[:, :], float(ES), None, ALU.mult).then_inc(s_w, 1)
                eng.wait_ge(s_w, 4)
                eng.wait_ge(s_mem, 2)

                def total(g, p, i):
                    eng.wait_ge(e["hx"], done(g))
                    eng.wait_ge(s_store[p], AHEAD + 16 * i)
                    for j in range(2):
                        eng.wait_ge(e["down"], done(2 * g + j))
                        ins = eng.tensor_tensor(h2[:, p, 2 * j:2 * j + 2, :], bank[4 + j][0:L, 0:2 * D].rearrange("t (j d) -> t j d", j=2),
                                                hx[:, p, 2 * j:2 * j + 2, :], ALU.add)
                        if j:
                            ins.then_inc(e["h2"], 1)
                        else:
                            ins.then_inc(s_h2a, 1)
                    eng.wait_ge(s_h2a, g + 1)
                    eng.wait_ge(e["h2"], done(g))
                    eng.wait_ge(e["q"], done(g - 2))
                    link = chain(eng, s_st, GT4 * g, settled=sp.settled)
                    for j in range(GT4):
                        link(eng.bn_stats(st[:, p, j, :], h2[:, p, j, :]))
                    for j in range(GT4):
                        ins = eng.bn_aggr(mv[:, p, j, :], st[:, p, j, :])
                    ins.then_inc(e["stats"], 1)

                def centred(g, p, i):
                    eng.wait_ge(e["q"], done(g))
                    eng.wait_ge(e["x3t_mm"], done(g - 2))
                    eng.wait_ge(e["z"], done(g - 2))
                    for j in range(GT4):
                        ins = eng.tensor_scalar(x3[:, p, j, :], h2[:, p, j, :], mv[:, p, j, 0:1], rstd[:, p, j:j + 1],
                                                ALU.subtract, ALU.mult)
                    ins.then_inc(e["x3"], 1)
                    at = bass.ds(g * GT4, GT4)
                    eng.tensor_copy(rt.mean[:, at], mv[:, p, :, 0])
                    eng.tensor_copy(rt.rstd[:, at], rstd[:, p, :]).then_inc(e["kept"], 1)
                    eng.wait_ge(e["x3t_mm"], done(g))
                    eng.wait_ge(e["lmm"], done(g - 2))
                    for k in range(2):
                        ins = eng.tensor_copy(x3t[:, p, k, :], bank[k][0:K2, 0:GW])
                    ins.then_inc(e["x3t"], 1)

                def choose(g, p, i):
                    link = chain(eng, s_choose, 13 * g)
                    eng.wait_ge(e["lmm"], done(g))
                    eng.wait_ge(e["count"], done(g - 2))
                    link(eng.tensor_copy(lg[:, p, :, :], bank[6][0:L, 0:GT4 * NE].rearrange("t (j e) -> t j e", j=GT4)))
                    ll = lg[:, p, :, :]
                    rk = rank[:, :].unsqueeze(1).to_broadcast([L, GT4, NE])

                    def wide(v):
                        return v.unsqueeze(2).to_broadcast([L, GT4, NE])

                    for k in range(2):
                        mk = mask[:, p, k, :, :]
                        link(eng.tensor_reduce(best[:, k, :], ll, AX.X, ALU.max))
                        link(eng.tensor_tensor(work[:, :, :], ll, wide(best[:, k, :]), ALU.is_equal))
                        link(eng.tensor_tensor(work[:, :, :], work[:, :, :], rk, ALU.mult))
                        link(eng.tensor_reduce(best[:, 2 + k, :], work[:, :, :], AX.X, ALU.max))
                        link(eng.tensor_tensor(mk, work[:, :, :], wide(best[:, 2 + k, :]), ALU.is_equal))
                        if k == 0:
                            link(eng.scalar_tensor_tensor(ll, mk, -1e30, ll, ALU.mult, ALU.add))
                    at = bass.ds(g * GT4, GT4)
                    link(eng.tensor_tensor(rt.gap[:, at], best[:, 1, :], best[:, 0, :], ALU.subtract))
                    eng.tensor_tensor(both[:, p, :, :], mask[:, p, 0, :, :], mask[:, p, 1, :, :], ALU.add).then_inc(s_both, 1)
                    eng.wait_ge(s_both, g + 1)
                    eng.tensor_tensor(both[:, p, :, :], both[:, p, :, :], wide(valid[:, at]), ALU.mult).then_inc(e["both"], 1)

                def places(g, p, i):
                    link = chain(eng, s_place, (1 + GT4 + 1 + 2 * 8) * g)
                    eng.wait_ge(e["count"], done(g))
                    eng.wait_ge(s_scat[p], 128 * i)
                    at = bass.ds(g * GT4, GT4)
                    link(eng.tensor_copy(run[:, 0, :], run[:, GT4, :]))
                    for j in range(GT4):
                        link(eng.tensor_tensor(run[:, j + 1, :], run[:, j, :], bank[7][0:L, 32 + NE * j:32 + NE * j + NE], ALU.add))
                    link(eng.tensor_tensor(place[:, :, :], run[:, 0:GT4, :],
                                           bank[7][0:L, 0:GT4 * NE].rearrange("t (j e) -> t j e", j=GT4), ALU.add))
                    bs = base[:, :].unsqueeze(1).to_broadcast([L, GT4, NE])
                    for k in range(2):
                        mk = mask[:, p, k, :, :]
                        pk, ek, kp, sl = (small[:, n, :] for n in range(4))
                        link(eng.tensor_tensor(work[:, :, :], mk, place[:, :, :], ALU.mult))
                        link(eng.tensor_reduce(pk, work[:, :, :], AX.X, ALU.add))
                        link(eng.tensor_tensor(work[:, :, :], mk, bs, ALU.mult))
                        link(eng.tensor_reduce(ek, work[:, :, :], AX.X, ALU.add))
                        link(eng.scalar_tensor_tensor(rt.keep[:, k, at], pk, float(CAP), valid[:, at], ALU.is_lt, ALU.mult))
                        link(eng.tensor_tensor(sl, pk, ek, ALU.add))
                        link(eng.tensor_tensor(rt.slot[:, k, at], sl, rt.keep[:, k, at], ALU.mult))
                        link(eng.scalar_tensor_tensor(kp, sl, -65536.0, rt.keep[:, k, at], ALU.add, ALU.mult))
                        ins = eng.tensor_scalar(sidx[:, p, k, :], kp, 65536.0, None, ALU.add)
                    ins.then_inc(e["sidx"], 1)

                turns(eng, NG, [(0, total), (0, centred), (0, choose), (0, places)], peeled=2)

            @block.tensor
            def _(eng):
                eng.wait_ge(s_const, 16 * 11)
                eng.wait_ge(s_w, 4)

                def transposed(src, dst):
                    for k in range(2):
                        for j in range(GT4):
                            ins = eng.transpose(dst[k][0:K2, L * j:L * j + L], src[:, j, K2 * k:K2 * k + K2], ident[0:L, 0:L])
                    return ins

                def up(g, p, i):
                    eng.wait_ge(e["xr"], done(g))
                    eng.wait_ge(e["x3t"], done(g - 1))
                    transposed(xr[:, p, :, :], bank).then_inc(e["xt_mm"], 1)
                    eng.wait_ge(e["xt"], done(g))
                    for f in range(NF):
                        eng.wait_ge(e["gelu"], done(NF * g + f - 2))
                        for k in range(2):
                            ins = eng.matmul(bank[2 + f % 2][:, 0:GW], w1[:, k, 128 * f:128 * f + 128], xt[:, p, k, :],
                                             start=(k == 0), stop=(k == 1))
                        ins.then_inc(e["up"], 1)

                def down(g, p, i):
                    eng.wait_ge(e["gelu"], done(NF * g + NF - 1))
                    eng.wait_ge(e["h2"], done(g - 1))
                    for j in range(GT4):
                        o = bank[4 + j // 2][0:L, D * (j % 2):D * (j % 2) + D]
                        for f in range(NF):
                            ins = eng.matmul(o, gt[:, p, f, L * j:L * j + L], w2[:, f, :], start=(f == 0), stop=(f == NF - 1))
                        if j % 2:
                            ins.then_inc(e["down"], 1)

                def logits(g, p, i):
                    eng.wait_ge(e["x3"], done(g))
                    transposed(x3[:, p, :, :], bank).then_inc(e["x3t_mm"], 1)
                    eng.wait_ge(e["x3t"], done(g))
                    eng.wait_ge(e["both"], done(g - 1))
                    for j in range(GT4):
                        for k in range(2):
                            ins = eng.matmul(bank[6][0:L, NE * j:NE * j + NE], x3t[:, p, k, L * j:L * j + L], gate[:, k, :],
                                             start=(k == 0), stop=(k == 1))
                    ins.then_inc(e["lmm"], 1)

                def counts(g, p, i):
                    eng.wait_ge(e["both"], done(g))
                    eng.wait_ge(e["sidx"], done(g - 1))
                    rhs = both[:, p, :, :].rearrange("t j e -> t (j e)")
                    eng.matmul(bank[7][0:L, 0:GT4 * NE], before[:, :], rhs, start=True, stop=True)
                    eng.matmul(bank[7][0:L, 32:32 + GT4 * NE], ones[:, :], rhs, start=True, stop=True).then_inc(e["count"], 1)

                turns(eng, NG, [(0, up), (0, down), (0, logits), (0, counts)])


def expert_turns(eng, stages, between=None):
    per = ES // SG
    half = per // 2

    def expert(x, px, first=False):
        for q in range(2):
            for lag, f in stages:
                if q >= lag:
                    f(x * per + (q - lag), (q - lag) % 2, x * half, x, px)
                elif not first:
                    f(x * per + (q - lag), (q - lag) % 2, x * half - 1, x - 1, 1 - px)
        with eng.Fori(1, half) as i:
            for q in range(2):
                for lag, f in stages:
                    f(x * per + (2 * i + (q - lag)), (q - lag) % 2, x * half + (i + (q - lag) // 2), x, px)

    between = between or (lambda x, px, turn: None)
    expert(0, 0, first=True)
    between(1, 1, 0)
    with eng.Fori(0, (NE - 2) // 2) as y:
        expert(2 * y + 1, 1)
        between(2 * y + 2, 0, y + 1)
        expert(2 * y + 2, 0)
        between(2 * y + 3, 1, y + 1)
    expert(NE - 1, 1)
    for q in range(2):
        for lag, f in stages:
            if lag > q:
                f(NE * per + q - lag, (q - lag) % 2, NE * half - 1, NE - 1, 1)


def experts(nc, sp, c, slots, answers):
    NJ = SG // 128
    NH = HID // 128
    per = ES // SG
    with sp.phase() as ctx:
        def sb(name, shape, dt=F32):
            return sp.sb(ctx, "ex_" + name, shape, dt)

        def sem(name):
            return sp.sem("ex_" + name)

        ident = sb("ident", [128, 128])
        norm = sb("norm", [K2, NE, 2])
        w13 = sb("w13", [K2, 2, 2, 2 * HID])
        w2 = sb("w2", [128, 2, NH, D])
        z = sb("z", [128, 2, NJ, D])
        zt = sb("zt", [K2, 2, 2, SG])
        sil = sb("sil", [128, 2, SG])
        ht = sb("ht", [128, 2, NH, SG])
        ans = sb("ans", [128, 2, NJ, D])
        bank = [sp.ps(ctx, f"ex_bank{i}", [128, 512]) for i in range(8)]
        s_const = sem("const")
        s_in = [sem("in0"), sem("in1")]
        s_win = [sem("w_in0"), sem("w_in1")]
        s_store = [sem("store0"), sem("store1")]
        s_half = sem("ans_first")
        names = ("w", "z_mm", "zt0", "zt1", "gu", "silu", "h", "down", "ans")
        e = {n: sem(n) for n in names}

        def group(buf, u):
            return buf[bass.ds(u * SG, SG), :].rearrange("(p j) d -> p j d", j=NJ)

        with nc.Block() as block:
            @block.sync
            def _(eng):
                start_counts(eng, *s_store, *e.values())
                eng.dma_start(ident[:, :], c["ident"]).then_inc(s_const, 16)
                eng.dma_start(norm[:, :, :], c["norm_e"]).then_inc(s_const, 16)

                def load(u, p, i):
                    eng.wait_ge(e["z_mm"], done(u - 2))
                    eng.dma_start(z[:, p, :, :], group(slots, u)).then_inc(s_in[p], 16)

                def store(u, p, i):
                    eng.wait_ge(e["ans"], done(2 * u + 1))
                    eng.dma_start(group(answers, u), ans[:, p, :, :]).then_inc(s_store[p], 16)

                turns(eng, NE * per, [(0, load), (3, store)])
                for p in range(2):
                    eng.wait_ge(s_store[p], AHEAD + 16 * NE * per // 2)

            @block.gpsimd
            def _(eng):
                def weights(x, px):
                    eng.dma_start(w13[:, px, :, :], c["w13"][bass.ds(x, 1)].rearrange("o (k p) n -> p (o k) n", p=K2)).then_inc(s_win[px], 16)
                    eng.dma_start(w2[:, px, :, :], c["w2"][bass.ds(x, 1)].rearrange("o (k p) n -> p (o k) n", p=128)).then_inc(s_win[px], 16)

                weights(0, 0)
                weights(1, 1)
                with eng.Fori(0, (NE - 2) // 2) as y:
                    for px in range(2):
                        eng.wait_ge(e["down"], done(2 * per * (2 * y + px + 1) - 1))
                        settle(eng, sp.settled)
                        weights(2 * y + px + 2, px)

            @block.scalar
            def _(eng):
                def kept(u, p, i, x, px):
                    eng.wait_ge(e["z_mm"], done(u))
                    eng.wait_ge(e["gu"], AHEAD + NH * (u - 1))
                    eng.activation(zt[:, p, 0, :], bank[0][0:K2, :], ACT.Copy).then_inc(e["zt0"], 1)

                def silu(u, p, i, x, px):
                    for f in range(NH):
                        eng.wait_ge(e["gu"], done(NH * u + f))
                        eng.wait_ge(e["h"], done(NH * u + f - 2))
                        eng.activation(sil[:, f % 2, :], bank[2 + 2 * (f % 2)][:, :], ACT.Silu).then_inc(e["silu"], 1)

                expert_turns(eng, [(0, kept), (1, silu)])

            @block.vector
            def _(eng):
                def scaled(x, px, turn):
                    eng.wait_ge(s_win[px], 32 * turn + 32)
                    for k in range(2):
                        ins = eng.tensor_scalar(w13[:, px, k, :], w13[:, px, k, :],
                                                norm[:, bass.ds(x, 1), k:k + 1].rearrange("p o s -> p (o s)"), None, ALU.mult)
                    ins.then_inc(e["w"], 1)

                def kept(u, p, i, x, px):
                    eng.wait_ge(e["z_mm"], done(u))
                    eng.wait_ge(e["gu"], AHEAD + NH * (u - 1))
                    eng.tensor_copy(zt[:, p, 1, :], bank[1][0:K2, :]).then_inc(e["zt1"], 1)

                def product(u, p, i, x, px):
                    eng.wait_ge(e["down"], AHEAD + 2 * (u - 1))
                    for f in range(NH):
                        eng.wait_ge(e["silu"], done(NH * u + f))
                        eng.tensor_tensor(ht[:, p, f, :], sil[:, f % 2, :], bank[3 + 2 * (f % 2)][:, :], ALU.mult).then_inc(e["h"], 1)

                def answer(u, p, i, x, px):
                    eng.wait_ge(s_store[p], AHEAD + 16 * i)
                    for j in range(2):
                        eng.wait_ge(e["down"], done(2 * u + j))
                        eng.tensor_copy(ans[:, p, 2 * j:2 * j + 2, :],
                                        bank[6 + j][:, 0:2 * D].rearrange("t (j d) -> t j d", j=2)).then_inc(e["ans"], 1)

                eng.wait_ge(s_const, 32)
                scaled(0, 0, 0)
                expert_turns(eng, [(0, kept), (1, product), (2, answer)], scaled)

            @block.tensor
            def _(eng):
                def turned(u, p, i, x, px):
                    eng.wait_ge(s_in[p], 16 * i + 16)
                    eng.wait_ge(e["zt0"], done(u - 1))
                    eng.wait_ge(e["zt1"], done(u - 1))
                    for k in range(2):
                        for j in range(NJ):
                            ins = eng.transpose(bank[k][0:K2, 128 * j:128 * j + 128], z[:, p, j, K2 * k:K2 * k + K2], ident[:, :])
                    ins.then_inc(e["z_mm"], 1)

                def up(u, p, i, x, px):
                    eng.wait_ge(e["zt0"], done(u))
                    eng.wait_ge(e["zt1"], done(u))
                    eng.wait_ge(e["w"], done(x))
                    for f in range(NH):
                        eng.wait_ge(e["h"], done(NH * u + f - 2))
                        for v in range(2):
                            for k in range(2):
                                ins = eng.matmul(bank[2 + 2 * (f % 2) + v][:, :], w13[:, px, k, HID * v + 128 * f:HID * v + 128 * f + 128],
                                                 zt[:, p, k, :], start=(k == 0), stop=(k == 1))
                        ins.then_inc(e["gu"], 1)

                def down(u, p, i, x, px):
                    eng.wait_ge(e["h"], done(NH * u + NH - 1))
                    for j in range(NJ):
                        if j % 2 == 0:
                            eng.wait_ge(e["ans"], done(2 * (u - 1) + j // 2))
                        o = bank[6 + j // 2][:, D * (j % 2):D * (j % 2) + D]
                        for f in range(NH):
                            ins = eng.matmul(o, ht[:, p, f, 128 * j:128 * j + 128], w2[:, px, f, :], start=(f == 0), stop=(f == NH - 1))
                        if j % 2:
                            ins.then_inc(e["down"], 1)

                eng.wait_ge(s_const, 32)
                expert_turns(eng, [(0, turned), (1, up), (2, down)])


def combine(nc, sp, h2_rows, answers, out, rt):
    with sp.phase() as ctx:
        def sb(name, shape, dt=F32):
            return sp.sb(ctx, "cb_" + name, shape, dt)

        def sem(name):
            return sp.sem("cb_" + name)

        h2 = sb("h2", [L, 2, GT4, D])
        f = sb("f", [L, 2, 2, GT4, D])
        o = sb("o", [L, 2, GT4, D])
        idx = sb("idx", [L, 2, 2, GT4], I32)
        e2 = sb("e2", [L, NT])
        w = sb("w", [L, 2, NT])
        alpha = sb("alpha", [L, NT])
        beta = sb("beta", [L, NT])
        s_in = [sem("in0"), sem("in1")]
        s_f = [sem("f0"), sem("f1")]
        s_store = [sem("store0"), sem("store1")]
        s_exp, s_prep, s_acc = sem("exp"), sem("prep"), sem("acc")
        e = {n: sem(n) for n in ("idx", "o")}

        with nc.Block() as block:
            @block.sync
            def _(eng):
                start_counts(eng, *s_store, *e.values())

                def load(g, p, i):
                    eng.wait_ge(e["o"], done(g - 2))
                    eng.dma_start(h2[:, p, :, :], row_tiles(h2_rows, g)).then_inc(s_in[p], 16)

                def store(g, p, i):
                    eng.wait_ge(e["o"], done(g))
                    eng.dma_start(row_tiles(out, g), o[:, p, :, :]).then_inc(s_store[p], 16)

                turns(eng, NG, [(0, load), (2, store)])
                for p in range(2):
                    eng.wait_ge(s_store[p], AHEAD + 16 * (NG // 2))

            @block.gpsimd
            def _(eng):
                def gather(g, p, i):
                    eng.wait_ge(e["idx"], done(g))
                    eng.wait_ge(e["o"], done(g - 2))
                    settle(eng, sp.settled)
                    for k in range(2):
                        for j in range(GT4):
                            eng.indirect_dma_start(out=f[:, p, k, j, :], out_offset=None, in_=answers[:, :],
                                                   in_offset=IndirectOffsetOnAxis(ap=idx[:, p, k, j:j + 1], axis=0)).then_inc(s_f[p], 16)

                turns(eng, NG, [(0, gather)])

            @block.scalar
            def _(eng):
                eng.activation(e2[:, :], rt.gap[:, :], ACT.Exp).then_inc(s_exp, 1)

            @block.vector
            def _(eng):
                def index(g, p, i):
                    eng.wait_ge(s_f[p], 128 * i)
                    eng.tensor_copy(idx[:, p, :, :], rt.slot[:, :, bass.ds(g * GT4, GT4)]).then_inc(e["idx"], 1)

                def summed(g, p, i):
                    eng.wait_ge(s_in[p], 16 * i + 16)
                    eng.wait_ge(s_store[p], AHEAD + 16 * i)
                    for j in range(GT4):
                        at = bass.ds(g * GT4 + j, 1)
                        ins = eng.tensor_scalar(o[:, p, j, :], h2[:, p, j, :], alpha[:, at], beta[:, at], ALU.mult, ALU.add)
                    ins.then_inc(s_acc, 1)
                    eng.wait_ge(s_acc, 2 * g + 1)
                    eng.wait_ge(s_f[p], 128 * i + 128)
                    for k in range(2):
                        if k:
                            eng.wait_ge(s_acc, 2 * g + 2)
                        for j in range(GT4):
                            ins = eng.scalar_tensor_tensor(o[:, p, j, :], f[:, p, k, j, :], w[:, k, bass.ds(g * GT4 + j, 1)],
                                                           o[:, p, j, :], ALU.mult, ALU.add)
                        ins.then_inc(e["o"] if k else s_acc, 1)

                link = chain(eng, s_prep, 0)
                eng.wait_ge(s_exp, 1)
                link(eng.tensor_scalar(alpha[:, :], e2[:, :], 1.0, None, ALU.add))
                link(eng.reciprocal(w[:, 0, :], alpha[:, :]))
                link(eng.tensor_tensor(w[:, 1, :], e2[:, :], w[:, 0, :], ALU.mult))
                link(eng.tensor_tensor(w[:, :, :], w[:, :, :], rt.keep[:, :, :], ALU.mult))
                link(eng.tensor_tensor(alpha[:, :], w[:, 0, :], w[:, 1, :], ALU.add))
                link(eng.tensor_tensor(alpha[:, :], alpha[:, :], rt.rstd[:, :], ALU.mult))
                link(eng.scalar_tensor_tensor(beta[:, :], rt.mean[:, :], -1.0, alpha[:, :], ALU.mult, ALU.mult))
                link(eng.tensor_scalar(alpha[:, :], alpha[:, :], 1.0, None, ALU.add))
                turns(eng, NG, [(0, index), (1, summed)], peeled=2)


def program(nc, a, out, upto=9, keep="Internal"):
    with ExitStack() as outer:
        sp = Space(nc, outer)

        def rows(name, n, w=D):
            return nc.dram_tensor(name, (n, w), F32, kind=keep).ap()

        h_rows, x_rows = rows("h_rows", N), rows("x_rows", N)
        x2_rows, h2_rows = rows("x2_rows", N), rows("h2_rows", N)
        xt = nc.dram_tensor("x_t", (K2, 2, N), F32, kind=keep).ap()
        params = rows("params", 2 * H, N)
        slots, answers = rows("slots", NE * ES), rows("answers", NE * ES)
        tokenizer(nc, sp, a["blocks"], a["tok_w"], a["tok_b"], a["cls"], a["pos"], a["txt"], h_rows, slots)
        if upto < 2:
            return
        normalise(nc, sp, a, h_rows, a["w_in"], a["norm1"], x_rows, xt, params)
        if upto < 3:
            return
        mixer(nc, sp, a, x_rows, xt, params, x2_rows)
        if upto < 4:
            return
        with ExitStack() as ctx:
            route = Route(sp, ctx)
            feed_forward(nc, sp, a, x2_rows, h_rows, h2_rows, slots, route)
            if upto < 5:
                return
            experts(nc, sp, a, slots, answers)
            if upto < 6:
                return
            combine(nc, sp, h2_rows, answers, out, route)


def constants():
    import numpy as np
    ident = np.eye(128, dtype=np.float32)
    rows = np.arange(EP)
    head_of = rows // (2 * NS)
    block_mask = (head_of[:, None] == (np.arange(DI) // P)[None, :]).astype(np.float32)
    step_mask = ((head_of[:, None] == head_of[None, :]) & (rows[:, None] % NS == rows[None, :] % NS)).astype(np.float32)
    head_col = (np.arange(H * NS)[:, None] // NS == np.arange(H)[None, :]).astype(np.float32)
    seq = np.arange(SEQ)
    comp = rows // NS % 2
    spread = np.stack([((seq // B)[:, None] == head_of[None, :]) & (comp == j)[None, :] for j in range(2)], 1).astype(np.float32)
    image_mask = (seq[:, None] % B == np.arange(B)[None, :]).astype(np.float32)
    before = (np.arange(L)[:, None] < np.arange(L)[None, :]).astype(np.float32)
    ones = np.ones((L, L), np.float32)
    valid = np.ones((L, CH), np.float32)
    valid[T - (CH - 1) * L:, CH - 1] = 0
    valid = np.tile(valid, (1, B))
    expert = np.tile(np.arange(NE, dtype=np.float32), (L, 1))
    return {"ident": ident, "block_mask": block_mask, "step_mask": step_mask, "head_col": head_col,
            "spread": spread, "image_mask": image_mask, "before": before, "ones": ones,
            "valid": valid, "expert": expert}


def lay_out(inputs):
    import numpy as np
    a = {k: np.asarray(v) for k, v in inputs.items()}
    w_in, w_bc = a["L0_attn_w_in"], a["L0_attn_w_bc"]
    out = {
        "blocks": a["x"].reshape(B, 3, BLK, 8, BLK, 8).transpose(1, 3, 5, 0, 2, 4).reshape(D, B, BLK * BLK),
        "txt": a["txt"],
        "tok_w": a["L0_tok_w"].reshape(D, 3, 2, 8, 2, 8).transpose(1, 3, 5, 2, 4, 0).reshape(D, 2, 2, D),
        "tok_b": a["L0_tok_b"],
        "cls": a["L0_tok_cls_token"].reshape(1, D),
        "pos": a["L0_tok_pos_embedding"].reshape(1 + NPATCH, D),
        "norm1": a["L0_attn_norm1_w"].reshape(2, K2).T,
        "w_in": np.concatenate([w_in[:, :2 * DI], w_in[:, 2 * DI::2], w_in[:, 2 * DI + 1::2]], axis=1),
        "conv_w": a["L0_attn_conv_w"].reshape(3, 128, 4).transpose(1, 0, 2),
        "w_bc": w_bc.reshape(DI, H, 2, NS).transpose(0, 2, 1, 3).reshape(DI, EP),
        "d_skip": a["L0_attn_D_skip"],
        "w_out": a["L0_attn_w_out"],
        "norm2": a["L0_attn_norm2_w"].reshape(2, K2).T,
        "ff_w1": a["L0_attn_ff_w1"], "ff_b1": a["L0_attn_ff_b1"].reshape(FF // 128, 128).T,
        "ff_w2": a["L0_attn_ff_w2"], "ff_b2": a["L0_attn_ff_b2"],
        "gate": a["L0_ffn_gate_w"].transpose(1, 0),
        "w13": a["L0_ffn_w13"].transpose(0, 2, 1),
        "w2": a["L0_ffn_w2"].transpose(0, 2, 1),
        "norm_e": a["L0_ffn_norm_w"].reshape(NE, 2, K2).transpose(2, 0, 1),
    }
    out.update(constants())
    return {k: np.ascontiguousarray(v) for k, v in out.items()}


def kernel(**inputs):
    import concourse.bacc as bacc
    from concourse import mybir as mb
    from concourse.bass_utils import run_bass_kernel_spmd as run

    nc = bacc.Bacc("TRN2", target_bir_lowering=False, num_devices=1)
    arrays = lay_out(inputs)
    aps = {k: nc.dram_tensor(f"in_{k}", v.shape, mb.dt.from_np(v.dtype), kind="ExternalInput").ap()
           for k, v in arrays.items()}
    out = nc.dram_tensor("out_rows", (N, D), F32, kind="ExternalOutput").ap()
    program(nc, aps, out)
    r = run(nc, [{f"in_{k}": v for k, v in arrays.items()}], core_ids=[0])
    return r.results[0]["out_rows"].reshape(B, TP, D)[:, :T]
```

```python
from contextlib import ExitStack

import concourse.bass as bass
from concourse import mybir
from concourse.bass import IndirectOffsetOnAxis

F32 = mybir.dt.float32
I32 = mybir.dt.int32
F32R = mybir.dt.float32r
ALU = mybir.AluOpType
ACT = mybir.ActivationFunctionType
AX = mybir.AxisListType

B = 16
D = 192
K2 = D // 2
GRID = 27
BLK = 28
NPATCH = GRID * GRID
NTXT = 77
T = 1 + NPATCH + NTXT
L = 120
CH = 7
TP = CH * L
NT = B * CH
N = B * TP
GT4 = 4
NG = NT // GT4
GW = GT4 * L
H = 6
P = 64
DI = H * P
NS = 8
SEQ = H * B
EP = H * 2 * NS
ROWS = 4
STEPS = 15
PAD = L - 1
KW = L + 2
FF = 768
NE = 8
HID = 512
CAP = -(-(2 * B * T * 5) // (4 * NE))
ES = 4096
SG = 512
LN_EPS = 1e-5
RMS_EPS = 1e-6
L2_EPS = 1e-12


AHEAD = 40


def done(n):
    return n + 1 + AHEAD


def start_counts(eng, *sems):
    for s in sems:
        eng.sem_inc(s, AHEAD)


def settle(eng, settled):
    eng.sem_inc(settled, 1)


def chain(eng, sem, before, settled=None):
    steps = [0]

    def link(ins):
        steps[0] += 1
        ins.then_inc(sem, 1)
        eng.wait_ge(sem, before + steps[0])
        if settled:
            settle(eng, settled)

    return link


def turns(eng, n, stages, peeled=0):
    deepest = max(lag for lag, _ in stages)
    head = deepest + deepest % 2 + peeled

    def slot(s):
        for lag, f in stages:
            if 0 <= s - lag < n:
                f(s - lag, (s - lag) % 2, (s - lag) // 2)

    for s in range(head):
        slot(s)
    with eng.Fori(head // 2, n // 2) as i:
        for q in range(2):
            for lag, f in stages:
                f(2 * i + (q - lag), (q - lag) % 2, i + (q - lag) // 2)
    for s in range(n, n + deepest):
        slot(s)


PARTS = ((0, 1), (1, 0), (0, 0))


def rest(eng, to, src, head):
    return eng.tensor_tensor(to, src, head.bitcast(F32), ALU.subtract)


class Space:

    def __init__(self, nc, outer):
        self.nc, self.outer = nc, outer
        self.settled = self.sem("settled")

    def phase(self):
        return ExitStack()

    def sb(self, ctx, name, shape, dt=F32):
        return ctx.enter_context(self.nc.sbuf_tensor(name, shape, dt))

    def ps(self, ctx, name, shape, dt=F32):
        return ctx.enter_context(self.nc.psum_tensor(name, shape, dt))

    def sem(self, name):
        return self.outer.enter_context(self.nc.semaphore(name))


def row_tiles(buf, g):
    return buf[bass.ds(g * GW, GW), :].rearrange("(j p) d -> p j d", p=L)


def tokenizer(nc, sp, blocks, tok_w, tok_b, cls, pos, txt, h_rows, slots):
    with sp.phase() as ctx:
        tiles = -(-GRID // ROWS)
        rows_of = [min(ROWS, GRID - g * ROWS) for g in range(tiles)]
        wide = [r * BLK - 1 for r in rows_of]
        tiles_with = [sum(r < n for n in rows_of) for r in range(ROWS)]

        def patch_rows(rows, r):
            return rows.rearrange("(g c) d -> g c d", c=GRID)[r:GRID:ROWS].rearrange("g c d -> c g d")

        main = sp.sb(ctx, "tk_main", [128, 2, BLK * BLK])
        rest = sp.sb(ctx, "tk_rest", [128, 2, BLK * BLK])
        w_main = sp.sb(ctx, "tk_w_main", [128, 4, D])
        w_rest = sp.sb(ctx, "tk_w_rest", [128, 2, D])
        bias = sp.sb(ctx, "tk_bias", [128, D])
        posb = sp.sb(ctx, "tk_posb", [ROWS * BLK, tiles, D])
        out = sp.sb(ctx, "tk_out", [ROWS * BLK, 2, tiles, D])
        share = NE * ES * D // 128 // (B // 2)
        zeros = sp.sb(ctx, "tk_zeros", [128, max(share, (TP - T) * D)])
        clsrow = sp.sb(ctx, "tk_clsrow", [B, D])
        posrow = sp.sb(ctx, "tk_posrow", [B, D])
        acc = sp.ps(ctx, "tk_acc", [128, 2, 512])
        s_const, s_zero, s_zout = sp.sem("tk_const"), sp.sem("tk_zero"), sp.sem("tk_zeroed")
        s_in = [sp.sem("tk_in0"), sp.sem("tk_in1")]
        s_mm, s_ev, s_posb = sp.sem("tk_mm"), sp.sem("tk_ev"), sp.sem("tk_posb_ready")
        s_st = [sp.sem("tk_st0"), sp.sem("tk_st1")]
        s_cls, s_misc = sp.sem("tk_cls"), sp.sem("tk_misc")
        hb = h_rows.rearrange("(b t) d -> b t d", b=B)
        with nc.Block() as block:
            @block.sync
            def _(eng):
                start_counts(eng, *s_st, s_ev)
                eng.dma_start(w_main[:, :, :], tok_w[0:128].rearrange("f a b d -> f (a b) d")).then_inc(s_const, 16)
                for dc in range(2):
                    eng.dma_start(w_rest[64 * dc:64 * dc + 64, :, :], tok_w[128:192, :, dc, :]).then_inc(s_const, 16)

                def load(b, p):
                    img = blocks[:, bass.ds(b, 1), :].rearrange("f o n -> f (o n)")
                    eng.dma_start(main[:, p, :], img[0:128, :]).then_inc(s_in[p], 16)
                    eng.dma_start(rest[0:64, p, :], img[128:192, :]).then_inc(s_in[p], 16)
                    eng.dma_start(rest[64:128, p, 0:BLK * BLK - 1], img[128:192, 1:BLK * BLK]).then_inc(s_in[p], 16)

                for p in range(2):
                    load(p, p)
                with eng.Fori(0, B // 2 - 1) as i:
                    for p in range(2):
                        eng.wait_ge(s_mm, 14 * i + 7 * p + 7)
                        load(2 * i + p + 2, p)

            @block.scalar
            def _(eng):
                eng.wait_ge(s_zero, 2)
                for r in range(ROWS):
                    eng.dma_start(posb[r * BLK:r * BLK + GRID, 0:tiles_with[r], :],
                                  patch_rows(pos[1:1 + NPATCH, :], r)).then_inc(s_const, 16)
                eng.dma_start(bias[:, :], tok_b.rearrange("(o d) -> o d", o=1).to_broadcast([128, D])).then_inc(s_const, 16)
                eng.dma_start(clsrow[:, :], cls.to_broadcast([B, D])).then_inc(s_const, 16)
                eng.dma_start(posrow[:, :], pos[0:1, :].to_broadcast([B, D])).then_inc(s_const, 16)
                eng.dma_start(hb[:, 1 + NPATCH:T, :], txt).then_inc(s_misc, 16)
                eng.wait_ge(s_cls, 1)
                eng.dma_start(hb[:, 0, :], clsrow[:, :]).then_inc(s_misc, 16)
                eng.dma_start(hb[:, T:TP, :], zeros[0:B, 0:(TP - T) * D].rearrange("b (t d) -> b t d", d=D)).then_inc(s_misc, 16)
                view = slots.rearrange("(p r) d -> p (r d)", p=128)
                with eng.Fori(0, B // 2) as i:
                    eng.dma_start(view[:, bass.ds(share * i, share)], zeros[:, 0:share]).then_inc(s_zout, 16)
                    for p in range(2):
                        b = 2 * i + p
                        eng.wait_ge(s_ev, AHEAD + 7 * b + 7)
                        img = hb[bass.ds(b, 1), 1:1 + NPATCH, :].rearrange("o t d -> (o t) d")
                        for r in range(ROWS):
                            eng.dma_start(patch_rows(img, r), out[r * BLK:r * BLK + GRID, p, 0:tiles_with[r], :]).then_inc(s_st[p], 16)
                for p in range(2):
                    eng.wait_ge(s_st[p], AHEAD + 16 * ROWS * (B // 2))
                eng.wait_ge(s_misc, 48)
                eng.wait_ge(s_zout, 16 * (B // 2))

            @block.gpsimd
            def _(eng):
                eng.memset(posb[:, :, :], 0.0).then_inc(s_zero, 1)
                eng.memset(zeros[:, :], 0.0).then_inc(s_zero, 1)

            @block.vector
            def _(eng):
                eng.wait_ge(s_const, 16 * 10)
                for g in range(tiles):
                    eng.tensor_tensor(posb[:, g, :], posb[:, g, :], bias[0:ROWS * BLK, :], ALU.add).then_inc(s_posb, 1)
                eng.tensor_tensor(clsrow[:, :], clsrow[:, :], posrow[:, :], ALU.add).then_inc(s_cls, 1)
                eng.wait_ge(s_posb, 7)
                with eng.Fori(0, B // 2) as i:
                    for p in range(2):
                        eng.wait_ge(s_st[p], AHEAD + 16 * ROWS * i)
                        for g in range(7):
                            m = wide[g]
                            eng.wait_ge(s_mm, 14 * i + 7 * p + g + 1)
                            eng.tensor_tensor(out[0:m, p, g, :], acc[0:m, (7 * p + g) % 2, 0:D],
                                              posb[0:m, g, :], ALU.add).then_inc(s_ev, 1)

            @block.tensor
            def _(eng):
                eng.wait_ge(s_const, 16 * 10)
                with eng.Fori(0, B // 2) as i:
                    for p in range(2):
                        eng.wait_ge(s_in[p], 48 * i + 48)
                        for g in range(tiles):
                            m = wide[g]
                            n = 14 * i + 7 * p + g
                            if 7 * p + g >= 2:
                                eng.wait_ge(s_ev, AHEAD + n - 1)
                            else:
                                eng.wait_ge(s_ev, AHEAD + 14 * i)
                            o = acc[0:m, (7 * p + g) % 2, 0:D]
                            for dr in range(2):
                                at = (g * ROWS + dr) * BLK
                                for dc in range(2):
                                    eng.matmul(o, main[:, p, at + dc:at + dc + m], w_main[:, 2 * dr + dc, :],
                                               start=(dr == 0 and dc == 0), stop=False)
                                mm = eng.matmul(o, rest[:, p, at:at + m], w_rest[:, dr, :],
                                                start=False, stop=(dr == 1))
                            mm.then_inc(s_mm, 1)


def normalise(nc, sp, c, h_rows, w_in, norm1, x_rows, xt, params):
    with sp.phase() as ctx:
        ident = sp.sb(ctx, "nm_ident", [128, 128])
        wp = sp.sb(ctx, "nm_wp", [K2, 2, 2 * H])
        n1 = sp.sb(ctx, "nm_n1", [K2, 2])
        half = sp.sb(ctx, "nm_half", [128, GT4])
        h = sp.sb(ctx, "nm_h", [L, 2, GT4, D])
        st = sp.sb(ctx, "nm_st", [L, 2, GT4, 6])
        mv = sp.sb(ctx, "nm_mv", [L, 2, GT4, 2])
        sc = sp.sb(ctx, "nm_sc", [L, 2, 4, GT4])
        x = sp.sb(ctx, "nm_x", [L, 2, GT4, D])
        xr = sp.sb(ctx, "nm_xr", [L, 2, GT4, D])
        xts = sp.sb(ctx, "nm_xts", [K2, 2, 2, GW])
        pts = sp.sb(ctx, "nm_pts", [2 * H, 2, GW])
        tp = sp.ps(ctx, "nm_tp", [128, 4, 512])
        pp = sp.ps(ctx, "nm_pp", [128, 2, 512])
        s_const, s_w = sp.sem("nm_const"), sp.sem("nm_w")
        s_in = [sp.sem("nm_in0"), sp.sem("nm_in1")]
        s_mv, s_sc, s_x, s_xr = sp.sem("nm_mv"), sp.sem("nm_sc"), sp.sem("nm_x"), sp.sem("nm_xr")
        s_tp, s_xt, s_pp, s_pt = sp.sem("nm_tp"), sp.sem("nm_xt"), sp.sem("nm_pp"), sp.sem("nm_pt")
        s_sx = [sp.sem("nm_stored_x0"), sp.sem("nm_stored_x1")]
        s_sxt = [sp.sem("nm_stored_xt0"), sp.sem("nm_stored_xt1")]
        s_sp = [sp.sem("nm_stored_params0"), sp.sem("nm_stored_params1")]
        s_link, s_glink = sp.sem("nm_link"), sp.sem("nm_glink")

        with nc.Block() as block:
            @block.sync
            def _(eng):
                start_counts(eng, *s_sx, *s_sxt, *s_sp, s_x, s_xr, s_tp, s_xt, s_pt, s_pp)
                eng.dma_start(ident[:, :], c["ident"]).then_inc(s_const, 16)
                eng.dma_start(wp[:, :, :], w_in[:, 2 * DI:2 * DI + 2 * H].rearrange("(k p) n -> p k n", p=K2)).then_inc(s_const, 16)
                eng.dma_start(n1[:, :], norm1).then_inc(s_const, 16)

                def load(g, p, i):
                    eng.wait_ge(s_x, done(g - 2))
                    eng.dma_start(h[:, p, :, :], row_tiles(h_rows, g)).then_inc(s_in[p], 16)

                turns(eng, NG, [(0, load)])

            @block.vector
            def _(eng):
                eng.wait_ge(s_const, 48)
                for k in range(2):
                    eng.tensor_scalar(wp[:, k, :], wp[:, k, :], n1[:, k:k + 1], None, ALU.mult).then_inc(s_w, 1)

                def stats(g, p, i):
                    eng.wait_ge(s_in[p], 16 * i + 16)
                    for j in range(GT4):
                        eng.bn_stats(st[:, p, j, :], h[:, p, j, :]).then_inc(s_link, 1)
                    eng.wait_ge(s_link, GT4 * g + GT4)
                    eng.wait_ge(s_x, done(g - 2))
                    settle(eng, sp.settled)
                    for j in range(GT4):
                        mm = eng.bn_aggr(mv[:, p, j, :], st[:, p, j, :])
                    mm.then_inc(s_mv, 1)

                def centred(g, p, i):
                    eng.wait_ge(s_sc, g + 1)
                    eng.wait_ge(s_sx[p], AHEAD + 16 * i)
                    eng.wait_ge(s_xr, done(g - 2))
                    for j in range(GT4):
                        mm = eng.tensor_scalar(x[:, p, j, :], h[:, p, j, :], mv[:, p, j, 0:1], sc[:, p, 0, j:j + 1],
                                               ALU.subtract, ALU.mult)
                    mm.then_inc(s_x, 1)

                def params_kept(g, p, i):
                    eng.wait_ge(s_pp, done(g))
                    eng.wait_ge(s_sp[p], AHEAD + 16 * i)
                    eng.tensor_copy(pts[:, p, :], pp[0:2 * H, p, 0:GW]).then_inc(s_pt, 1)

                turns(eng, NG, [(1, centred), (0, stats), (3, params_kept)])

            @block.gpsimd
            def _(eng):
                eng.memset(half[:, :], -0.5).then_inc(s_glink, 1)
                eng.wait_ge(s_glink, 1)

                def scales(g, p, i):
                    link = chain(eng, s_glink, 1 + 5 * g, settled=sp.settled)
                    eng.wait_ge(s_mv, g + 1)
                    eng.wait_ge(s_xr, done(g - 2))
                    settle(eng, sp.settled)
                    rstd, r, tmp, tm2 = (sc[:, p, q, :] for q in range(4))
                    link(eng.tensor_scalar(tmp, mv[:, p, :, 1], LN_EPS, None, ALU.add))
                    link(eng.tensor_tensor(rstd, tmp, half[0:L, :], ALU.pow))
                    link(eng.tensor_tensor(tm2, rstd, rstd, ALU.mult))
                    link(eng.tensor_tensor(tm2, tm2, mv[:, p, :, 1], ALU.mult))
                    link(eng.tensor_scalar(tm2, tm2, RMS_EPS, None, ALU.add))
                    eng.tensor_tensor(r, tm2, half[0:L, :], ALU.pow).then_inc(s_sc, 1)

                turns(eng, NG, [(0, scales)])

            @block.scalar
            def _(eng):
                def kept(g, p, i):
                    eng.wait_ge(s_tp, done(g))
                    eng.wait_ge(s_sxt[p], AHEAD + 16 * i)
                    eng.wait_ge(s_pp, done(g - 2))
                    for k in range(2):
                        mm = eng.activation(xts[:, p, k, :], tp[0:K2, 2 * p + k, 0:GW], ACT.Copy)
                    mm.then_inc(s_xt, 1)

                def scaled(g, p, i):
                    eng.wait_ge(s_x, done(g))
                    eng.wait_ge(s_tp, done(g - 2))
                    for j in range(GT4):
                        mm = eng.activation(xr[:, p, j, :], x[:, p, j, :], ACT.Copy, scale=sc[:, p, 1, j:j + 1])
                    mm.then_inc(s_xr, 1)
                    eng.dma_start(row_tiles(x_rows, g), x[:, p, :, :]).then_inc(s_sx[p], 16)

                def store_xt(g, p, i):
                    eng.wait_ge(s_xt, done(g))
                    eng.dma_start(xt[:, :, bass.ds(g * GW, GW)], xts[:, p, :, :]).then_inc(s_sxt[p], 16)

                def store_params(g, p, i):
                    eng.wait_ge(s_pt, done(g))
                    eng.dma_start(params[:, bass.ds(g * GW, GW)], pts[:, p, :]).then_inc(s_sp[p], 16)

                turns(eng, NG, [(2, kept), (1, scaled), (2, store_xt), (4, store_params)])
                for p in range(2):
                    for stored in (s_sx, s_sxt, s_sp):
                        eng.wait_ge(stored[p], AHEAD + 16 * (NG // 2))

            @block.tensor
            def _(eng):
                eng.wait_ge(s_w, 2)

                def turned(g, p, i):
                    eng.wait_ge(s_xr, done(g))
                    eng.wait_ge(s_xt, done(g - 2))
                    for k in range(2):
                        for j in range(GT4):
                            mm = eng.transpose(tp[0:K2, 2 * p + k, L * j:L * j + L],
                                               xr[:, p, j, K2 * k:K2 * k + K2], ident[0:L, 0:L])
                    mm.then_inc(s_tp, 1)

                def step_params(g, p, i):
                    eng.wait_ge(s_xt, done(g))
                    eng.wait_ge(s_pt, done(g - 2))
                    for k in range(2):
                        mm = eng.matmul(pp[0:2 * H, p, 0:GW], wp[:, k, :], xts[:, p, k, :], start=(k == 0), stop=(k == 1))
                    mm.then_inc(s_pp, 1)

                turns(eng, NG, [(1, turned), (2, step_params)])


GROUPS = ((0, 4), (4, 8), (8, 12), (12, 15))
KG = len(GROUPS) * L // STEPS


def mixer_turns(eng, slot, boundary):
    half = B // 2

    def emit(c, j, q, first, last):
        inside = not isinstance(j, int)

        def tile(lag):
            b = 2 * j + (q - lag)
            if inside or b >= 0:
                return (c, b, (q - lag) % 2, c * half + j + (q - lag) // 2) if inside or b < B else None
            return None if first else (c - 1, B + b, (q - lag) % 2, c * half + j + (q - lag) // 2)

        if inside or j > 0:
            kernel = None if last else (c + 1, j - 1, q)
        else:
            kernel = None if first else (c, half - 1, q)
        slot(tile, kernel)

    def chunk(c, first=False, last=False):
        for n in range(4):
            emit(c, n // 2, n % 2, first, last)
            if n == 1 and not first:
                boundary(c)
        with eng.Fori(2, half) as j:
            for q in range(2):
                emit(c, j, q, first, last)

    def nothing(lag):
        return None

    with eng.Fori(0, half) as j:
        for q in range(2):
            slot(nothing, (0, j, q))
    boundary(0)
    chunk(0, first=True)
    with eng.Fori(1, CH - 1) as c:
        chunk(c)
    chunk(CH - 1, last=True)
    for n in range(4):
        def drained(lag):
            return (CH - 1, B + n - lag, (n - lag) % 2, CH * half + (n - lag) // 2) if lag > n else None
        slot(drained, None)


def in_order(*stages):
    def slot(tile, kernel):
        for lag, f in stages:
            at = kernel if lag is None else tile(lag)
            if at is not None:
                f(*at)
    return slot


def mixer(nc, sp, c, x_rows, xt, params, x2_rows):
    with sp.phase() as ctx:
        def sb(name, shape):
            return sp.sb(ctx, "mx_" + name, shape)

        def sem(name):
            return sp.sem("mx_" + name)

        ident = sb("ident", [128, 128])
        wg = sb("wg", [K2, 2, 2 * DI])
        n1 = sb("n1", [K2, 2])
        wbc = sb("wbc", [128, 3, EP])
        wout = sb("wout", [128, 3, D])
        cw = sb("cw", [128, 3, 4])
        dskip = sb("dskip", [L, H])
        block_mask = sb("block_mask", [EP, DI])
        step_mask = sb("step_mask", [EP, EP])
        head_col = sb("head_col", [H * NS, H])
        spread = sb("spread", [SEQ, 2, EP])
        image_mask = sb("image_mask", [SEQ, B])
        half = sb("half", [L, 2 * H])
        s_all, d_all, n_all, tmp_all = (sb(n, [SEQ, TP]) for n in ("s", "d", "n", "t"))
        ring = sb("ring", [SEQ, STEPS, PAD + KW])
        z = sb("z", [SEQ, PAD + KW])
        unit_rows = tmp_all[:, 0:2 * L].rearrange("s (u t) -> s u t", u=2)
        zt = tmp_all[:, 2 * L:2 * L + KW]
        kern = sb("kern", [L, 2, L, SEQ])
        coef = sb("coef", [L, 2, 4, SEQ])
        phi_rhs = sb("phi_rhs", [SEQ, 2, 2, B])
        phi = sb("phi", [EP, 2, 2, B])
        halo = sb("halo", [128, B, 3, 3])
        state = sb("state", [EP, B, DI])
        xts = sb("xts", [K2, 2, 2, L])
        xin = sb("xin", [L, 2, D])
        vb = sb("vb", [128, 2, 3, 3 + L])
        cv = sb("cv", [128, 2, 3, L])
        vt = sb("vt", [128, 2, 3, L])
        u = sb("u", [L, 2, DI])
        ud = sb("ud", [L, 2, DI])
        sg = sb("sg", [L, 4, DI])
        sq = sb("sq", [L, 2, EP])
        rs = sb("rs", [L, 2, 2 * H])
        rn = sb("rn", [L, 2, 2 * H])
        bcn = sb("bcn", [L, 2, EP])
        br = sb("br", [L, 2, EP])
        cr = sb("cr", [L, 2, EP])
        tb = sb("tb", [EP, 2, EP])
        bt = sb("bt", [H * NS, 2, L])
        cm = sb("cm", [H * NS, 2, H, L])
        crt = sb("crt", [EP, 2, L])
        m = sb("m", [L, 2, H, L])
        gy = sb("gy", [L, 2, DI])
        gyt = sb("gyt", [128, 2, 3, L])
        x2 = sb("x2", [L, 2, D])

        bank = [sp.ps(ctx, f"mx_bank{i}", [128, 512]) for i in range(8)]
        b_v, b_gate, b_bc, b_u, b_s0, b_s1, b_y, b_st = bank
        b_s = (b_s0, b_s1)

        s_const, s_w, s_mem, s_par = sem("const"), sem("w"), sem("mem"), sem("par")
        s_xt = [sem("xt0"), sem("xt1")]
        s_xin = [sem("xin0"), sem("xin1")]
        s_store = [sem("store0"), sem("store1")]
        s_prep, s_alink = sem("prep"), sem("prep_act")
        s_conv_part = sem("conv_part")
        s_start, s_ring, s_link = sem("start"), sem("ring"), sem("link")
        s_kt, s_kern = sem("kernel_transposed"), sem("kernel_kept")
        s_ct, s_coef, s_pr, s_pm, s_phi = sem("coef_t"), sem("coef"), sem("phi_rhs"), sem("phi_mm"), sem("phi")
        names = ("vmm", "gmm", "vtaken", "halo_in", "halo_out", "conv", "silu", "bcmm", "ut", "sq", "u", "gate",
                 "rs", "rn", "bcn", "br", "cr", "tb", "tr", "cm", "crt", "smm", "m", "ymm", "stmm", "st",
                 "ud", "gsum", "gy", "gyt_mm", "gyt", "omm", "x2", "rlink")
        e = {n: sem(n) for n in names}

        def tile(buf, k_c, k_b):
            return buf[bass.ds((k_b * CH + k_c) * L, L), :]

        def image(buf, b):
            return buf[:, bass.ds(b, 1)]

        with nc.Block() as block:
            @block.sync
            def _(eng):
                start_counts(eng, *s_store, s_kt, s_ct, s_pm, s_kern, s_link, *e.values())
                pv = params.rearrange("(q h) (b t) -> q h b t", q=2, b=B)
                for h in range(H):
                    eng.dma_start(s_all[h * B:(h + 1) * B, :], pv[0, h]).then_inc(s_par, 16)
                    eng.dma_start(d_all[h * B:(h + 1) * B, :], pv[1, h]).then_inc(s_par, 16)
                for dst, name in ((ident, "ident"), (block_mask, "block_mask"), (step_mask, "step_mask"),
                                  (head_col, "head_col"), (image_mask, "image_mask"), (n1, "norm1")):
                    eng.dma_start(dst[:, :], c[name]).then_inc(s_const, 16)
                for dst, name in ((spread, "spread"), (cw, "conv_w")):
                    eng.dma_start(dst[:, :, :], c[name]).then_inc(s_const, 16)
                eng.dma_start(wg[:, :, :], c["w_in"][:, 0:2 * DI].rearrange("(k p) n -> p k n", p=K2)).then_inc(s_const, 16)
                eng.dma_start(wbc[:, :, :], c["w_bc"].rearrange("(k p) n -> p k n", p=128)).then_inc(s_const, 16)
                eng.dma_start(wout[:, :, :], c["w_out"].rearrange("(k p) n -> p k n", p=128)).then_inc(s_const, 16)
                eng.dma_start(dskip[:, :], c["d_skip"].rearrange("(o h) -> o h", o=1).to_broadcast([L, H])).then_inc(s_const, 16)
                xtv = xt.rearrange("p k (b t) -> p k b t", b=B)

                def load_xt(ci, b, p, i):
                    k = ci * B + b
                    eng.wait_ge(e["gmm"], done(k - 2))
                    src = xtv[:, :, bass.ds(b, 1), bass.ds(ci * L, L)].rearrange("p k o t -> p k (o t)")
                    eng.dma_start(xts[:, p, :, :], src).then_inc(s_xt[p], 16)

                def load_x(ci, b, p, i):
                    k = ci * B + b
                    eng.wait_ge(e["x2"], done(k - 2))
                    eng.dma_start(xin[:, p, :], tile(x_rows, ci, b)).then_inc(s_xin[p], 16)

                mixer_turns(eng, in_order((0, load_xt), (3, load_x)), lambda ci: None)

            @block.gpsimd
            def _(eng):
                eng.memset(half[:, :], -0.5).then_inc(s_mem, 1)
                eng.memset(halo[:, :, :, :], 0.0).then_inc(s_mem, 1)
                eng.memset(state[:, :, :], 0.0).then_inc(s_mem, 1)
                eng.wait_ge(s_mem, 3)
                eng.wait_ge(s_const, 16 * 12)

                def halos(ci, b, p, i):
                    k = ci * B + b
                    hb = image(halo, b).rearrange("p o f t -> p (o f) t")
                    eng.wait_ge(e["conv"], done(k - 2))
                    eng.wait_ge(e["halo_out"], done(k - 1))
                    settle(eng, sp.settled)
                    eng.tensor_copy(vb[:, p, :, 0:3], hb).then_inc(e["halo_in"], 1)
                    eng.wait_ge(e["vtaken"], done(k))
                    eng.wait_ge(e["halo_in"], done(k))
                    settle(eng, sp.settled)
                    eng.tensor_copy(hb, vb[:, p, :, L:L + 3]).then_inc(e["halo_out"], 1)

                def step(ci, b, p, i):
                    k = ci * B + b
                    eng.wait_ge(s_phi, ci + 1)
                    eng.wait_ge(e["stmm"], done(k - 2))
                    settle(eng, sp.settled)
                    pb = phi[:, bass.ds(ci % 2, 1), :, bass.ds(b, 1)].rearrange("q o j u -> q j (o u)")
                    eng.tensor_tensor(tb[:, p, :].rearrange("q (h j n) -> q h j n", h=H, j=2),
                                      step_mask[:, :].rearrange("q (h j n) -> q h j n", h=H, j=2),
                                      pb.unsqueeze(1).to_broadcast([EP, H, 2, NS]), ALU.mult).then_inc(e["tb"], 1)

                def norms(ci, b, p, i):
                    k = ci * B + b
                    eng.wait_ge(e["rs"], done(k))
                    eng.wait_ge(e["bcn"], done(k - 2))
                    settle(eng, sp.settled)
                    eng.tensor_scalar(rs[:, p, :], rs[:, p, :], L2_EPS, None, ALU.add).then_inc(e["rlink"], 1)
                    eng.wait_ge(e["rlink"], done(k))
                    settle(eng, sp.settled)
                    eng.tensor_tensor(rn[:, p, :], rs[:, p, :], half[:, :], ALU.pow).then_inc(e["rn"], 1)

                def weighted(ci, b, p, i):
                    k = ci * B + b
                    eng.wait_ge(e["bcn"], done(k))
                    eng.wait_ge(s_coef, ci + 1)
                    eng.wait_ge(e["tr"], done(k - 2))
                    eng.wait_ge(e["stmm"], done(k - 2))
                    settle(eng, sp.settled)
                    for dst, off, q0, name in ((cr, H * NS, 0, "cr"), (br, 0, 2, "br")):
                        src = bcn[:, p, off:off + H * NS].rearrange("t (h n) -> t h n", h=H)
                        for j in range(2):
                            w = coef[:, bass.ds(ci % 2, 1), q0 + j, :].rearrange("t o (h b) -> t (o h) b", h=H)[:, :, bass.ds(b, 1)]
                            ins = eng.tensor_tensor(dst[:, p, :].rearrange("t (h j n) -> t h j n", h=H, j=2)[:, :, j, :],
                                                    src, w.to_broadcast([L, H, NS]), ALU.mult)
                        ins.then_inc(e[name], 1)

                def skipped(ci, b, p, i):
                    k = ci * B + b
                    eng.wait_ge(e["u"], done(k))
                    eng.wait_ge(e["gsum"], done(k - 2))
                    settle(eng, sp.settled)
                    eng.tensor_tensor(ud[:, p, :].rearrange("t (h q) -> t h q", h=H),
                                      u[:, p, :].rearrange("t (h q) -> t h q", h=H),
                                      dskip[:, :].unsqueeze(2).to_broadcast([L, H, P]), ALU.mult).then_inc(e["ud"], 1)

                mixer_turns(eng, in_order((2, step), (2, norms), (2, weighted), (2, skipped), (0, halos)), lambda ci: None)

            @block.scalar
            def _(eng):
                eng.wait_ge(s_prep, 3)
                eng.activation(tmp_all[:, :], tmp_all[:, :], ACT.Exp, scale=-1.0).then_inc(s_alink, 1)
                eng.wait_ge(s_alink, 1)
                eng.activation(tmp_all[:, :], tmp_all[:, :], ACT.Ln, bias=1.0).then_inc(s_alink, 1)
                eng.activation(d_all[:, :], d_all[:, :], ACT.Exp, scale=-1.0).then_inc(s_alink, 1)
                eng.wait_ge(s_const, 16 * 12)

                def masked(ci, b, p, i):
                    k = ci * B + b
                    eng.wait_ge(e["tr"], done(k))
                    eng.wait_ge(e["smm"], done(k - 2))
                    eng.activation(bt[:, p, :], b_bc[0:H * NS, 128:128 + L], ACT.Copy)
                    for h in range(H):
                        ins = eng.activation(cm[:, p, h, :], b_bc[0:H * NS, 128 + L:128 + 2 * L], ACT.Copy, scale=head_col[:, h:h + 1])
                    ins.then_inc(e["cm"], 1)

                def unit_c(ci, b, p, i):
                    k = ci * B + b
                    eng.wait_ge(e["ymm"], done(k - 2))
                    eng.activation(crt[:, p, :], b_bc[0:EP, 128 + 2 * L:128 + 3 * L], ACT.Copy).then_inc(e["crt"], 1)

                def values(ci, b, p, i):
                    k = ci * B + b
                    eng.wait_ge(e["vmm"], done(k))
                    eng.wait_ge(e["conv"], done(k - 2))
                    eng.wait_ge(e["halo_out"], done(k - 2))
                    eng.activation(vb[:, p, :, 3:3 + L], b_v[:, 0:3 * L].rearrange("q (f t) -> q f t", f=3), ACT.Copy).then_inc(e["vtaken"], 1)

                def gates(ci, b, p, i):
                    k = ci * B + b
                    eng.wait_ge(e["gmm"], done(k))
                    eng.wait_ge(e["gy"], done(k - 4))
                    eng.activation(sg[:, bass.ds(k % 4, 1), :].rearrange("t o n -> t (o n)"), b_gate[0:L, 0:DI], ACT.Silu).then_inc(e["gate"], 1)

                def silu(ci, b, p, i):
                    k = ci * B + b
                    eng.wait_ge(e["conv"], done(k))
                    eng.wait_ge(e["ut"], done(k - 2))
                    eng.activation(vt[:, p, :, :], cv[:, p, :, :], ACT.Silu).then_inc(e["silu"], 1)

                def squares(ci, b, p, i):
                    k = ci * B + b
                    eng.wait_ge(e["bcmm"], done(k))
                    eng.wait_ge(e["rs"], done(k - 2))
                    eng.activation(sq[:, p, :], b_bc[0:L, 0:EP], ACT.Square).then_inc(e["sq"], 1)

                def inputs(ci, b, p, i):
                    k = ci * B + b
                    eng.wait_ge(e["ut"], done(k))
                    eng.wait_ge(e["stmm"], done(k - 2))
                    eng.wait_ge(e["ud"], done(k - 2))
                    eng.activation(u[:, p, :], b_u[0:L, 0:DI], ACT.Copy).then_inc(e["u"], 1)

                def gated(ci, b, p, i):
                    k = ci * B + b
                    eng.wait_ge(e["gyt_mm"], done(k))
                    eng.wait_ge(e["omm"], done(k - 2))
                    eng.activation(gyt[:, p, :, :], b_u[:, 0:3 * L].rearrange("q (f t) -> q f t", f=3), ACT.Copy).then_inc(e["gyt"], 1)

                def store(ci, b, p, i):
                    k = ci * B + b
                    eng.wait_ge(e["x2"], done(k))
                    eng.dma_start(tile(x2_rows, ci, b), x2[:, p, :]).then_inc(s_store[p], 16)

                def kernel_rows(ci, j, q):
                    eng.wait_ge(e["m"], done(ci * B - B - 1))
                    for a in range(2):
                        r0, r1 = GROUPS[2 * q + a]
                        eng.wait_ge(s_kt, AHEAD + KG * ci + 4 * j + 2 * q + a + 1)
                        eng.activation(kern[:, bass.ds(ci % 2, 1), bass.ds(j * STEPS + r0, r1 - r0), :].rearrange("t o r s -> t (o r) s"),
                                       b_s[a][0:L, 0:(r1 - r0) * SEQ].rearrange("t (r s) -> t r s", s=SEQ), ACT.Copy).then_inc(s_kern, 1)

                def boundary(ci):
                    eng.wait_ge(s_ct, AHEAD + ci + 1)
                    eng.wait_ge(e["br"], done(ci * B - B - 1))
                    eng.activation(coef[:, bass.ds(ci % 2, 1), :, :].rearrange("t o q s -> t (o q) s"),
                                   b_s0[0:L, 0:4 * SEQ].rearrange("t (q s) -> t q s", q=4), ACT.Copy).then_inc(s_coef, 1)
                    eng.wait_ge(s_pm, AHEAD + ci + 1)
                    eng.wait_ge(e["tb"], done(ci * B - B - 1))
                    eng.activation(phi[:, bass.ds(ci % 2, 1), :, :].rearrange("q o j b -> q (o j) b"),
                                   b_s1[0:EP, 0:2 * B].rearrange("q (j b) -> q j b", j=2), ACT.Copy).then_inc(s_phi, 1)

                mixer_turns(eng, in_order((2, squares), (2, inputs), (1, silu), (2, masked), (2, unit_c), (0, values),
                                          (3, gated), (None, kernel_rows), (0, gates), (4, store)), boundary)
                for p in range(2):
                    eng.wait_ge(s_store[p], AHEAD + 16 * (NT // 2))

            @block.vector
            def _(eng):
                link = chain(eng, s_prep, 0)
                link(eng.memset(z[:, 0:PAD], 0.0))
                link(eng.memset(ring[:, :, 0:PAD], 0.0))
                eng.wait_ge(s_par, 16 * 2 * H)
                link(eng.scalar_tensor_tensor(tmp_all[:, :], s_all[:, :], -1.0, s_all[:, :], ALU.mult, ALU.max))
                eng.wait_ge(s_alink, 3)
                link(eng.scalar_tensor_tensor(n_all[:, :], s_all[:, :], 0.0, tmp_all[:, :], ALU.max, ALU.add))
                link(eng.tensor_scalar(d_all[:, :], d_all[:, :], 1.0, None, ALU.add))
                link(eng.reciprocal(d_all[:, :], d_all[:, :]))
                link(eng.tensor_tensor(n_all[:, :], n_all[:, :], d_all[:, :], ALU.mult))
                link(eng.tensor_tensor(tmp_all[:, :], n_all[:, :], d_all[:, :], ALU.mult))
                link(eng.tensor_scalar(tmp_all[:, :], tmp_all[:, :], 1.0, None, ALU.add))
                link(eng.reciprocal(s_all[:, :], tmp_all[:, :]))
                link(eng.scalar_tensor_tensor(n_all[:, :], n_all[:, :], -1.0, s_all[:, :], ALU.mult, ALU.mult))
                eng.wait_ge(s_const, 16 * 12)
                for k in range(2):
                    eng.tensor_scalar(wg[:, k, :], wg[:, k, :], n1[:, k:k + 1], None, ALU.mult).then_inc(s_w, 1)

                def start(ci):
                    eng.wait_ge(s_kt, AHEAD + KG * ci)
                    eng.wait_ge(s_ct, AHEAD + ci)
                    eng.memset(ring[:, :, PAD:PAD + KW], 0.0).then_inc(s_start, 1)
                    eng.memset(z[:, PAD:PAD + 1], 1.0).then_inc(s_start, 1)
                    eng.memset(z[:, PAD + 1:PAD + 2], 0.0).then_inc(s_start, 1)
                    eng.tensor_copy(z[:, PAD + 2:PAD + 2 + L], d_all[:, bass.ds(ci * L, L)]).then_inc(s_start, 1)
                    eng.wait_ge(s_start, 5 * ci + 4)
                    eng.memset(ring[:, STEPS - 1, PAD + 1:PAD + 2], 1.0).then_inc(s_start, 1)
                    eng.wait_ge(s_start, 5 * ci + 5)
                    settle(eng, sp.settled)

                def recur(kernel, first, last):
                    if kernel is None:
                        return
                    ci, j, q = kernel
                    rows = range(GROUPS[2 * q][0], GROUPS[2 * q + 1][1])
                    for n in range(first, min(last, 3 * len(rows))):
                        r, part = rows[n // 3], n % 3
                        at = ci * L + j * STEPS + r
                        zz = z[:, bass.ds(j * STEPS + r, KW)]
                        old = ring[:, (r - 1) % STEPS, bass.ds(j * STEPS + r, KW)]
                        group = 2 * q + (r >= GROUPS[2 * q + 1][0])
                        if part == 0 and r == GROUPS[group][0]:
                            eng.wait_ge(s_kt, AHEAD + KG * ci + 4 * j + group - 3)
                        eng.wait_ge(s_link, AHEAD + 3 * at + part)
                        if part == 0:
                            eng.tensor_scalar(zt, old, n_all[:, bass.ds(at, 1)], None, ALU.mult).then_inc(s_link, 1)
                        elif part == 1:
                            eng.scalar_tensor_tensor(zz, zz, s_all[:, bass.ds(at, 1)], zt, ALU.mult, ALU.add).then_inc(s_link, 1)
                        else:
                            eng.scalar_tensor_tensor(ring[:, r, bass.ds(j * STEPS + r, KW)], zz, d_all[:, bass.ds(at, 1)], old,
                                                     ALU.mult, ALU.add).then_inc(s_link, 1)
                        r0, r1 = GROUPS[group]
                        if part == 2 and r == r1 - 1:
                            eng.wait_ge(s_link, AHEAD + 3 * at + 3)
                            eng.tensor_copy(unit_rows[:, :, bass.ds(j * STEPS + r0, r1 - r0)].rearrange("s u t -> s t u"),
                                            ring[:, r0:r1, PAD:PAD + 2]).then_inc(s_ring, 1)

                def boundary(ci):
                    eng.wait_ge(s_pm, AHEAD + ci)
                    for to, src in ((0, z[:, PAD:PAD + 2]), (1, ring[:, STEPS - 1, PAD:PAD + 2])):
                        for fr in range(2):
                            ins = eng.tensor_scalar(phi_rhs[:, fr, to, :], image_mask[:, :], src[:, fr:fr + 1], None, ALU.mult)
                    ins.then_inc(s_pr, 1)
                    if not (isinstance(ci, int) and ci == CH - 1):
                        eng.wait_ge(s_pr, ci + 1)
                        start(ci + 1)

                def conv(at, taps, kernel, n):
                    if at is None:
                        return recur(kernel, n, n + 3 * len(taps))
                    ci, b, p, i = at
                    k = ci * B + b
                    if taps[0] == 0:
                        eng.wait_ge(e["vtaken"], done(k))
                        eng.wait_ge(e["halo_in"], done(k))
                        eng.wait_ge(e["silu"], done(k - 2))
                    for tap in taps:
                        if tap > 0:
                            eng.wait_ge(s_conv_part, 9 * k + 3 * tap)
                        for f in range(3):
                            if tap == 0:
                                ins = eng.tensor_scalar(cv[:, p, f, :], vb[:, p, f, 0:L], cw[:, f, 0:1], None, ALU.mult)
                            else:
                                ins = eng.scalar_tensor_tensor(cv[:, p, f, :], vb[:, p, f, tap:tap + L], cw[:, f, tap:tap + 1],
                                                               cv[:, p, f, :], ALU.mult, ALU.add)
                            if tap < 3:
                                ins.then_inc(s_conv_part, 1)
                            elif f == 2:
                                ins.then_inc(e["conv"], 1)
                            recur(kernel, n, n + 1)
                            n += 1

                def sums(ci, b, p, i):
                    k = ci * B + b
                    eng.wait_ge(e["sq"], done(k))
                    eng.wait_ge(e["rn"], done(k - 2))
                    eng.tensor_reduce(rs[:, p, :], sq[:, p, :].rearrange("t (g n) -> t g n", n=NS), AX.X, ALU.add).then_inc(e["rs"], 1)

                def unit(ci, b, p, i):
                    k = ci * B + b
                    eng.wait_ge(e["rn"], done(k))
                    eng.wait_ge(e["br"], done(k - 2))
                    eng.wait_ge(e["tr"], done(k - 2))
                    eng.tensor_tensor(bcn[:, p, :].rearrange("t (g n) -> t g n", n=NS),
                                      b_bc[0:L, 0:EP].rearrange("t (g n) -> t g n", n=NS),
                                      rn[:, p, :].unsqueeze(2).to_broadcast([L, 2 * H, NS]), ALU.mult).then_inc(e["bcn"], 1)

                def kernel_by(ci, b, p, i):
                    k = ci * B + b
                    eng.wait_ge(e["smm"], done(k))
                    eng.wait_ge(e["ymm"], done(k - 2))
                    eng.wait_ge(s_kern, AHEAD + KG * ci + KG)
                    for part in range(2):
                        kv = kern[:, bass.ds(ci % 2, 1), :, :].rearrange("q o t (h b) -> q h b (o t)", h=H)[:, 3 * part:3 * part + 3, bass.ds(b, 1), :]
                        ins = eng.tensor_tensor(m[:, p, 3 * part:3 * part + 3, :],
                                                b_s[part][0:L, 0:3 * L].rearrange("q (h t) -> q h t", h=3),
                                                kv.rearrange("q h o t -> q (h o) t"), ALU.mult)
                    ins.then_inc(e["m"], 1)

                def new_state(ci, b, p, i):
                    k = ci * B + b
                    eng.wait_ge(e["stmm"], done(k))
                    eng.tensor_tensor(image(state, b).rearrange("q o n -> q (o n)"),
                                      b_st[0:EP, 0:DI], block_mask[:, :], ALU.mult).then_inc(e["st"], 1)

                def skipped_in(ci, b, p, i):
                    k = ci * B + b
                    eng.wait_ge(e["ymm"], done(k))
                    eng.wait_ge(e["ud"], done(k))
                    eng.wait_ge(e["gyt_mm"], done(k - 2))
                    eng.tensor_tensor(gy[:, p, :], b_y[0:L, 0:DI], ud[:, p, :], ALU.add).then_inc(e["gsum"], 1)

                def gating(ci, b, p, i):
                    k = ci * B + b
                    eng.wait_ge(e["gsum"], done(k))
                    eng.wait_ge(e["gate"], done(k))
                    eng.tensor_tensor(gy[:, p, :], gy[:, p, :],
                                      sg[:, bass.ds(k % 4, 1), :].rearrange("t o n -> t (o n)"), ALU.mult).then_inc(e["gy"], 1)

                def output(ci, b, p, i):
                    k = ci * B + b
                    eng.wait_ge(e["omm"], done(k))
                    eng.wait_ge(s_xin[p], 16 * i + 16)
                    eng.wait_ge(s_store[p], AHEAD + 16 * i)
                    eng.tensor_tensor(x2[:, p, :], b_st[0:L, 0:D], xin[:, p, :], ALU.add).then_inc(e["x2"], 1)

                def slot(tile, kernel):
                    def other(lag, f):
                        if tile(lag) is not None:
                            f(*tile(lag))

                    recur(kernel, 0, 4)
                    conv(tile(1), (0, 1), kernel, 4)
                    other(4, output)
                    other(2, sums)
                    recur(kernel, 10, 11)
                    other(3, kernel_by)
                    recur(kernel, 11, 12)
                    conv(tile(1), (2,), kernel, 12)
                    other(2, unit)
                    recur(kernel, 15, 16)
                    conv(tile(1), (3,), kernel, 16)
                    other(3, skipped_in)
                    recur(kernel, 19, 20)
                    other(3, gating)
                    recur(kernel, 20, 21)
                    other(3, new_state)
                    recur(kernel, 21, 24)

                start(0)
                mixer_turns(eng, slot, boundary)

            @block.tensor
            def _(eng):
                eng.wait_ge(s_const, 16 * 12)
                eng.wait_ge(s_w, 2)
                eng.wait_ge(s_mem, 3)

                def turned(ci, b, p, i):
                    k = ci * B + b
                    eng.wait_ge(e["bcn"], done(k))
                    eng.wait_ge(e["cr"], done(k))
                    settle(eng, sp.settled)
                    for j in range(2):
                        eng.transpose(b_bc[0:H * NS, 128 + L * j:128 + L * j + L], bcn[:, p, H * NS * j:H * NS * (j + 1)], ident[0:L, 0:L])
                    eng.transpose(b_bc[0:EP, 128 + 2 * L:128 + 3 * L], cr[:, p, :], ident[0:L, 0:L]).then_inc(e["tr"], 1)

                def values(ci, b, p, i):
                    k = ci * B + b
                    eng.wait_ge(s_xt[p], 16 * i + 16)
                    eng.wait_ge(e["vtaken"], done(k - 1))
                    for f in range(3):
                        for kk in range(2):
                            mm = eng.matmul(b_v[:, L * f:L * f + L], wg[:, kk, DI + 128 * f:DI + 128 * f + 128],
                                            xts[:, p, kk, :], start=(kk == 0), stop=(kk == 1))
                    mm.then_inc(e["vmm"], 1)

                def gates(ci, b, p, i):
                    k = ci * B + b
                    eng.wait_ge(e["gate"], done(k - 1))
                    for kk in range(2):
                        mm = eng.matmul(b_gate[0:L, 0:DI], xts[:, p, kk, :], wg[:, kk, 0:DI], start=(kk == 0), stop=(kk == 1))
                    mm.then_inc(e["gmm"], 1)

                def project(ci, b, p, i):
                    k = ci * B + b
                    eng.wait_ge(e["gyt"], done(k))
                    eng.wait_ge(e["st"], done(k))
                    for f in range(3):
                        mm = eng.matmul(b_st[0:L, 0:D], gyt[:, p, f, :], wout[:, f, :], start=(f == 0), stop=(f == 2))
                    mm.then_inc(e["omm"], 1)

                def scores(ci, b, p, i):
                    k = ci * B + b
                    eng.wait_ge(e["cm"], done(k))
                    eng.wait_ge(e["m"], done(k - 1))
                    if isinstance(ci, int) and ci == CH - 1:
                        eng.wait_ge(s_kern, AHEAD + KG * CH)
                    else:
                        eng.wait_ge(s_kern, AHEAD + KG + 2 * (k + 1))
                    ends = 1 + (isinstance(b, int) and b == B - 1 and not (isinstance(ci, int) and ci == CH - 1))
                    eng.wait_ge(s_coef, ci + ends)
                    eng.wait_ge(s_phi, ci + ends)
                    for part in range(2):
                        mm = eng.matmul(b_s[part][0:L, 0:3 * L], bt[:, p, :],
                                        cm[:, p, 3 * part:3 * part + 3, :].rearrange("q h t -> q (h t)"), start=True, stop=True)
                    mm.then_inc(e["smm"], 1)

                def states_in(ci, b, p, i):
                    k = ci * B + b
                    eng.wait_ge(e["silu"], done(k))
                    eng.wait_ge(e["crt"], done(k - 1))
                    eng.wait_ge(e["cm"], done(k - 1))
                    for f in range(3):
                        mm = eng.matmul(b_bc[0:L, 0:EP], vt[:, p, f, :], wbc[:, f, :], start=(f == 0), stop=(f == 2))
                    mm.then_inc(e["bcmm"], 1)
                    eng.wait_ge(e["gyt"], done(k - 2))
                    for f in range(3):
                        mm = eng.transpose(b_u[0:L, 128 * f:128 * f + 128], vt[:, p, f, :], ident[:, :])
                    mm.then_inc(e["ut"], 1)

                def scan(ci, b, p, i):
                    k = ci * B + b
                    sv = image(state, b).rearrange("q o n -> q (o n)")
                    eng.wait_ge(e["crt"], done(k))
                    eng.wait_ge(e["st"], done(k - 1))
                    eng.wait_ge(e["gsum"], done(k - 1))
                    eng.matmul(b_y[0:L, 0:DI], crt[:, p, :], sv, start=True, stop=False)
                    eng.wait_ge(e["m"], done(k))
                    eng.wait_ge(e["u"], done(k))
                    for h in range(H):
                        mm = eng.matmul(b_y[0:L, P * h:P * h + P], m[:, p, h, :], u[:, p, P * h:P * h + P],
                                        start=False, stop=(h == H - 1))
                    mm.then_inc(e["ymm"], 1)
                    eng.wait_ge(e["br"], done(k))
                    eng.wait_ge(e["tb"], done(k))
                    eng.wait_ge(e["x2"], done(k - 1))
                    eng.matmul(b_st[0:EP, 0:DI], br[:, p, :], u[:, p, :], start=True, stop=False)
                    eng.matmul(b_st[0:EP, 0:DI], tb[:, p, :], sv, start=False, stop=True).then_inc(e["stmm"], 1)

                def gated(ci, b, p, i):
                    k = ci * B + b
                    eng.wait_ge(e["gy"], done(k))
                    if not (isinstance(ci, int) and ci == CH - 1 and isinstance(b, int) and b == B - 1):
                        eng.wait_ge(e["u"], done(k + 1))
                    for f in range(3):
                        mm = eng.transpose(b_u[:, L * f:L * f + L], gy[:, p, 128 * f:128 * f + 128], ident[0:L, 0:L])
                    mm.then_inc(e["gyt_mm"], 1)

                def kernel_rows(ci, j, q):
                    for a in range(2):
                        r0, r1 = GROUPS[2 * q + a]
                        group = KG * ci + 4 * j + 2 * q + a
                        eng.wait_ge(s_ring, group + 1)
                        eng.wait_ge(e["m"], done((ci - 1) * B + 2 * j + q - 1))
                        eng.wait_ge(s_kern, AHEAD + group - 1)
                        for r in range(r0, r1):
                            mm = eng.transpose(b_s[a][0:L, SEQ * (r - r0):SEQ * (r - r0) + SEQ],
                                               ring[:, r, PAD + 2:PAD + 2 + L], ident[0:SEQ, 0:SEQ])
                        mm.then_inc(s_kt, 1)

                def boundary(ci):
                    eng.wait_ge(s_kern, AHEAD + KG * ci + KG)
                    for n, src in enumerate((unit_rows[:, 0, :], unit_rows[:, 1, :], z[:, PAD + 2:PAD + 2 + L],
                                             ring[:, STEPS - 1, PAD + 2:PAD + 2 + L])):
                        mm = eng.transpose(b_s0[0:L, SEQ * n:SEQ * n + SEQ], src, ident[0:SEQ, 0:SEQ])
                    mm.then_inc(s_ct, 1)
                    eng.wait_ge(s_pr, ci + 1)
                    for fr in range(2):
                        mm = eng.matmul(b_s1[0:EP, 0:2 * B], spread[:, fr, :], phi_rhs[:, fr, :, :].rearrange("s j b -> s (j b)"),
                                        start=(fr == 0), stop=(fr == 1))
                    mm.then_inc(s_pm, 1)

                mixer_turns(eng, in_order((4, project), (2, states_in), (3, scores), (0, values), (3, scan), (2, turned), (0, gates),
                                          (3, gated), (None, kernel_rows)), boundary)


class Route:

    def __init__(self, sp, ctx):
        self.mean = sp.sb(ctx, "rt_mean", [L, NT])
        self.rstd = sp.sb(ctx, "rt_rstd", [L, NT])
        self.gap = sp.sb(ctx, "rt_gap", [L, NT])
        self.keep = sp.sb(ctx, "rt_keep", [L, 2, NT])
        self.slot = sp.sb(ctx, "rt_slot", [L, 2, NT])


def feed_forward(nc, sp, c, x2_rows, h_rows, h2_rows, slots, rt):
    NF = FF // 128
    with sp.phase() as ctx:
        def sb(name, shape, dt=F32):
            return sp.sb(ctx, "ff_" + name, shape, dt)

        def sem(name):
            return sp.sem("ff_" + name)

        ident = sb("ident", [128, 128])
        w1 = sb("w1", [K2, 2, FF])
        n2 = sb("n2", [K2, 2])
        w2 = sb("w2", [128, NF, D])
        b1 = sb("b1", [128, NF])
        b2 = sb("b2", [L, D])
        gate = sb("gate", [K2, 2, NE])
        before = sb("before", [L, L])
        ones = sb("ones", [L, L])
        valid = sb("valid", [L, NT])
        expert = sb("expert", [L, NE])
        rank = sb("rank", [L, NE])
        base = sb("base", [L, NE])
        half = sb("half", [L, GT4])
        x2 = sb("x2", [L, 2, GT4, D])
        h = sb("h", [L, 2, GT4, D])
        hx = sb("hx", [L, 2, GT4, D])
        ss = sb("ss", [L, 2, GT4])
        r = sb("r", [L, 2, GT4])
        xr = sb("xr", [L, 2, GT4, D])
        gt = sb("gt", [128, 2, NF, GW])
        w1s = [sb(f"w1_{n}", [K2, 2, FF], F32R) for n in ("head", "rest")]
        xts = [sb(f"xt_{n}", [K2, 2, 2, GW], F32R) for n in ("head", "rest")]
        h2 = sb("h2", [L, 2, GT4, D])
        st = sb("st", [L, 2, GT4, 6])
        mv = sb("mv", [L, 2, GT4, 2])
        rstd = sb("rstd", [L, 2, GT4])
        q = sb("q", [L, 2, GT4])
        x3 = sb("x3", [L, 2, GT4, D])
        x3t = sb("x3t", [K2, 2, 2, GW])
        z = sb("z", [L, 2, GT4, D])
        lg = sb("lg", [L, 2, GT4, NE])
        mask = sb("mask", [L, 2, 2, GT4, NE])
        both = sb("both", [L, 2, GT4, NE])
        work = sb("work", [L, GT4, NE])
        best = sb("best", [L, 4, GT4])
        run = sb("run", [L, GT4 + 1, NE])
        place = sb("place", [L, GT4, NE])
        small = sb("small", [L, 4, GT4])
        sidx = sb("sidx", [L, 2, 2, GT4], I32)
        bank = [sp.ps(ctx, f"ff_bank{i}", [128, 512]) for i in range(8)]
        s_const, s_w, s_mem = sem("const"), sem("w"), sem("mem")
        s_in = [sem("in0"), sem("in1")]
        s_store = [sem("store0"), sem("store1")]
        s_scat = [sem("scat0"), sem("scat1")]
        s_scale, s_norm = sem("scale_link"), sem("norm_link")
        s_st, s_choose, s_place = sem("st_link"), sem("choose_link"), sem("place_link")
        names = ("ss", "r", "xr", "xt_mm", "xt_head", "xt", "up", "gelu", "down", "hx", "h2", "stats", "q", "x3", "x3t_mm", "x3t",
                 "z", "lmm", "both", "count", "sidx")
        e = {n: sem(n) for n in names}

        with nc.Block() as block:
            @block.sync
            def _(eng):
                start_counts(eng, *s_store, *e.values())
                for dst, name in ((ident, "ident"), (n2, "norm2"), (b1, "ff_b1"), (before, "before"), (ones, "ones"),
                                  (valid, "valid"), (expert, "expert")):
                    eng.dma_start(dst[:, :], c[name]).then_inc(s_const, 16)
                eng.dma_start(w1[:, :, :], c["ff_w1"].rearrange("(k p) n -> p k n", p=K2)).then_inc(s_const, 16)
                eng.dma_start(w2[:, :, :], c["ff_w2"].rearrange("(k p) n -> p k n", p=128)).then_inc(s_const, 16)
                eng.dma_start(gate[:, :, :], c["gate"].rearrange("(k p) n -> p k n", p=K2)).then_inc(s_const, 16)
                eng.dma_start(b2[:, :], c["ff_b2"].rearrange("(o d) -> o d", o=1).to_broadcast([L, D])).then_inc(s_const, 16)

                def load(g, p, i):
                    eng.wait_ge(e["xr"], done(g - 2))
                    eng.wait_ge(e["hx"], done(g - 2))
                    eng.dma_start(x2[:, p, :, :], row_tiles(x2_rows, g)).then_inc(s_in[p], 16)
                    eng.dma_start(h[:, p, :, :], row_tiles(h_rows, g)).then_inc(s_in[p], 16)

                def store(g, p, i):
                    eng.wait_ge(e["h2"], done(g))
                    eng.dma_start(row_tiles(h2_rows, g), h2[:, p, :, :]).then_inc(s_store[p], 16)

                turns(eng, NG, [(0, load), (3, store)])
                for p in range(2):
                    eng.wait_ge(s_store[p], AHEAD + 16 * (NG // 2))

            @block.gpsimd
            def _(eng):
                eng.memset(half[:, :], -0.5).then_inc(s_mem, 1)
                eng.memset(run[:, GT4, :], 0.0).then_inc(s_mem, 1)
                eng.wait_ge(s_mem, 2)
                eng.wait_ge(s_const, 16 * 11)

                def scale(g, p, i):
                    link = chain(eng, s_scale, 2 * g, settled=sp.settled)
                    eng.wait_ge(e["ss"], done(g))
                    eng.wait_ge(e["xr"], done(g - 2))
                    settle(eng, sp.settled)
                    link(eng.tensor_scalar(ss[:, p, :], ss[:, p, :], 1.0 / D, RMS_EPS, ALU.mult, ALU.add))
                    eng.tensor_tensor(r[:, p, :], ss[:, p, :], half[:, :], ALU.pow).then_inc(e["r"], 1)
                    eng.wait_ge(e["h2"], done(g - 2))
                    eng.wait_ge(s_in[p], 32 * i + 32)
                    settle(eng, sp.settled)
                    link(eng.tensor_tensor(hx[:, p, :, :], x2[:, p, :, :], h[:, p, :, :], ALU.add))
                    eng.tensor_tensor(hx[:, p, :, :], hx[:, p, :, :], b2[:, :].unsqueeze(1).to_broadcast([L, GT4, D]), ALU.add).then_inc(e["hx"], 1)

                def norm(g, p, i):
                    link = chain(eng, s_norm, 6 * g, settled=sp.settled)
                    var, rs, qq = mv[:, p, :, 1], rstd[:, p, :], q[:, p, :]
                    eng.wait_ge(e["stats"], done(g))
                    eng.wait_ge(e["z"], done(g - 2))
                    eng.wait_ge(e["x3"], done(g - 2))
                    settle(eng, sp.settled)
                    link(eng.tensor_scalar(qq, var, LN_EPS, None, ALU.add))
                    link(eng.tensor_tensor(rs, qq, half[:, :], ALU.pow))
                    link(eng.tensor_tensor(qq, rs, rs, ALU.mult))
                    link(eng.tensor_tensor(qq, qq, var, ALU.mult))
                    link(eng.tensor_scalar(qq, qq, 4.0, RMS_EPS, ALU.mult, ALU.add))
                    link(eng.tensor_tensor(qq, qq, half[:, :], ALU.pow))
                    eng.tensor_scalar(qq, qq, 2.0, None, ALU.mult).then_inc(e["q"], 1)

                def scatter(g, p, i):
                    eng.wait_ge(e["sidx"], done(g))
                    eng.wait_ge(e["z"], done(g))
                    settle(eng, sp.settled)
                    for k in range(2):
                        for j in range(GT4):
                            eng.indirect_dma_start(
                                out=slots[:, :], out_offset=IndirectOffsetOnAxis(ap=sidx[:, p, k, j:j + 1], axis=0),
                                in_=z[:, p, j, :], in_offset=None, bounds_check=NE * ES - 1, oob_is_err=False).then_inc(s_scat[p], 16)

                turns(eng, NG, [(0, scale), (2, norm), (5, scatter)])
                for p in range(2):
                    eng.wait_ge(s_scat[p], 128 * (NG // 2))

            @block.scalar
            def _(eng):
                def squares(g, p, i):
                    eng.wait_ge(s_in[p], 32 * i + 32)
                    eng.wait_ge(e["r"], done(g - 2))
                    eng.wait_ge(e["xt_mm"], done(g - 2))
                    for j in range(GT4):
                        ins = eng.activation(xr[:, p, j, :], x2[:, p, j, :], ACT.Square, accum_out=ss[:, p, j:j + 1])
                    ins.then_inc(e["ss"], 1)

                def scaled(g, p, i):
                    eng.wait_ge(e["r"], done(g))
                    for j in range(GT4):
                        ins = eng.activation(xr[:, p, j, :], x2[:, p, j, :], ACT.Copy, scale=r[:, p, j:j + 1])
                    ins.then_inc(e["xr"], 1)

                def kept(g, p, i):
                    eng.wait_ge(e["xt_mm"], done(g))
                    eng.wait_ge(e["up"], AHEAD + NF * (g - 1))
                    for k in range(2):
                        ins = eng.activation(xts[0][:, p, k, :], bank[k][0:K2, 0:GW], ACT.Copy)
                    ins.then_inc(e["xt_head"], 1)

                def x3_kept(g, p, i):
                    eng.wait_ge(e["x3t_mm"], done(g))
                    eng.wait_ge(e["lmm"], done(g - 2))
                    for k in range(2):
                        ins = eng.activation(x3t[:, p, k, :], bank[k][0:K2, 0:GW], ACT.Copy)
                    ins.then_inc(e["x3t"], 1)

                def gelu(g, p, i):
                    eng.wait_ge(e["down"], done(2 * (g - 2) + 1))
                    for f in range(NF):
                        eng.wait_ge(e["up"], done(NF * g + f))
                        eng.activation(gt[:, p, f, :], bank[2 + f % 2][:, 0:GW], ACT.Gelu_apprx_tanh, bias=b1[:, f:f + 1]).then_inc(e["gelu"], 1)

                def zrow(g, p, i):
                    eng.wait_ge(e["q"], done(g))
                    eng.wait_ge(e["x3"], done(g))
                    eng.wait_ge(s_scat[p], 128 * i)
                    for j in range(GT4):
                        ins = eng.activation(z[:, p, j, :], x3[:, p, j, :], ACT.Copy, scale=q[:, p, j:j + 1])
                    ins.then_inc(e["z"], 1)

                eng.wait_ge(s_const, 16 * 11)
                turns(eng, NG, [(0, squares), (1, kept), (3, x3_kept), (4, zrow), (1, gelu), (0, scaled)], peeled=2)

            @block.vector
            def _(eng):
                eng.wait_ge(s_const, 16 * 11)
                for k in range(2):
                    eng.tensor_scalar(w1[:, k, :], w1[:, k, :], n2[:, k:k + 1], None, ALU.mult).then_inc(s_w, 1)
                eng.tensor_scalar(rank[:, :], expert[:, :], -1.0, float(NE), ALU.mult, ALU.add).then_inc(s_w, 1)
                eng.tensor_scalar(base[:, :], expert[:, :], float(ES), None, ALU.mult).then_inc(s_w, 1)
                eng.wait_ge(s_w, 4)
                eng.wait_ge(s_mem, 2)
                eng.tensor_copy(w1s[0][:, :, :], w1[:, :, :]).then_inc(s_w, 1)
                eng.wait_ge(s_w, 5)
                rest(eng, w1s[1][:, :, :], w1[:, :, :], w1s[0][:, :, :]).then_inc(s_w, 1)

                def xt_rest(g, p, i):
                    eng.wait_ge(e["xt_head"], done(g))
                    for k in range(2):
                        ins = rest(eng, xts[1][:, p, k, :], bank[k][0:K2, 0:GW], xts[0][:, p, k, :])
                    ins.then_inc(e["xt"], 1)

                def total(g, p, i):
                    eng.wait_ge(e["hx"], done(g))
                    eng.wait_ge(s_store[p], AHEAD + 16 * i)
                    for j in range(2):
                        eng.wait_ge(e["down"], done(2 * g + j))
                        ins = eng.tensor_tensor(h2[:, p, 2 * j:2 * j + 2, :], bank[4 + j][0:L, 0:2 * D].rearrange("t (j d) -> t j d", j=2),
                                                hx[:, p, 2 * j:2 * j + 2, :], ALU.add)
                        if j:
                            ins.then_inc(e["h2"], 1)
                        else:
                            ins.then_inc(s_st, 1)
                    eng.wait_ge(s_st, (1 + GT4) * g + 1)
                    eng.wait_ge(e["h2"], done(g))
                    eng.wait_ge(e["q"], done(g - 2))
                    link = chain(eng, s_st, (1 + GT4) * g + 1, settled=sp.settled)
                    for j in range(GT4):
                        link(eng.bn_stats(st[:, p, j, :], h2[:, p, j, :]))
                    for j in range(GT4):
                        ins = eng.bn_aggr(mv[:, p, j, :], st[:, p, j, :])
                    ins.then_inc(e["stats"], 1)

                def centred(g, p, i):
                    eng.wait_ge(e["q"], done(g))
                    eng.wait_ge(e["x3t_mm"], done(g - 2))
                    eng.wait_ge(e["z"], done(g - 2))
                    at = bass.ds(g * GT4, GT4)
                    eng.tensor_copy(rt.mean[:, at], mv[:, p, :, 0])
                    eng.tensor_copy(rt.rstd[:, at], rstd[:, p, :])
                    for j in range(GT4):
                        ins = eng.tensor_scalar(x3[:, p, j, :], h2[:, p, j, :], mv[:, p, j, 0:1], rstd[:, p, j:j + 1],
                                                ALU.subtract, ALU.mult)
                    ins.then_inc(e["x3"], 1)

                def choose(g, p, i):
                    link = chain(eng, s_choose, 14 * g)
                    eng.wait_ge(e["lmm"], done(g))
                    eng.wait_ge(e["count"], done(g - 2))
                    link(eng.tensor_copy(lg[:, p, :, :], bank[6][0:L, 0:GT4 * NE].rearrange("t (j e) -> t j e", j=GT4)))
                    ll = lg[:, p, :, :]
                    rk = rank[:, :].unsqueeze(1).to_broadcast([L, GT4, NE])

                    def wide(v):
                        return v.unsqueeze(2).to_broadcast([L, GT4, NE])

                    for k in range(2):
                        mk = mask[:, p, k, :, :]
                        link(eng.tensor_reduce(best[:, k, :], ll, AX.X, ALU.max))
                        link(eng.tensor_tensor(work[:, :, :], ll, wide(best[:, k, :]), ALU.is_equal))
                        link(eng.tensor_tensor(work[:, :, :], work[:, :, :], rk, ALU.mult))
                        link(eng.tensor_reduce(best[:, 2 + k, :], work[:, :, :], AX.X, ALU.max))
                        link(eng.tensor_tensor(mk, work[:, :, :], wide(best[:, 2 + k, :]), ALU.is_equal))
                        if k == 0:
                            link(eng.scalar_tensor_tensor(ll, mk, -1e30, ll, ALU.mult, ALU.add))
                    at = bass.ds(g * GT4, GT4)
                    link(eng.tensor_tensor(rt.gap[:, at], best[:, 1, :], best[:, 0, :], ALU.subtract))
                    link(eng.tensor_tensor(both[:, p, :, :], mask[:, p, 0, :, :], mask[:, p, 1, :, :], ALU.add))
                    eng.tensor_tensor(both[:, p, :, :], both[:, p, :, :], wide(valid[:, at]), ALU.mult).then_inc(e["both"], 1)

                def places(g, p, i):
                    link = chain(eng, s_place, (1 + GT4 + 1 + 2 * 8) * g)
                    eng.wait_ge(e["count"], done(g))
                    eng.wait_ge(s_scat[p], 128 * i)
                    at = bass.ds(g * GT4, GT4)
                    link(eng.tensor_copy(run[:, 0, :], run[:, GT4, :]))
                    for j in range(GT4):
                        link(eng.tensor_tensor(run[:, j + 1, :], run[:, j, :], bank[7][0:L, 32 + NE * j:32 + NE * j + NE], ALU.add))
                    link(eng.tensor_tensor(place[:, :, :], run[:, 0:GT4, :],
                                           bank[7][0:L, 0:GT4 * NE].rearrange("t (j e) -> t j e", j=GT4), ALU.add))
                    bs = base[:, :].unsqueeze(1).to_broadcast([L, GT4, NE])
                    for k in range(2):
                        mk = mask[:, p, k, :, :]
                        pk, ek, kp, sl = (small[:, n, :] for n in range(4))
                        link(eng.tensor_tensor(work[:, :, :], mk, place[:, :, :], ALU.mult))
                        link(eng.tensor_reduce(pk, work[:, :, :], AX.X, ALU.add))
                        link(eng.tensor_tensor(work[:, :, :], mk, bs, ALU.mult))
                        link(eng.tensor_reduce(ek, work[:, :, :], AX.X, ALU.add))
                        link(eng.scalar_tensor_tensor(rt.keep[:, k, at], pk, float(CAP), valid[:, at], ALU.is_lt, ALU.mult))
                        link(eng.tensor_tensor(sl, pk, ek, ALU.add))
                        link(eng.tensor_tensor(rt.slot[:, k, at], sl, rt.keep[:, k, at], ALU.mult))
                        link(eng.scalar_tensor_tensor(kp, sl, -65536.0, rt.keep[:, k, at], ALU.add, ALU.mult))
                        ins = eng.tensor_scalar(sidx[:, p, k, :], kp, 65536.0, None, ALU.add)
                    ins.then_inc(e["sidx"], 1)

                turns(eng, NG, [(3, centred), (1, xt_rest), (4, choose), (2, total), (5, places)], peeled=2)

            @block.tensor
            def _(eng):
                eng.wait_ge(s_const, 16 * 11)
                eng.wait_ge(s_w, 6)

                def transposed(src, dst):
                    for k in range(2):
                        for j in range(GT4):
                            ins = eng.transpose(dst[k][0:K2, L * j:L * j + L], src[:, j, K2 * k:K2 * k + K2], ident[0:L, 0:L])
                    return ins

                def turned(g, p, i):
                    eng.wait_ge(e["xr"], done(g))
                    eng.wait_ge(e["x3t"], done(g - 3))
                    transposed(xr[:, p, :, :], bank).then_inc(e["xt_mm"], 1)

                def x3_turned(g, p, i):
                    eng.wait_ge(e["x3"], done(g))
                    eng.wait_ge(e["xt"], done(min(g + 2, NG - 1) if isinstance(g, int) else g + 2))
                    transposed(x3[:, p, :, :], bank).then_inc(e["x3t_mm"], 1)

                def up(g, p, i):
                    eng.wait_ge(e["xt"], done(g))
                    for f in range(NF):
                        eng.wait_ge(e["gelu"], done(NF * g + f - 2))
                        terms = [(a, b, k) for k in range(2) for a, b in PARTS]
                        for n, (a, b, k) in enumerate(terms):
                            ins = eng.matmul(bank[2 + f % 2][:, 0:GW], w1s[a][:, k, 128 * f:128 * f + 128], xts[b][:, p, k, :],
                                             start=(n == 0), stop=(n == len(terms) - 1))
                        ins.then_inc(e["up"], 1)

                def down(g, p, i):
                    eng.wait_ge(e["gelu"], done(NF * g + NF - 1))
                    eng.wait_ge(e["h2"], done(g - 1))
                    for j in range(GT4):
                        o = bank[4 + j // 2][0:L, D * (j % 2):D * (j % 2) + D]
                        for f in range(NF):
                            ins = eng.matmul(o, gt[:, p, f, L * j:L * j + L], w2[:, f, :], start=(f == 0), stop=(f == NF - 1))
                        if j % 2:
                            ins.then_inc(e["down"], 1)

                def logits(g, p, i):
                    eng.wait_ge(e["x3t"], done(g))
                    eng.wait_ge(e["both"], done(g - 1))
                    for j in range(GT4):
                        for k in range(2):
                            ins = eng.matmul(bank[6][0:L, NE * j:NE * j + NE], x3t[:, p, k, L * j:L * j + L], gate[:, k, :],
                                             start=(k == 0), stop=(k == 1))
                    ins.then_inc(e["lmm"], 1)

                def counts(g, p, i):
                    eng.wait_ge(e["both"], done(g))
                    eng.wait_ge(e["sidx"], done(g - 1))
                    rhs = both[:, p, :, :].rearrange("t j e -> t (j e)")
                    eng.matmul(bank[7][0:L, 0:GT4 * NE], before[:, :], rhs, start=True, stop=True)
                    eng.matmul(bank[7][0:L, 32:32 + GT4 * NE], ones[:, :], rhs, start=True, stop=True).then_inc(e["count"], 1)

                turns(eng, NG, [(1, turned), (2, down), (3, x3_turned), (1, up), (3, logits), (4, counts)])


def expert_turns(eng, stages):
    per = ES // SG
    half = per // 2

    def expert(x, px, first=False):
        for q in range(2):
            for lag, f in stages:
                if q >= lag:
                    f(x * per + (q - lag), (q - lag) % 2, x * half, x, px)
                elif not first:
                    f(x * per + (q - lag), (q - lag) % 2, x * half - 1, x - 1, 1 - px)
        with eng.Fori(1, half) as i:
            for q in range(2):
                for lag, f in stages:
                    f(x * per + (2 * i + (q - lag)), (q - lag) % 2, x * half + (i + (q - lag) // 2), x, px)

    expert(0, 0, first=True)
    with eng.Fori(0, (NE - 2) // 2) as y:
        expert(2 * y + 1, 1)
        expert(2 * y + 2, 0)
    expert(NE - 1, 1)
    for q in range(2):
        for lag, f in stages:
            if lag > q:
                f(NE * per + q - lag, (q - lag) % 2, NE * half - 1, NE - 1, 1)


def experts(nc, sp, c, slots, answers):
    NJ = SG // 128
    NH = HID // 128
    per = ES // SG
    with sp.phase() as ctx:
        def sb(name, shape, dt=F32):
            return sp.sb(ctx, "ex_" + name, shape, dt)

        def sem(name):
            return sp.sem("ex_" + name)

        ident = sb("ident", [128, 128])
        norm = sb("norm", [K2, 2, 2])
        w13 = sb("w13", [K2, 2, 2, 2 * HID])
        w2 = sb("w2", [128, 2, NH, D])
        z = sb("z", [128, 2, NJ, D])
        sil = sb("sil", [128, 2, SG])
        w13s = [sb(f"w13_{n}", [K2, 2, 2, 2 * HID], F32R) for n in ("head", "rest")]
        zts = [sb(f"zt_{n}", [K2, 2, 2, SG], F32R) for n in ("head", "rest")]
        ht = sb("ht", [128, 2, NH, SG])
        ans = sb("ans", [128, 2, NJ, D])
        bank = [sp.ps(ctx, f"ex_bank{i}", [128, 512]) for i in range(8)]
        s_const = sem("const")
        s_in = [sem("in0"), sem("in1")]
        s_win = [sem("w13_in0"), sem("w13_in1")]
        s_w2in = [sem("w2_in0"), sem("w2_in1")]
        s_store = [sem("store0"), sem("store1")]
        s_wlink, s_zlink = sem("w_link"), sem("z_link")
        names = ("w", "z_mm", "zt", "gu", "silu", "h", "down", "ans")
        e = {n: sem(n) for n in names}

        def group(buf, u):
            return buf[bass.ds(u * SG, SG), :].rearrange("(p j) d -> p j d", j=NJ)

        with nc.Block() as block:
            @block.sync
            def _(eng):
                start_counts(eng, *s_store, *e.values())
                eng.dma_start(ident[:, :], c["ident"]).then_inc(s_const, 16)

                def load(u, p, i):
                    eng.wait_ge(e["z_mm"], done(u - 2))
                    eng.dma_start(z[:, p, :, :], group(slots, u)).then_inc(s_in[p], 16)

                def store(u, p, i):
                    eng.wait_ge(e["ans"], done(2 * u + 1))
                    eng.dma_start(group(answers, u), ans[:, p, :, :]).then_inc(s_store[p], 16)

                turns(eng, NE * per, [(0, load), (3, store)])
                for p in range(2):
                    eng.wait_ge(s_store[p], AHEAD + 16 * NE * per // 2)

            @block.gpsimd
            def _(eng):
                def fetch(x, px):
                    at = bass.ds(x, 1)
                    eng.dma_start(w13[:, px, :, :], c["w13"][at].rearrange("o (k p) n -> p (o k) n", p=K2)).then_inc(s_win[px], 16)
                    eng.dma_start(norm[:, px, :], c["norm_e"][:, at, :].rearrange("p o k -> p (o k)")).then_inc(s_win[px], 16)

                def split(x, px, turn):
                    link = chain(eng, s_wlink, 2 * x, settled=sp.settled)
                    eng.wait_ge(s_win[px], 32 * turn + 32)
                    settle(eng, sp.settled)
                    eng.tensor_scalar(w13[:, px, 0, :], w13[:, px, 0, :], norm[:, px, 0:1], None, ALU.mult)
                    link(eng.tensor_scalar(w13[:, px, 1, :], w13[:, px, 1, :], norm[:, px, 1:2], None, ALU.mult))
                    if not isinstance(x, int):
                        eng.wait_ge(e["down"], done(2 * per * (x - 1) - 1))
                        settle(eng, sp.settled)
                    eng.dma_start(w2[:, px, :, :], c["w2"][bass.ds(x, 1)].rearrange("o (k p) n -> p (o k) n", p=128)).then_inc(s_w2in[px], 16)
                    link(eng.tensor_copy(w13s[0][:, px, :, :], w13[:, px, :, :]))
                    rest(eng, w13s[1][:, px, :, :], w13[:, px, :, :], w13s[0][:, px, :, :]).then_inc(e["w"], 1)

                for x in range(2):
                    fetch(x, x)
                for x in range(2):
                    split(x, x, 0)
                with eng.Fori(0, (NE - 2) // 2) as y:
                    for px in range(2):
                        eng.wait_ge(e["w"], done(2 * y + px))
                        settle(eng, sp.settled)
                        fetch(2 * y + px + 2, px)
                    for px in range(2):
                        split(2 * y + px + 2, px, y + 1)

            @block.scalar
            def _(eng):
                def silu(u, p, i, x, px):
                    for f in range(NH):
                        eng.wait_ge(e["gu"], done(NH * u + f))
                        eng.wait_ge(e["h"], done(NH * u + f - 2))
                        eng.activation(sil[:, f % 2, :], bank[2 + 2 * (f % 2)][:, :], ACT.Silu).then_inc(e["silu"], 1)

                def answer(u, p, i, x, px):
                    eng.wait_ge(s_store[p], AHEAD + 16 * i)
                    for j in range(2):
                        eng.wait_ge(e["down"], done(2 * u + j))
                        eng.activation(ans[:, p, 2 * j:2 * j + 2, :],
                                       bank[6 + j][:, 0:2 * D].rearrange("t (j d) -> t j d", j=2), ACT.Copy).then_inc(e["ans"], 1)

                expert_turns(eng, [(1, silu), (2, answer)])

            @block.vector
            def _(eng):
                def kept(u, p, i, x, px):
                    eng.wait_ge(e["z_mm"], done(u))
                    eng.wait_ge(e["gu"], AHEAD + NH * (u - 1))
                    for k in range(2):
                        eng.tensor_copy(zts[0][:, p, k, :], bank[k][0:K2, :]).then_inc(s_zlink, 1)
                    eng.wait_ge(s_zlink, 2 * u + 2)
                    for k in range(2):
                        ins = rest(eng, zts[1][:, p, k, :], bank[k][0:K2, :], zts[0][:, p, k, :])
                    ins.then_inc(e["zt"], 1)

                def product(u, p, i, x, px):
                    eng.wait_ge(e["down"], AHEAD + 2 * (u - 1))
                    for f in range(NH):
                        eng.wait_ge(e["silu"], done(NH * u + f))
                        eng.tensor_tensor(ht[:, p, f, :], sil[:, f % 2, :], bank[3 + 2 * (f % 2)][:, :], ALU.mult).then_inc(e["h"], 1)

                expert_turns(eng, [(0, kept), (1, product)])

            @block.tensor
            def _(eng):
                def turned(u, p, i, x, px):
                    eng.wait_ge(s_in[p], 16 * i + 16)
                    eng.wait_ge(e["zt"], done(u - 1))
                    for k in range(2):
                        for j in range(NJ):
                            ins = eng.transpose(bank[k][0:K2, 128 * j:128 * j + 128], z[:, p, j, K2 * k:K2 * k + K2], ident[:, :])
                    ins.then_inc(e["z_mm"], 1)

                def up(u, p, i, x, px):
                    eng.wait_ge(e["zt"], done(u))
                    eng.wait_ge(e["w"], done(x))
                    for f in range(NH):
                        eng.wait_ge(e["h"], done(NH * u + f - 2))
                        for v in range(2):
                            cols = slice(HID * v + 128 * f, HID * v + 128 * f + 128)
                            terms = [(a, b, k) for k in range(2) for a, b in PARTS]
                            for n, (a, b, k) in enumerate(terms):
                                ins = eng.matmul(bank[2 + 2 * (f % 2) + v][:, :], w13s[a][:, px, k, cols], zts[b][:, p, k, :],
                                                 start=(n == 0), stop=(n == len(terms) - 1))
                        ins.then_inc(e["gu"], 1)

                def down(u, p, i, x, px):
                    eng.wait_ge(e["h"], done(NH * u + NH - 1))
                    eng.wait_ge(s_w2in[px], 8 * (x - px) + 16)
                    for j in range(NJ):
                        if j % 2 == 0:
                            eng.wait_ge(e["ans"], done(2 * (u - 1) + j // 2))
                        o = bank[6 + j // 2][:, D * (j % 2):D * (j % 2) + D]
                        for f in range(NH):
                            ins = eng.matmul(o, ht[:, p, f, 128 * j:128 * j + 128], w2[:, px, f, :],
                                             start=(f == 0), stop=(f == NH - 1))
                        if j % 2:
                            ins.then_inc(e["down"], 1)

                eng.wait_ge(s_const, 16)
                expert_turns(eng, [(0, turned), (1, up), (2, down)])


def combine(nc, sp, h2_rows, answers, out, rt):
    with sp.phase() as ctx:
        def sb(name, shape, dt=F32):
            return sp.sb(ctx, "cb_" + name, shape, dt)

        def sem(name):
            return sp.sem("cb_" + name)

        h2 = sb("h2", [L, 2, GT4, D])
        f = sb("f", [L, 2, 2, GT4, D])
        o = sb("o", [L, 2, GT4, D])
        idx = sb("idx", [L, 2, 2, GT4], I32)
        e2 = sb("e2", [L, NT])
        w = sb("w", [L, 2, NT])
        alpha = sb("alpha", [L, NT])
        beta = sb("beta", [L, NT])
        s_in = [sem("in0"), sem("in1")]
        s_f = [sem("f0"), sem("f1")]
        s_store = [sem("store0"), sem("store1")]
        s_exp, s_prep, s_acc = sem("exp"), sem("prep"), sem("acc")
        e = {n: sem(n) for n in ("idx", "o")}

        with nc.Block() as block:
            @block.sync
            def _(eng):
                start_counts(eng, *s_store, *e.values())

                def load(g, p, i):
                    eng.wait_ge(e["o"], done(g - 2))
                    eng.dma_start(h2[:, p, :, :], row_tiles(h2_rows, g)).then_inc(s_in[p], 16)

                def store(g, p, i):
                    eng.wait_ge(e["o"], done(g))
                    eng.dma_start(row_tiles(out, g), o[:, p, :, :]).then_inc(s_store[p], 16)

                turns(eng, NG, [(0, load), (2, store)])
                for p in range(2):
                    eng.wait_ge(s_store[p], AHEAD + 16 * (NG // 2))

            @block.gpsimd
            def _(eng):
                def gather(g, p, i):
                    eng.wait_ge(e["idx"], done(g))
                    eng.wait_ge(e["o"], done(g - 2))
                    settle(eng, sp.settled)
                    for k in range(2):
                        for j in range(GT4):
                            eng.indirect_dma_start(out=f[:, p, k, j, :], out_offset=None, in_=answers[:, :],
                                                   in_offset=IndirectOffsetOnAxis(ap=idx[:, p, k, j:j + 1], axis=0)).then_inc(s_f[p], 16)

                turns(eng, NG, [(0, gather)])

            @block.scalar
            def _(eng):
                eng.activation(e2[:, :], rt.gap[:, :], ACT.Exp).then_inc(s_exp, 1)

            @block.vector
            def _(eng):
                def index(g, p, i):
                    eng.wait_ge(s_f[p], 128 * i)
                    eng.tensor_copy(idx[:, p, :, :], rt.slot[:, :, bass.ds(g * GT4, GT4)]).then_inc(e["idx"], 1)

                def summed(g, p, i):
                    eng.wait_ge(s_in[p], 16 * i + 16)
                    eng.wait_ge(s_store[p], AHEAD + 16 * i)
                    for j in range(GT4):
                        at = bass.ds(g * GT4 + j, 1)
                        ins = eng.tensor_scalar(o[:, p, j, :], h2[:, p, j, :], alpha[:, at], beta[:, at], ALU.mult, ALU.add)
                    ins.then_inc(s_acc, 1)
                    eng.wait_ge(s_acc, 2 * g + 1)
                    eng.wait_ge(s_f[p], 128 * i + 128)
                    for k in range(2):
                        if k:
                            eng.wait_ge(s_acc, 2 * g + 2)
                        for j in range(GT4):
                            ins = eng.scalar_tensor_tensor(o[:, p, j, :], f[:, p, k, j, :], w[:, k, bass.ds(g * GT4 + j, 1)],
                                                           o[:, p, j, :], ALU.mult, ALU.add)
                        ins.then_inc(e["o"] if k else s_acc, 1)

                link = chain(eng, s_prep, 0)
                eng.wait_ge(s_exp, 1)
                link(eng.tensor_scalar(alpha[:, :], e2[:, :], 1.0, None, ALU.add))
                link(eng.reciprocal(w[:, 0, :], alpha[:, :]))
                link(eng.tensor_tensor(w[:, 1, :], e2[:, :], w[:, 0, :], ALU.mult))
                link(eng.tensor_tensor(w[:, :, :], w[:, :, :], rt.keep[:, :, :], ALU.mult))
                link(eng.tensor_tensor(alpha[:, :], w[:, 0, :], w[:, 1, :], ALU.add))
                link(eng.tensor_tensor(alpha[:, :], alpha[:, :], rt.rstd[:, :], ALU.mult))
                link(eng.scalar_tensor_tensor(beta[:, :], rt.mean[:, :], -1.0, alpha[:, :], ALU.mult, ALU.mult))
                link(eng.tensor_scalar(alpha[:, :], alpha[:, :], 1.0, None, ALU.add))
                turns(eng, NG, [(0, index), (1, summed)], peeled=2)


def program(nc, a, out, upto=9, keep="Internal"):
    with ExitStack() as outer:
        sp = Space(nc, outer)

        def rows(name, n, w=D):
            return nc.dram_tensor(name, (n, w), F32, kind=keep).ap()

        h_rows, x_rows = rows("h_rows", N), rows("x_rows", N)
        x2_rows, h2_rows = rows("x2_rows", N), rows("h2_rows", N)
        xt = nc.dram_tensor("x_t", (K2, 2, N), F32, kind=keep).ap()
        params = rows("params", 2 * H, N)
        slots, answers = rows("slots", NE * ES), rows("answers", NE * ES)
        tokenizer(nc, sp, a["blocks"], a["tok_w"], a["tok_b"], a["cls"], a["pos"], a["txt"], h_rows, slots)
        if upto < 2:
            return
        normalise(nc, sp, a, h_rows, a["w_in"], a["norm1"], x_rows, xt, params)
        if upto < 3:
            return
        mixer(nc, sp, a, x_rows, xt, params, x2_rows)
        if upto < 4:
            return
        with ExitStack() as ctx:
            route = Route(sp, ctx)
            feed_forward(nc, sp, a, x2_rows, h_rows, h2_rows, slots, route)
            if upto < 5:
                return
            experts(nc, sp, a, slots, answers)
            if upto < 6:
                return
            combine(nc, sp, h2_rows, answers, out, route)


def constants():
    import numpy as np
    ident = np.eye(128, dtype=np.float32)
    rows = np.arange(EP)
    head_of = rows // (2 * NS)
    block_mask = (head_of[:, None] == (np.arange(DI) // P)[None, :]).astype(np.float32)
    step_mask = ((head_of[:, None] == head_of[None, :]) & (rows[:, None] % NS == rows[None, :] % NS)).astype(np.float32)
    head_col = (np.arange(H * NS)[:, None] // NS == np.arange(H)[None, :]).astype(np.float32)
    seq = np.arange(SEQ)
    comp = rows // NS % 2
    spread = np.stack([((seq // B)[:, None] == head_of[None, :]) & (comp == j)[None, :] for j in range(2)], 1).astype(np.float32)
    image_mask = (seq[:, None] % B == np.arange(B)[None, :]).astype(np.float32)
    before = (np.arange(L)[:, None] < np.arange(L)[None, :]).astype(np.float32)
    ones = np.ones((L, L), np.float32)
    valid = np.ones((L, CH), np.float32)
    valid[T - (CH - 1) * L:, CH - 1] = 0
    valid = np.tile(valid, (1, B))
    expert = np.tile(np.arange(NE, dtype=np.float32), (L, 1))
    return {"ident": ident, "block_mask": block_mask, "step_mask": step_mask, "head_col": head_col,
            "spread": spread, "image_mask": image_mask, "before": before, "ones": ones,
            "valid": valid, "expert": expert}


def lay_out(inputs):
    import numpy as np
    a = {k: np.asarray(v) for k, v in inputs.items()}
    w_in, w_bc = a["L0_attn_w_in"], a["L0_attn_w_bc"]
    out = {
        "blocks": a["x"].reshape(B, 3, BLK, 8, BLK, 8).transpose(1, 3, 5, 0, 2, 4).reshape(D, B, BLK * BLK),
        "txt": a["txt"],
        "tok_w": a["L0_tok_w"].reshape(D, 3, 2, 8, 2, 8).transpose(1, 3, 5, 2, 4, 0).reshape(D, 2, 2, D),
        "tok_b": a["L0_tok_b"],
        "cls": a["L0_tok_cls_token"].reshape(1, D),
        "pos": a["L0_tok_pos_embedding"].reshape(1 + NPATCH, D),
        "norm1": a["L0_attn_norm1_w"].reshape(2, K2).T,
        "w_in": np.concatenate([w_in[:, :2 * DI], w_in[:, 2 * DI::2], w_in[:, 2 * DI + 1::2]], axis=1),
        "conv_w": a["L0_attn_conv_w"].reshape(3, 128, 4).transpose(1, 0, 2),
        "w_bc": w_bc.reshape(DI, H, 2, NS).transpose(0, 2, 1, 3).reshape(DI, EP),
        "d_skip": a["L0_attn_D_skip"],
        "w_out": a["L0_attn_w_out"],
        "norm2": a["L0_attn_norm2_w"].reshape(2, K2).T,
        "ff_w1": a["L0_attn_ff_w1"], "ff_b1": a["L0_attn_ff_b1"].reshape(FF // 128, 128).T,
        "ff_w2": a["L0_attn_ff_w2"], "ff_b2": a["L0_attn_ff_b2"],
        "gate": a["L0_ffn_gate_w"].transpose(1, 0),
        "w13": a["L0_ffn_w13"].transpose(0, 2, 1),
        "w2": a["L0_ffn_w2"].transpose(0, 2, 1),
        "norm_e": a["L0_ffn_norm_w"].reshape(NE, 2, K2).transpose(2, 0, 1),
    }
    out.update(constants())
    return {k: np.ascontiguousarray(v) for k, v in out.items()}


def kernel(**inputs):
    import concourse.bacc as bacc
    from concourse import mybir as mb
    from concourse.bass_utils import run_bass_kernel_spmd as run

    nc = bacc.Bacc("TRN2", target_bir_lowering=False, num_devices=1)
    arrays = lay_out(inputs)
    aps = {k: nc.dram_tensor(f"in_{k}", v.shape, mb.dt.from_np(v.dtype), kind="ExternalInput").ap()
           for k, v in arrays.items()}
    out = nc.dram_tensor("out_rows", (N, D), F32, kind="ExternalOutput").ap()
    program(nc, aps, out)
    r = run(nc, [{f"in_{k}": v for k, v in arrays.items()}], core_ids=[0])
    return r.results[0]["out_rows"].reshape(B, TP, D)[:, :T]
```
